# Optimizing a Trainium2 kernel written in Bass

```python
import numpy as np
import jax
import jax.numpy as jnp

def _softmax(x, axis=-1):
    return jax.nn.softmax(x, axis=axis)

def _gelu(x):
    return jax.nn.gelu(x, approximate=True)

def _silu(x):
    return jax.nn.silu(x)

def _sigmoid(x):
    return jax.nn.sigmoid(x)

def _layernorm(x, axis=-1, eps=1e-05):
    m = jnp.mean(x, axis=axis, keepdims=True)
    v = jnp.var(x, axis=axis, keepdims=True)
    return (x - m) / jnp.sqrt(v + eps)

def _scatter_add(tgt, idx, src, axis=0):
    return tgt.at[idx].add(src)

def _segment_sum(src, seg, n):
    return jax.ops.segment_sum(src, seg, n)
kernel_name = 'mk_seq_postln_d2_jaxref_r8_878303'

def setup_inputs(seed: int=0):
    np.random.seed(seed)
    _w = jnp.asarray

    def _L0_attn_setup():
        import jax, jax.numpy as jnp
        import numpy as np
        import math
        B, T, E = (2, 256, 256)
        HQ, HKV = (32, 8)
        G = HQ // HKV
        D = E // HQ

        def _rope(y):
            d = y.shape[-1]
            t = y.shape[-2]
            pos = jnp.arange(1, t + 1, dtype=jnp.float32)[:, None]
            freqs = 10000.0 ** (-(2.0 * jnp.arange(d // 2, dtype=jnp.float32)) / d)
            theta = pos * freqs
            cos = jnp.cos(theta)
            sin = jnp.sin(theta)
            y1, y2 = jnp.split(y, 2, axis=-1)
            return jnp.concatenate([y1 * cos - y2 * sin, y2 * cos + y1 * sin], axis=-1)
        key = jax.random.key(seed)
        ks = jax.random.split(key, 9)
        s = 0.02
        return {'x': jax.random.normal(ks[0], (B, T, E), jnp.float32), 'Wq': jax.random.normal(ks[1], (E, E), jnp.float32) * s, 'bq': jax.random.normal(ks[2], (E,), jnp.float32) * s, 'Wk': jax.random.normal(ks[3], (E, HKV * D), jnp.float32) * s, 'bk': jax.random.normal(ks[4], (HKV * D,), jnp.float32) * s, 'Wv': jax.random.normal(ks[5], (E, HKV * D), jnp.float32) * s, 'bv': jax.random.normal(ks[6], (HKV * D,), jnp.float32) * s, 'Wo': jax.random.normal(ks[7], (E, E), jnp.float32) * s, 'bo': jax.random.normal(ks[8], (E,), jnp.float32) * s}
    _L0_attn_in = _L0_attn_setup()

    def _L0_ffn_setup():
        import jax, jax.numpy as jnp
        import numpy as np
        HIDDEN = 256
        INTER = 1024
        B, S = (4, 128)

        def _qmatmul(x, w_int8, scale):
            y = jnp.einsum('bsh,ho->bso', x, w_int8.astype(x.dtype))
            return y * scale
        key = jax.random.key(seed)
        ks = jax.random.split(key, 7)
        x = jax.random.normal(ks[0], (B, S, HIDDEN), dtype=jnp.float32)
        w_gate = jax.random.randint(ks[1], (HIDDEN, INTER), -128, 128, dtype=jnp.int32).astype(jnp.int8)
        w_up = jax.random.randint(ks[2], (HIDDEN, INTER), -128, 128, dtype=jnp.int32).astype(jnp.int8)
        w_down = jax.random.randint(ks[3], (INTER, HIDDEN), -128, 128, dtype=jnp.int32).astype(jnp.int8)
        s_gate = jax.random.uniform(ks[4], (INTER,), dtype=jnp.float32) * 0.02 + 0.001
        s_up = jax.random.uniform(ks[5], (INTER,), dtype=jnp.float32) * 0.02 + 0.001
        s_down = jax.random.uniform(ks[6], (HIDDEN,), dtype=jnp.float32) * 0.02 + 0.001
        return {'x': x, 'w_gate': w_gate, 'w_up': w_up, 'w_down': w_down, 's_gate': s_gate, 's_up': s_up, 's_down': s_down}
    _L0_ffn_in = _L0_ffn_setup()

    def _L1_attn_setup():
        import jax, jax.numpy as jnp
        import numpy as np
        HID, H, DK, DV, KS = (256, 16, 128, 128, 4)

        def _p(key, shape, scale=0.02):
            return jax.random.normal(key, shape, dtype=jnp.float32) * scale

        def _dwconv_causal(y, w, b):
            out = jax.lax.conv_general_dilated(y.transpose(0, 2, 1), w, window_strides=(1,), padding=[(KS - 1, 0)], feature_group_count=w.shape[0])
            return out.transpose(0, 2, 1) + b

        def _silu(x):
            return x * jax.nn.sigmoid(x)

        def _gated_delta(q, k, v, alpha, beta, scale):
            B, T, nH, _ = q.shape
            qs = q.transpose(1, 0, 2, 3)
            ks = k.transpose(1, 0, 2, 3) * scale
            vs = v.transpose(1, 0, 2, 3)
            al = alpha.transpose(1, 0, 2)
            be = beta.transpose(1, 0, 2)

            def step(S, inp):
                qt, kt, vt, at, bt = inp
                err = jnp.einsum('bhvk,bhk->bhv', S, kt) - vt
                S = at[..., None, None] * S - bt[..., None, None] * err[..., None] * kt[:, :, None, :]
                o = jnp.einsum('bhvk,bhk->bhv', S, qt)
                return (S, o)
            S0 = jnp.zeros((B, nH, DV, DK), dtype=q.dtype)
            _, o = jax.lax.scan(step, S0, (qs, ks, vs, al, be))
            return o.transpose(1, 0, 2, 3)
        key = jax.random.key(seed)
        ks = jax.random.split(key, 20)
        B, T = (2, 256)
        x = jax.random.normal(ks[0], (B, T, HID), dtype=jnp.float32)
        inp = {'x': x, 'Wq': _p(ks[1], (HID, H * DK)), 'Wk': _p(ks[2], (HID, H * DK)), 'Wv': _p(ks[3], (HID, H * DV)), 'Wa': _p(ks[4], (HID, H)), 'ba': jnp.zeros((H,), jnp.float32), 'Wb': _p(ks[5], (HID, H)), 'bb': jnp.zeros((H,), jnp.float32), 'Wg': _p(ks[6], (HID, H * DV)), 'Wo': _p(ks[7], (H * DV, HID)), 'conv_q_w': _p(ks[8], (H * DK, 1, KS), 0.3), 'conv_q_b': jnp.zeros((H * DK,), jnp.float32), 'conv_k_w': _p(ks[9], (H * DK, 1, KS), 0.3), 'conv_k_b': jnp.zeros((H * DK,), jnp.float32), 'conv_v_w': _p(ks[10], (H * DV, 1, KS), 0.3), 'conv_v_b': jnp.zeros((H * DV,), jnp.float32), 'ln_w': jnp.ones((DV,), jnp.float32), 'ln_b': jnp.zeros((DV,), jnp.float32)}
        return inp
    _L1_attn_in = _L1_attn_setup()

    def _L1_ffn_setup():
        import jax, jax.numpy as jnp
        import numpy as np

        @jax.custom_vjp
        def ste_sign(x):
            return jnp.sign(x)

        def _ste_fwd(x):
            return (jnp.sign(x), None)

        def _ste_bwd(_, g):
            return (g,)
        ste_sign.defvjp(_ste_fwd, _ste_bwd)
        D_MODEL = 256
        D_HIDDEN = 1024
        key = jax.random.key(seed)
        k_x, k_up, k_dn = jax.random.split(key, 3)
        x = jax.random.normal(k_x, (2, 256, D_MODEL), dtype=jnp.float32)
        up_weight = jax.random.normal(k_up, (D_HIDDEN, D_MODEL), dtype=jnp.float32) * 0.02
        down_weight = jax.random.normal(k_dn, (D_MODEL, D_HIDDEN), dtype=jnp.float32) * 0.02
        up_scale = jnp.ones((D_HIDDEN,), dtype=jnp.float32)
        down_scale = jnp.ones((D_MODEL,), dtype=jnp.float32)
        output_scale = jnp.ones((1,), dtype=jnp.float32)
        return {'x': x, 'up_weight': up_weight, 'down_weight': down_weight, 'up_scale': up_scale, 'down_scale': down_scale, 'output_scale': output_scale}
    _L1_ffn_in = _L1_ffn_setup()
    _d = {'L0_attn_x': _L0_attn_in['x'], 'L0_attn_Wq': _L0_attn_in['Wq'], 'L0_attn_bq': _L0_attn_in['bq'], 'L0_attn_Wk': _L0_attn_in['Wk'], 'L0_attn_bk': _L0_attn_in['bk'], 'L0_attn_Wv': _L0_attn_in['Wv'], 'L0_attn_bv': _L0_attn_in['bv'], 'L0_attn_Wo': _L0_attn_in['Wo'], 'L0_attn_bo': _L0_attn_in['bo'], 'L0_ffn_w_gate': _L0_ffn_in['w_gate'], 'L0_ffn_w_up': _L0_ffn_in['w_up'], 'L0_ffn_w_down': _L0_ffn_in['w_down'], 'L0_ffn_s_gate': _L0_ffn_in['s_gate'], 'L0_ffn_s_up': _L0_ffn_in['s_up'], 'L0_ffn_s_down': _L0_ffn_in['s_down'], 'L1_attn_Wq': _L1_attn_in['Wq'], 'L1_attn_Wk': _L1_attn_in['Wk'], 'L1_attn_Wv': _L1_attn_in['Wv'], 'L1_attn_Wa': _L1_attn_in['Wa'], 'L1_attn_ba': _L1_attn_in['ba'], 'L1_attn_Wb': _L1_attn_in['Wb'], 'L1_attn_bb': _L1_attn_in['bb'], 'L1_attn_Wg': _L1_attn_in['Wg'], 'L1_attn_Wo': _L1_attn_in['Wo'], 'L1_attn_conv_q_w': _L1_attn_in['conv_q_w'], 'L1_attn_conv_q_b': _L1_attn_in['conv_q_b'], 'L1_attn_conv_k_w': _L1_attn_in['conv_k_w'], 'L1_attn_conv_k_b': _L1_attn_in['conv_k_b'], 'L1_attn_conv_v_w': _L1_attn_in['conv_v_w'], 'L1_attn_conv_v_b': _L1_attn_in['conv_v_b'], 'L1_attn_ln_w': _L1_attn_in['ln_w'], 'L1_attn_ln_b': _L1_attn_in['ln_b'], 'L1_ffn_up_weight': _L1_ffn_in['up_weight'], 'L1_ffn_down_weight': _L1_ffn_in['down_weight'], 'L1_ffn_up_scale': _L1_ffn_in['up_scale'], 'L1_ffn_down_scale': _L1_ffn_in['down_scale'], 'L1_ffn_output_scale': _L1_ffn_in['output_scale']}
    _x0 = _d['L0_attn_x']
    _d['L0_attn_x'] = jax.random.normal(jax.random.fold_in(jax.random.key(seed), 1), (2, 1024, 256), dtype=_x0.dtype)
    del _x0
    return _d

def reference(L0_attn_x, L0_attn_Wq, L0_attn_bq, L0_attn_Wk, L0_attn_bk, L0_attn_Wv, L0_attn_bv, L0_attn_Wo, L0_attn_bo, L0_ffn_w_gate, L0_ffn_w_up, L0_ffn_w_down, L0_ffn_s_gate, L0_ffn_s_up, L0_ffn_s_down, L1_attn_Wq, L1_attn_Wk, L1_attn_Wv, L1_attn_Wa, L1_attn_ba, L1_attn_Wb, L1_attn_bb, L1_attn_Wg, L1_attn_Wo, L1_attn_conv_q_w, L1_attn_conv_q_b, L1_attn_conv_k_w, L1_attn_conv_k_b, L1_attn_conv_v_w, L1_attn_conv_v_b, L1_attn_ln_w, L1_attn_ln_b, L1_ffn_up_weight, L1_ffn_down_weight, L1_ffn_up_scale, L1_ffn_down_scale, L1_ffn_output_scale):

    def _L0_attn_ref(x, Wq, bq, Wk, bk, Wv, bv, Wo, bo):
        import jax, jax.numpy as jnp
        import numpy as np
        import math
        B, T, E = (2, 256, 256)
        HQ, HKV = (32, 8)
        G = HQ // HKV
        D = E // HQ

        def _rope(y):
            d = y.shape[-1]
            t = y.shape[-2]
            pos = jnp.arange(1, t + 1, dtype=jnp.float32)[:, None]
            freqs = 10000.0 ** (-(2.0 * jnp.arange(d // 2, dtype=jnp.float32)) / d)
            theta = pos * freqs
            cos = jnp.cos(theta)
            sin = jnp.sin(theta)
            y1, y2 = jnp.split(y, 2, axis=-1)
            return jnp.concatenate([y1 * cos - y2 * sin, y2 * cos + y1 * sin], axis=-1)
        b, t, _ = x.shape
        q = x @ Wq + bq
        k = x @ Wk + bk
        v = x @ Wv + bv
        q = q.reshape(b, t, HQ, D).transpose(0, 2, 1, 3)
        k = k.reshape(b, t, HKV, D).transpose(0, 2, 1, 3)
        v = v.reshape(b, t, HKV, D).transpose(0, 2, 1, 3)
        q = _rope(q)
        k = _rope(k)
        q = q.reshape(b, HKV, G, t, D)
        scale = math.sqrt(D)
        att = jnp.einsum('bkgid,bkjd->bkgij', q, k) / scale
        causal = jnp.tril(jnp.ones((t, t), dtype=bool))
        att = jnp.where(causal, att, -jnp.inf)
        att = jax.nn.softmax(att, axis=-1)
        y = jnp.einsum('bkgij,bkjd->bkgid', att, v)
        y = y.transpose(0, 3, 1, 2, 4).reshape(b, t, E)
        y = y @ Wo + bo
        return y

    def _L0_ffn_ref(x, w_gate, w_up, w_down, s_gate, s_up, s_down):
        import jax, jax.numpy as jnp
        import numpy as np
        HIDDEN = 256
        INTER = 1024
        B, S = (4, 128)

        def _qmatmul(x, w_int8, scale):
            y = jnp.einsum('bsh,ho->bso', x, w_int8.astype(x.dtype))
            return y * scale
        gate = jax.nn.silu(_qmatmul(x, w_gate, s_gate))
        up = _qmatmul(x, w_up, s_up)
        fuse = gate * up
        return _qmatmul(fuse, w_down, s_down)

    def _L1_attn_ref(x, Wq, Wk, Wv, Wa, ba, Wb, bb, Wg, Wo, conv_q_w, conv_q_b, conv_k_w, conv_k_b, conv_v_w, conv_v_b, ln_w, ln_b):
        import jax, jax.numpy as jnp
        import numpy as np
        HID, H, DK, DV, KS = (256, 16, 128, 128, 4)

        def _p(key, shape, scale=0.02):
            return jax.random.normal(key, shape, dtype=jnp.float32) * scale

        def _dwconv_causal(y, w, b):
            out = jax.lax.conv_general_dilated(y.transpose(0, 2, 1), w, window_strides=(1,), padding=[(KS - 1, 0)], feature_group_count=w.shape[0])
            return out.transpose(0, 2, 1) + b

        def _silu(x):
            return x * jax.nn.sigmoid(x)

        def _gated_delta(q, k, v, alpha, beta, scale):
            B, T, nH, _ = q.shape
            qs = q.transpose(1, 0, 2, 3)
            ks = k.transpose(1, 0, 2, 3) * scale
            vs = v.transpose(1, 0, 2, 3)
            al = alpha.transpose(1, 0, 2)
            be = beta.transpose(1, 0, 2)

            def step(S, inp):
                qt, kt, vt, at, bt = inp
                err = jnp.einsum('bhvk,bhk->bhv', S, kt) - vt
                S = at[..., None, None] * S - bt[..., None, None] * err[..., None] * kt[:, :, None, :]
                o = jnp.einsum('bhvk,bhk->bhv', S, qt)
                return (S, o)
            S0 = jnp.zeros((B, nH, DV, DK), dtype=q.dtype)
            _, o = jax.lax.scan(step, S0, (qs, ks, vs, al, be))
            return o.transpose(1, 0, 2, 3)
        B, T, _ = x.shape
        scale = DK ** (-0.5)
        q = _silu(_dwconv_causal(x @ Wq, conv_q_w, conv_q_b))
        k = _silu(_dwconv_causal(x @ Wk, conv_k_w, conv_k_b))
        v = _silu(_dwconv_causal(x @ Wv, conv_v_w, conv_v_b))
        q = q.reshape(B, T, H, DK)
        k = k.reshape(B, T, H, DK)
        v = v.reshape(B, T, H, DV)
        alpha = jax.nn.sigmoid(x @ Wa + ba)
        beta = jax.nn.sigmoid(x @ Wb + bb)
        o = _gated_delta(q, k, v, alpha, beta, scale)
        mu = o.mean(-1, keepdims=True)
        var = ((o - mu) ** 2).mean(-1, keepdims=True)
        o = (o - mu) * jax.lax.rsqrt(var + 1e-05) * ln_w + ln_b
        g = jax.nn.sigmoid(x @ Wg).reshape(B, T, H, DV)
        o = (o * g).reshape(B, T, H * DV)
        return o @ Wo

    def _L1_ffn_ref(x, up_weight, down_weight, up_scale, down_scale, output_scale):
        import jax, jax.numpy as jnp
        import numpy as np

        @jax.custom_vjp
        def ste_sign(x):
            return jnp.sign(x)

        def _ste_fwd(x):
            return (jnp.sign(x), None)

        def _ste_bwd(_, g):
            return (g,)
        ste_sign.defvjp(_ste_fwd, _ste_bwd)
        D_MODEL = 256
        D_HIDDEN = 1024
        up_w = ste_sign(up_weight)
        down_w = ste_sign(down_weight)
        hidden = jnp.einsum('bsd,hd->bsh', x, up_w) * up_scale
        hidden = jax.nn.relu(hidden)
        out = jnp.einsum('bsh,dh->bsd', hidden, down_w) * down_scale
        return out * output_scale
    x = L0_attn_x
    x = _layernorm(x + _L0_attn_ref(x, L0_attn_Wq, L0_attn_bq, L0_attn_Wk, L0_attn_bk, L0_attn_Wv, L0_attn_bv, L0_attn_Wo, L0_attn_bo), axis=-1)
    x = _layernorm(x + _L0_ffn_ref(x, L0_ffn_w_gate, L0_ffn_w_up, L0_ffn_w_down, L0_ffn_s_gate, L0_ffn_s_up, L0_ffn_s_down), axis=-1)
    x = _layernorm(x + _L1_attn_ref(x, L1_attn_Wq, L1_attn_Wk, L1_attn_Wv, L1_attn_Wa, L1_attn_ba, L1_attn_Wb, L1_attn_bb, L1_attn_Wg, L1_attn_Wo, L1_attn_conv_q_w, L1_attn_conv_q_b, L1_attn_conv_k_w, L1_attn_conv_k_b, L1_attn_conv_v_w, L1_attn_conv_v_b, L1_attn_ln_w, L1_attn_ln_b), axis=-1)
    x = _layernorm(x + _L1_ffn_ref(x, L1_ffn_up_weight, L1_ffn_down_weight, L1_ffn_up_scale, L1_ffn_down_scale, L1_ffn_output_scale), axis=-1)
    return x

_drawn_inputs = setup_inputs


def setup_inputs(seed=0):
    import zlib

    import numpy as np

    out = dict(_drawn_inputs(seed))
    spreads = {'L1_attn_ba': (0.0, 0.8),
     'L1_attn_bb': (0.0, 0.8),
     'L1_attn_conv_q_b': (0.0, 0.1),
     'L1_attn_conv_k_b': (0.0, 0.1),
     'L1_attn_conv_v_b': (0.0, 0.1),
     'L1_attn_ln_w': (1.0, 0.6),
     'L1_attn_ln_b': (0.0, 0.1),
     'L1_ffn_up_scale': (1.0, 0.2),
     'L1_ffn_down_scale': (1.0, 0.2)}
    factors = {'L0_attn_Wq': 8.0,
     'L0_attn_bq': 8.0,
     'L0_attn_Wk': 8.0,
     'L0_attn_bk': 8.0,
     'L0_attn_Wv': 4.381,
     'L0_attn_bv': 5.248,
     'L0_attn_Wo': 3.347,
     'L1_attn_Wa': 5.472,
     'L1_attn_Wb': 3.392,
     'L1_attn_Wg': 2.941,
     'L0_attn_bo': 2.906}
    for name, (base, spread) in spreads.items():
        noise = np.random.default_rng([zlib.crc32(name.encode()), seed]).standard_normal(out[name].shape)
        drawn = base * np.exp(spread * noise) if base else spread * noise
        out[name] = jnp.asarray(drawn.astype(out[name].dtype))
    for name, factor in factors.items():
        out[name] = (out[name] * factor).astype(out[name].dtype)
    return out
```

```python
from contextlib import ExitStack, contextmanager

import numpy as np
import concourse.bass as bass
from concourse import mybir

F32 = mybir.dt.float32
BF16 = mybir.dt.bfloat16
ALU = mybir.AluOpType
ACT = mybir.ActivationFunctionType
AX = mybir.AxisListType

B, T, E = 2, 1024, 256
P = 128
NT = B * T // P
TB = T // P
KE = E // P
TOK = B * T
HQ, HKV, D = 32, 8, 8
G = HQ // HKV
BIG = -1.0e30
HALF = 512
EPS = 1e-5


@contextmanager
def phase(nc):
    before = nc.snapshot_sems()
    with ExitStack() as ctx:
        yield ctx
    nc.clear_and_free_semaphores(nc.allocated_since(before))
    nc.all_engine_barrier()


COST = [72, 0.79, 1.5, 308, 790, 136]


class Loop:

    def __init__(self):
        self.i = 0

    def at(self, n, per):
        return n + self.i * per


def load_and_project(nc, ps, x_tok, cst, dram, w):
    with phase(nc) as ctx:
        sb = lambda n, s, d=F32: ctx.enter_context(nc.sbuf_tensor(n, s, d))
        sem = lambda n: nc.alloc_semaphore(n)
        xT = sb("p_xT", [P, KE, TOK])
        wq = sb("p_wq", [P, KE, 2, E])
        wk = sb("p_wk", [P, KE, 2, HKV * D])
        wv = sb("p_wv", [P, KE, HKV * D])
        bq = sb("p_bq", [P, 2, KE])
        bk = sb("p_bk", [HKV * D, 2])
        bv = sb("p_bv", [P, HKV * D])
        cos = sb("p_cos", [P, T])
        sin = sb("p_sin", [P, T])
        t1 = sb("p_t1", [P, 2, HALF])
        t2 = sb("p_t2", [P, 2, HALF])
        rot = sb("p_rot", [P, 2, HALF])
        rest = sb("p_rest", [P, 2, HALF])
        rest2 = sb("p_rest2", [P, 2, HALF])
        parts = sb("p_parts", [P, 2, 3, HALF], BF16)
        ident, v_aug = cst["ident"], cst["v_aug"]

        x_in, w_in = sem("p_x_in"), sem("p_w_in")
        transposed, xT_ready = sem("p_transposed"), sem("p_xT_ready")
        xT_done_act, xT_done_dve = sem("p_xT_act"), sem("p_xT_dve")
        projected = sem("p_projected")
        rotated, summed = sem("p_rotated"), sem("p_summed")
        high, high_left, mid = sem("p_high"), sem("p_high_left"), sem("p_mid")
        low, stored = sem("p_low"), [sem("p_stored0"), sem("p_stored1")]
        v_ready, v_added, v_clear = sem("p_v_ready"), sem("p_v_added"), sem("p_v_clear")

        NG = NT // 4 * KE
        NB = TOK // HALF
        kinds = [("q", 0), ("q", 1), ("k", 0)]
        jobs = [(kind, c, n) for kind, c in kinds for n in range(NB)]
        rows = {"q": P, "k": HKV * D}
        block = ctx.enter_context(nc.Block())

        @block.sync
        def _(sp):
            sp.dma_start(x_tok[:, 0:NT // 2, :], dram["x"][0:NT // 2].rearrange("n p c -> p n c")).then_inc(x_in, 16)
            sp.dma_start(x_tok[:, NT // 2:, :], dram["x"][NT // 2:].rearrange("n p c -> p n c")).then_inc(x_in, 16)
            sp.dma_start(wq[:], w["wq"].rearrange("(k p) s n -> p k s n", p=P)).then_inc(w_in, 16)
            sp.dma_start(wk[:], w["wk"].rearrange("(k p) s n -> p k s n", p=P)).then_inc(w_in, 16)
            sp.dma_start(wv[:], w["wv"].rearrange("(k p) n -> p k n", p=P)).then_inc(w_in, 16)
            sp.dma_start(bq[:], w["bq"]).then_inc(w_in, 16)
            sp.dma_start(bk[:], w["bk"]).then_inc(w_in, 16)
            sp.dma_start(bv[:], w["bv"].partition_broadcast(P)).then_inc(w_in, 16)
            sp.dma_start(cos[:], w["cos"]).then_inc(w_in, 16)
            sp.dma_start(sin[:], w["sin"]).then_inc(w_in, 16)
            for m, (kind, c, n) in enumerate(jobs):
                r = rows[kind]
                sp.wait_ge(low, m + 1)
                sp.dma_start(dram[kind][:, c * P:c * P + r, n * HALF:(n + 1) * HALF].rearrange("s p t -> p s t"),
                             parts[0:r, m % 2]).then_inc(stored[m % 2], 16)
            for s in range(2):
                sp.wait_ge(stored[s], 16 * (len(jobs) // 2))

        @block.tensor
        def _(pe):
            pe.wait_ge(cst["in"], cst["in_n"])
            for g in range(NG):
                k, t4 = g % KE, g // KE
                if g == 0:
                    pe.wait_ge(x_in, 32)
                if g >= 2:
                    pe.wait_ge(xT_done_act if g % 2 == 0 else xT_done_dve, g // 2)
                for a in range(4):
                    last = nc.tensor.transpose(ps[:, g % 2, a * P:(a + 1) * P],
                                               x_tok[:, t4 * 4 + a, k * P:(k + 1) * P], ident[:])
                last.then_inc(transposed, 1)
            pe.wait_ge(xT_done_act, NG // 2)
            pe.wait_ge(xT_done_dve, NG // 2)
            pe.wait_ge(w_in, 16 * 8)
            for n in range(NT):
                for k in range(KE):
                    last = nc.tensor.matmul(ps[:, 2 + n // 8, (n % 8) * 64:(n % 8) * 64 + 64],
                                            xT[:, k, n * P:(n + 1) * P], wv[:, k, :], start=(k == 0), stop=(k == KE - 1))
                last.then_inc(v_ready, 1)
            for m, (kind, c, n) in enumerate(jobs):
                r, wt = rows[kind], wq if kind == "q" else wk
                if m >= 2:
                    pe.wait_ge(rotated, 2 * (m - 1))
                for s in range(2):
                    for k in range(KE):
                        last = nc.tensor.matmul(ps[0:r, 4 + 2 * (m % 2) + s, :], wt[:, k, s, c * P:c * P + r],
                                                xT[:, k, n * HALF:(n + 1) * HALF], start=(k == 0), stop=(k == KE - 1))
                last.then_inc(projected, 1)

        @block.gpsimd
        def _(pool):
            nc.gpsimd.memset(v_aug[:], 0.0).then_inc(v_clear, 1)
            pool.wait_ge(v_clear, 1)
            nc.gpsimd.memset(v_aug[:, :, :, D:D + 1], 1.0).then_inc(v_clear, 1)
            U32 = mybir.dt.uint32
            for p in range(2):
                for buf in (cst["q1"][p], cst["q2"][p]):
                    nc.gpsimd.memset(buf[:].rearrange("p g t -> p (g t)").bitcast(U32), 0).then_inc(v_clear, 1)
                nc.gpsimd.memset(cst["k1"][p][:].bitcast(U32), 0).then_inc(v_clear, 1)
                nc.gpsimd.memset(cst["k2"][p][:], 1.0).then_inc(v_clear, 1)
            pool.wait_ge(v_clear, 10)
            for m, (kind, c, n) in enumerate(jobs):
                r = rows[kind]
                pool.wait_ge(rotated, 2 * m + 2)
                if m >= 2:
                    pool.wait_ge(high_left, m - 1)
                nc.gpsimd.tensor_tensor(rot[0:r, m % 2], t1[0:r, m % 2], t2[0:r, m % 2], ALU.add).then_inc(summed, 1)

        @block.scalar
        def _(act):
            for g in range(0, NG, 2):
                k, t4 = g % KE, g // KE
                act.wait_ge(transposed, g + 1)
                nc.scalar.activation(xT[:, k, t4 * HALF:(t4 + 1) * HALF], ps[:, g % 2, :], ACT.Copy).then_inc(xT_done_act, 1)
            for m, (kind, c, n) in enumerate(jobs):
                r = rows[kind]
                act.wait_ge(summed, m + 1)
                if m >= 2:
                    act.wait_ge(stored[m % 2], 16 * (m // 2))
                nc.scalar.activation(parts[0:r, m % 2, 0], rot[0:r, m % 2], ACT.Copy).then_inc(high, 1)
                act.wait_ge(high_left, m + 1)
                nc.scalar.activation(parts[0:r, m % 2, 1], rest[0:r, m % 2], ACT.Copy).then_inc(mid, 1)

        @block.vector
        def _(dve):
            for g in range(1, NG, 2):
                k, t4 = g % KE, g // KE
                dve.wait_ge(transposed, g + 1)
                nc.vector.tensor_copy(xT[:, k, t4 * HALF:(t4 + 1) * HALF], ps[:, g % 2, :]).then_inc(xT_done_dve, 1)
            dve.wait_ge(v_clear, 2)
            dve.wait_ge(w_in, 16 * 8)
            for n in range(NT):
                dve.wait_ge(v_ready, (n // 8 + 1) * 8)
                nc.vector.tensor_tensor(v_aug[:, n, :, 0:D],
                                        ps[:, 2 + n // 8, (n % 8) * 64:(n % 8) * 64 + 64].rearrange("p (h d) -> p h d", d=D),
                                        bv[:].rearrange("p (h d) -> p h d", d=D), ALU.add).then_inc(v_added, 1)
            def split(m):
                r = rows[jobs[m][0]]
                dve.wait_ge(high, m + 1)
                nc.vector.tensor_tensor(rest[0:r, m % 2], rot[0:r, m % 2], parts[0:r, m % 2, 0], ALU.subtract).then_inc(high_left, 1)

            def split_low(m):
                r = rows[jobs[m][0]]
                dve.wait_ge(mid, m + 1)
                nc.vector.tensor_tensor(parts[0:r, m % 2, 2], rest[0:r, m % 2], parts[0:r, m % 2, 1],
                                        ALU.subtract).then_inc(low, 1)

            for m, (kind, c, n) in enumerate(jobs):
                r = rows[kind]
                tt = (n * HALF) % T
                bias = bq if kind == "q" else bk
                dve.wait_ge(projected, m + 1)
                if m >= 2:
                    dve.wait_ge(summed, m - 1)
                b0 = bias[0:r, 0, c:c + 1] if kind == "q" else bias[0:r, 0:1]
                b1 = bias[0:r, 1, c:c + 1] if kind == "q" else bias[0:r, 1:2]
                nc.vector.scalar_tensor_tensor(t1[0:r, m % 2], ps[0:r, 4 + 2 * (m % 2), :], b0, cos[0:r, tt:tt + HALF],
                                               ALU.add, ALU.mult).then_inc(rotated, 1)
                nc.vector.scalar_tensor_tensor(t2[0:r, m % 2], ps[0:r, 5 + 2 * (m % 2), :], b1, sin[0:r, tt:tt + HALF],
                                               ALU.add, ALU.mult).then_inc(rotated, 1)
                if m >= 1:
                    split(m - 1)
                    split_low(m - 1)
            split(len(jobs) - 1)
            split_low(len(jobs) - 1)


Q_PARTS = (0, 0, 1, 0, 2, 1)
K_PARTS = (0, 1, 0, 2, 0, 1)
NPROD = len(Q_PARTS) * D
NROW = NPROD + 3
UNITS = B * HKV
VW = 32
MAXCOLS = TB + TB // 2


def head_pieces():
    out = []
    for i in range(TB):
        n = (i + 1) * P
        for c0 in range(0, n, HALF):
            w = min(HALF, n - c0)
            out.append((i, c0, w, c0 + w == n, i if c0 == 0 else TB + i - TB // 2))
    return out


def attention(nc, ps, y_tok, cst, dram):
    with phase(nc) as ctx:
        sb = lambda n, s, d=F32: ctx.enter_context(nc.sbuf_tensor(n, s, d))
        sem = lambda n: nc.alloc_semaphore(n)
        ident, identb, neg_qk, neg_kq, v_aug = (cst[n] for n in ("ident", "identb", "neg_qk", "neg_kq", "v_aug"))
        q1, k1, q2, k2 = (cst[n] for n in ("q1", "k1", "q2", "k2"))
        v1 = [sb(f"a_v_{p}", [P, TB, VW]) for p in range(2)]
        mx = sb("a_mx", [P, 2, G, MAXCOLS])
        nm = sb("a_nm", [P, 2, G, TB])
        nmT = sb("a_nmT", [G * TB, P])
        nrest = sb("a_nrest", [G * TB, 2, P])
        nparts = sb("a_nparts", [G * TB, 3, P], BF16)
        prob = sb("a_prob", [P, 2, G, T])
        oT = sb("a_oT", [P, T])
        rden = sb("a_rden", [P, TB, G])

        q1_in = [sem(f"a_q1_in{p}") for p in range(2)]
        q2_in = [sem(f"a_q2_in{p}") for p in range(2)]
        row_in = [sem(f"a_row_in{p}") for p in range(2)]
        scored = sem("a_scored")
        reduced = sem("a_reduced")
        piece_max = sem("a_piece_max")
        maxima = sem("a_maxima")
        copied = sem("a_copied")
        high, rest, mid, rest2, low = (sem(f"a_{n}") for n in ("high", "rest", "mid", "rest2", "low"))
        st_ready = sem("a_st_ready")
        st_exp = sem("a_st_exp")
        pv_done = sem("a_pv_done")
        o_copied = sem("a_o_copied")
        o_turned = sem("a_o_turned")
        o_recip = sem("a_o_recip")
        o_scaled = sem("a_o_scaled")
        v_in = sem("a_v_in")
        past = sem("a_past")
        block = ctx.enter_context(nc.Block())
        S1, ST, O = 0, 2, 6
        PIECES = head_pieces()
        ITEMS = len(PIECES) * G + 1
        STEPS = TB * G
        LOOPED = (UNITS - 2) // 2
        Q_DMAS = 16 * 2 * len(Q_PARTS)

        def items_of(heads):
            out = [("piece", u, g, x) for u, g in heads for x in PIECES]
            for n, (_, u, g, x) in enumerate(out):
                if g == G - 1 and x is PIECES[-1]:
                    out.insert(min(n + 5, len(out)), ("turn", u, None, None))
                    break
            return out

        FIRST = items_of([(0, g) for g in range(G)] + [(1, 0), (1, 1)])

        def stage_plan(u, last):
            heads = [] if u == last else [(u + 1, 2), (u + 1, 3)]
            if u + 2 <= last:
                heads += [(u + 2, 0), (u + 2, 1)]
            items = items_of(heads)
            steps = []
            for s in range(2, STEPS):
                steps.append((COST[0] + COST[1] * (T - s // G * P), ("scores", u, s, None)))
                if s % G == 1:
                    steps += [(COST[2] * (min(T, (h + 1) * HALF) - max(h * HALF, (s // G - 1) * P)), ("values", u, s // G - 1, h))
                              for h in range(2) if (s // G - 1) * P < (h + 1) * HALF]
            if u < last:
                steps += [(COST[0] + COST[1] * T, ("scores", u + 1, n, None)) for n in range(2)]
            steps += [(COST[3], ("values", u, TB - 1, 1)), (COST[4], ("output", u, None, None))]
            cost = lambda it: COST[5] + (it[3][2] if it[0] == "piece" else P)
            total, items_total = sum(c for c, _ in steps), sum(map(cost, items)) * 4 / max(1, len(heads))
            plan, done, items_done, n = [], 0, 0, 0
            for c, step in steps:
                if step[0] == "output":
                    done += c
                while n < len(items) and (items_done + cost(items[n]) / 2) * total <= done * items_total:
                    items_done += cost(items[n])
                    plan.append(items[n])
                    n += 1
                plan.append(step)
                if step[0] != "output":
                    done += c
            plan = plan[:-1] + items[n:] + plan[-1:]
            return plan

        def stages(eng, run, lp):
            with eng.Fori(0, LOOPED) as i:
                lp.i = i
                for u in range(2):
                    run(stage_plan(u, 99), i * 2)
            lp.i = LOOPED - 1
            for u in range(2, 4):
                run(stage_plan(u, 3), (LOOPED - 1) * 2)

        @block.sync
        def _(sp):
            lp = Loop()

            def load(dst_q, dst_k, u, arrived):
                b, kv = u // HKV, u % HKV
                for j in range(len(Q_PARTS)):
                    sp.dma_start(dst_q[j * D:(j + 1) * D, :, :],
                                 dram["q"][Q_PARTS[j], bass.ds(kv * (G * D), G * D), bass.ds(b * T, T)]
                                 .rearrange("(g d) t -> d g t", d=D)).then_inc(arrived, 16)
                    sp.dma_start(dst_k[j * D:(j + 1) * D, :],
                                 dram["k"][K_PARTS[j], bass.ds(kv * D, D), bass.ds(b * T, T)]).then_inc(arrived, 16)

            def rows(p):
                for j in range(3):
                    sp.dma_start(q2[p][NPROD + j:NPROD + j + 1, :, :].rearrange("o g (i t) -> o (g i) t", t=P),
                                 nparts[:, j, :]).then_inc(row_in[p], 16)

            load(q1[0], k1[0], 0, q1_in[0])
            load(q1[1], k1[1], 1, q1_in[1])
            load(q2[0], k2[0], 0, q2_in[0])
            sp.wait_ge(low, 1)
            rows(0)

            def stage(u, n, ahead):
                p = n % 2
                if ahead == 2:
                    sp.wait_ge(maxima, lp.at(n + 1, 2))
                    load(q1[p], k1[p], u + 2, q1_in[p])
                sp.wait_ge(pv_done, lp.at(TB * n + 2, 2 * TB))
                load(q2[1 - p], k2[1 - p], u + 1, q2_in[1 - p])
                sp.wait_ge(low, lp.at(n + 2, 2))
                rows(1 - p)

            with sp.Fori(0, LOOPED) as i:
                lp.i = i
                stage(i * 2, 0, 2)
                stage(i * 2 + 1, 1, 2)
            lp.i = LOOPED - 1
            stage(UNITS - 2, 2, 1)

        @block.gpsimd
        def _(pool):
            lp = Loop()
            def values(u, n):
                nc.gpsimd.tensor_copy(v1[n % 2][:], v_aug[:, bass.ds((u // HKV) * TB, TB), bass.ds(u % HKV, 1), :]
                                      .rearrange("p n o c -> p n (o c)")).then_inc(v_in, 1)

            def cut(n):
                c = lp.at(n + 1, 2)
                pool.wait_ge(copied, c)
                pool.sem_inc(past, 1)
                nc.gpsimd.tensor_copy(nparts[:, 0, :], nmT[:]).then_inc(high, 1)
                pool.wait_ge(high, c)
                nc.gpsimd.tensor_tensor(nrest[:, 0, :], nmT[:], nparts[:, 0, :], ALU.subtract).then_inc(rest, 1)
                pool.wait_ge(rest, c)
                pool.sem_inc(past, 1)
                nc.gpsimd.tensor_copy(nparts[:, 1, :], nrest[:, 0, :]).then_inc(mid, 1)
                pool.wait_ge(mid, c)
                nc.gpsimd.tensor_tensor(nrest[:, 1, :], nrest[:, 0, :], nparts[:, 1, :], ALU.subtract).then_inc(rest2, 1)
                pool.wait_ge(rest2, c)
                pool.sem_inc(past, 1)
                nc.gpsimd.tensor_copy(nparts[:, 2, :], nrest[:, 1, :]).then_inc(low, 1)

            values(0, 0)
            cut(0)

            def stage(u, n):
                pool.wait_ge(pv_done, lp.at(TB * n + 2, 2 * TB))
                values(u + 1, n + 1)
                pool.wait_ge(row_in[n % 2], lp.at(48 * (n // 2 + 1), 48))
                cut(n + 1)

            with pool.Fori(0, LOOPED) as i:
                lp.i = i
                stage(i * 2, 0)
                stage(i * 2 + 1, 1)
            lp.i = LOOPED - 1
            stage(UNITS - 2, 2)

        @block.tensor
        def _(pe):
            lp = Loop()
            n_item, n_step, n_pv, n_out = [0], [0], [0], [0]

            def item(it):
                kind, u, g, x = it
                p, bank = u % 2, S1 + n_item[0] % 2
                n_item[0] += 1
                if kind == "piece":
                    i, c0, w, diagonal, _ = x
                    if g == 0 and x is PIECES[0]:
                        pe.wait_ge(q1_in[p], lp.at(Q_DMAS * (u // 2 + 1), Q_DMAS))
                    pe.wait_ge(reduced, lp.at(n_item[0], 2 * ITEMS))
                    q = q1[p][:, g, i * P:(i + 1) * P]
                    last = nc.tensor.matmul(ps[:, bank, 0:w], q, k1[p][:, c0:c0 + w], start=True, stop=not diagonal)
                    if diagonal:
                        last = nc.tensor.matmul(ps[:, bank, w - P:w], identb[:], neg_qk[:], start=False, stop=True)
                else:
                    pe.wait_ge(maxima, lp.at(u + 1, 2))
                    pe.wait_ge(reduced, lp.at(n_item[0], 2 * ITEMS))
                    last = nc.tensor.transpose(ps[0:G * TB, bank, 0:P], nm[:, p].rearrange("p g i -> p (g i)"), ident[:])
                last.then_inc(scored, 1)

            def scores(u, s):
                j, g = s // G, s % G
                p, bank = u % 2, ST + 2 * (s % 2)
                n_step[0] += 1
                if s == 0:
                    pe.wait_ge(q2_in[p], lp.at(Q_DMAS * (u // 2 + 1), Q_DMAS))
                    pe.wait_ge(row_in[p], lp.at(48 * (u // 2 + 1), 48))
                pe.wait_ge(st_exp, lp.at(n_step[0], 2 * STEPS))
                k = k2[p][:, j * P:(j + 1) * P]
                c0 = j * P
                while c0 < T:
                    w = min(HALF - c0 % HALF, T - c0)
                    out = ps[:, bank + c0 // HALF, c0 % HALF:c0 % HALF + w]
                    masked = c0 == j * P
                    last = nc.tensor.matmul(out, k, q2[p][:, g, c0:c0 + w], start=True, stop=not masked)
                    if masked:
                        last = nc.tensor.matmul(out[:, 0:P], identb[:], neg_kq[:], start=False, stop=True)
                    c0 += w
                last.then_inc(st_ready, 1)

            def products(u, j, half):
                p = u % 2
                first = half == 0 or j * P >= HALF
                n_pv[0] += first
                if j == 0 and first:
                    pe.wait_ge(v_in, lp.at(u + 1, 2))
                    pe.wait_ge(o_scaled, lp.at(u + 1, 2))
                if first:
                    pe.wait_ge(st_exp, lp.at(2 + G * n_pv[0], 2 * STEPS))
                c0, c1 = max(j * P, half * HALF), (half + 1) * HALF
                for g in range(G):
                    last = nc.tensor.matmul(ps[g * VW:(g + 1) * VW, O + half, c0 % HALF:c0 % HALF + c1 - c0], v1[p][:, j, :],
                                            prob[:, j % 2, g, c0:c1], start=(j == 0),
                                            stop=(j == min(TB - 1, c1 // P - 1)), skip_group_check=True)
                if half == 1:
                    last.then_inc(pv_done, 1)

            def output(u):
                n_out[0] += 1
                pe.wait_ge(o_copied, lp.at(n_out[0], 2))
                for i in range(TB):
                    last = nc.tensor.transpose(ps[:, O + i // 4, (i % 4) * P:(i % 4 + 1) * P], oT[:, i * P:(i + 1) * P], ident[:])
                last.then_inc(o_turned, 1)

            def run(plan, _):
                for ev in plan:
                    if ev[0] == "scores":
                        scores(ev[1], ev[2])
                    elif ev[0] == "values":
                        products(ev[1], ev[2], ev[3])
                    elif ev[0] == "output":
                        output(ev[1])
                    else:
                        item(ev)

            pe.sem_inc(pv_done, 2)
            for it in FIRST:
                item(it)
            scores(0, 0)
            scores(0, 1)
            stages(pe, run, lp)

        @block.scalar
        def _(act):
            lp = Loop()
            n_step, n_out = [0], [0]
            act.sem_inc(st_exp, 2)

            def exponentials(u, s):
                j, g = s // G, s % G
                n_step[0] += 1
                act.wait_ge(st_ready, lp.at(n_step[0], 2 * STEPS))
                if g == 0:
                    act.wait_ge(pv_done, lp.at(TB * u + j + 1, 2 * TB))
                bank = ST + 2 * (s % 2)
                st = ps[:, bank:bank + 2, :].rearrange("p b c -> p (b c)")
                nc.scalar.activation(prob[:, j % 2, g, j * P:T], st[:, j * P:T], ACT.Exp, scale=float(D) ** -0.5).then_inc(st_exp, 1)

            def output(u):
                n_out[0] += 1
                act.wait_ge(pv_done, lp.at(TB * n_out[0] + 2, 2 * TB))
                nc.scalar.activation(oT[:], ps[:, O:O + 2, :].rearrange("p b c -> p (b c)"), ACT.Copy).then_inc(o_copied, 1)

            def run(plan, _):
                for ev in plan:
                    if ev[0] == "scores":
                        exponentials(ev[1], ev[2])
                    elif ev[0] == "output":
                        output(ev[1])

            exponentials(0, 0)
            exponentials(0, 1)
            stages(act, run, lp)

        @block.vector
        def _(dve):
            lp = Loop()
            n_item, n_out = [0], [0]
            dve.sem_inc(reduced, 2)
            dve.sem_inc(o_scaled, 1)

            def item(it):
                kind, u, g, x = it
                p, bank = u % 2, S1 + n_item[0] % 2
                n_item[0] += 1
                dve.wait_ge(scored, lp.at(n_item[0], 2 * ITEMS))
                if kind == "turn":
                    dve.wait_ge(low, lp.at(u, 2)) if u else None
                    nc.vector.tensor_copy(nmT[:], ps[0:G * TB, bank, 0:P]).then_inc(copied, 1)
                    dve.wait_ge(copied, lp.at(u + 1, 2))
                    dve.sem_inc(reduced, 1)
                    return
                i, c0, w, diagonal, col = x
                nc.vector.tensor_reduce(mx[:, p, g, col:col + 1], ps[:, bank, 0:w], AX.X, ALU.max, negate=True).then_inc(reduced, 1)
                if g == G - 1 and x is PIECES[-1]:
                    dve.wait_ge(reduced, lp.at(n_item[0] + 2, 2 * ITEMS))
                    nc.vector.tensor_copy(nm[:, p, :, 0:TB // 2], mx[:, p, :, 0:TB // 2]).then_inc(piece_max, 1)
                    dve.wait_ge(piece_max, lp.at(u + 1, 2))
                    nc.vector.tensor_tensor(nm[:, p, :, TB // 2:], mx[:, p, :, TB // 2:TB], mx[:, p, :, TB:], ALU.min).then_inc(maxima, 1)

            def output(u, base):
                n_out[0] += 1
                unit = base + u
                dve.wait_ge(o_turned, lp.at(n_out[0], 2))
                o = ps[:, O:O + 2, :].rearrange("p b (i g c) -> p (b i) g c", g=G, c=VW)
                nc.vector.reciprocal(rden[:], o[:, :, :, D]).then_inc(o_recip, 1)
                dve.wait_ge(o_recip, lp.at(n_out[0], 2))
                y = y_tok[:, bass.ds((unit // HKV) * TB, TB), bass.ds((unit % HKV) * (G * D), G * D)]
                nc.vector.tensor_tensor(y.rearrange("p i (g d) -> p i g d", d=D), o[:, :, :, 0:D],
                                        rden[:].unsqueeze(3).to_broadcast([P, TB, G, D]), ALU.mult).then_inc(o_scaled, 1)

            def run(plan, base):
                for ev in plan:
                    if ev[0] in ("piece", "turn"):
                        item(ev)
                    elif ev[0] == "output":
                        output(ev[1], base)

            for it in FIRST:
                item(it)
            stages(dve, run, lp)


BLK = TOK // HALF
BT = HALF // P


class Norm:

    def __init__(self, nc, ctx, name, x_tok, cst):
        sb = lambda n, s, d=F32: ctx.enter_context(nc.sbuf_tensor(f"{name}_{n}", s, d))
        sem = lambda n: nc.alloc_semaphore(f"{name}_{n}")
        self.nc, self.x, self.pow_half = nc, x_tok, cst["pow_half"]
        self.tmp, self.st = sb("tmp", [P, BT, E]), sb("st", [P, BT, 6])
        self.mv, self.rs = sb("mv", [P, 2, BT, 2]), sb("rs", [P, 2, 2, BT])
        self.chain, self.links = sem("chain"), 0
        self.stats, self.eps_in, self.rstd, self.done = sem("stats"), sem("eps_in"), sem("rstd"), sem("normed")

    def link(self, dve, ins):
        self.links += 1
        ins.then_inc(self.chain, 1)
        dve.wait_ge(self.chain, self.links)

    def residual(self, dve, n, acc, scale, freed):
        nc, xs = self.nc, self.x[:, n * BT:(n + 1) * BT, :]
        if scale is None:
            ins = nc.vector.tensor_tensor(xs, acc, xs, ALU.add)
        else:
            self.link(dve, nc.vector.tensor_tensor(self.tmp[:], acc, scale.unsqueeze(1).to_broadcast([P, BT, E]), ALU.mult))
            ins = nc.vector.tensor_tensor(xs, self.tmp[:], xs, ALU.add)
        ins.then_inc(freed, 1)
        dve.wait_ge(freed, n + 1)
        for a in range(BT):
            ins = nc.vector.bn_stats(self.st[:, a, :], xs[:, a, :])
        self.link(dve, ins)
        if n >= 2:
            dve.wait_ge(self.done, n - 1)
        for a in range(BT):
            ins = nc.vector.bn_aggr(self.mv[:, n % 2, a, :], self.st[:, a, :])
        ins.then_inc(self.stats, 1)

    def inverse_root(self, pool, n):
        nc = self.nc
        pool.wait_ge(self.stats, n + 1)
        nc.gpsimd.tensor_scalar(self.rs[:, n % 2, 0], self.mv[:, n % 2, :, 1], EPS, None, ALU.add).then_inc(self.eps_in, 1)
        pool.wait_ge(self.eps_in, n + 1)
        nc.gpsimd.tensor_tensor(self.rs[:, n % 2, 1], self.rs[:, n % 2, 0], self.pow_half[:, 0:BT], ALU.pow).then_inc(self.rstd, 1)

    def normalise(self, dve, n):
        nc, xs = self.nc, self.x[:, n * BT:(n + 1) * BT, :]
        dve.wait_ge(self.rstd, n + 1)
        for a in range(BT):
            ins = nc.vector.tensor_scalar(xs[:, a, :], xs[:, a, :], self.mv[:, n % 2, a, 0:1], self.rs[:, n % 2, 1, a:a + 1],
                                          ALU.subtract, ALU.mult)
        ins.then_inc(self.done, 1)


def pair_view(ps, bank):
    return ps[:, bank:bank + 2, :].rearrange("p b (h c) -> p (b h) c", c=E)


def output_projection(nc, ps, x_tok, y_tok, cst, w):
    with phase(nc) as ctx:
        sb = lambda n, s, d=F32: ctx.enter_context(nc.sbuf_tensor(n, s, d))
        sem = lambda n: nc.alloc_semaphore(n)
        yT = sb("o_yT", [P, 2, KE, HALF])
        wo, bo = sb("o_wo", [P, KE, E]), sb("o_bo", [P, E])
        w_in, biased = sem("o_w_in"), sem("o_biased")
        turned, evacuated, projected, freed = sem("o_turned"), sem("o_evacuated"), sem("o_projected"), sem("o_freed")
        norm = Norm(nc, ctx, "o", x_tok, cst)
        ident = cst["ident"]
        block = ctx.enter_context(nc.Block())

        @block.sync
        def _(sp):
            sp.dma_start(wo[:], w["wo"].rearrange("(k p) n -> p k n", p=P)).then_inc(w_in, 16)
            sp.dma_start(bo[:], w["bo"].partition_broadcast(P)).then_inc(w_in, 16)

        @block.tensor
        def _(pe):
            def turn(n):
                for k in range(KE):
                    if n >= 1:
                        pe.wait_ge(evacuated, KE * (n - 1) + k + 1)
                    for a in range(BT):
                        last = nc.tensor.transpose(ps[:, k, a * P:(a + 1) * P], y_tok[:, n * BT + a, k * P:(k + 1) * P], ident[:])
                    last.then_inc(turned, 1)

            turn(0)
            pe.wait_ge(w_in, 32)
            for n in range(BLK):
                if n + 1 < BLK:
                    turn(n + 1)
                pe.wait_ge(evacuated, KE * (n + 1))
                if n >= 2:
                    pe.wait_ge(freed, n - 1)
                for a in range(BT):
                    for k in range(KE):
                        last = nc.tensor.matmul(ps[:, 2 + 2 * (n % 2) + a // 2, (a % 2) * E:(a % 2 + 1) * E],
                                                yT[:, n % 2, k, a * P:(a + 1) * P], wo[:, k, :], start=(k == 0), stop=(k == KE - 1))
                last.then_inc(projected, 1)

        @block.scalar
        def _(act):
            for n in range(BLK):
                for k in range(KE):
                    act.wait_ge(turned, KE * n + k + 1)
                    if n >= 2:
                        act.wait_ge(projected, n - 1)
                    nc.scalar.activation(yT[:, n % 2, k, :], ps[:, k, :], ACT.Copy).then_inc(evacuated, 1)

        @block.gpsimd
        def _(pool):
            pool.wait_ge(w_in, 32)
            for n in range(BLK):
                nc.gpsimd.tensor_tensor(x_tok[:, n * BT:(n + 1) * BT, :], x_tok[:, n * BT:(n + 1) * BT, :],
                                        bo[:].unsqueeze(1).to_broadcast([P, BT, E]), ALU.add).then_inc(biased, 1)
            for n in range(BLK):
                norm.inverse_root(pool, n)

        @block.vector
        def _(dve):
            for n in range(BLK):
                dve.wait_ge(biased, n + 1)
                dve.wait_ge(projected, n + 1)
                norm.residual(dve, n, pair_view(ps, 2 + 2 * (n % 2)), None, freed)
                if n >= 1:
                    norm.normalise(dve, n - 1)
            norm.normalise(dve, BLK - 1)


def feed_forward(nc, ps, x_tok, cst, w, gated, out=None):
    FF = 1024
    NC = FF // P
    t = "g" if gated else "s"
    NU = 2 if gated else 1
    with phase(nc) as ctx:
        sb = lambda n, s, d=F32: ctx.enter_context(nc.sbuf_tensor(f"{t}_{n}", s, d))
        sem = lambda n: nc.alloc_semaphore(f"{t}_{n}")
        xT = sb("xT", [P, 2, KE, HALF])
        wu = sb("wu", [P, NU, KE, FF])
        wd = sb("wd", [P, NC, E])
        if gated:
            in_u, in_d = sb("raw_u", [P, NU, KE, FF // 4], mybir.dt.int32), sb("raw_d", [P, NC, E // 4], mybir.dt.int32)
            raw_u, raw_d = in_u[:].bitcast(mybir.dt.int8), in_d[:].bitcast(mybir.dt.int8)
        else:
            in_u, in_d = sb("raw_u", [P, NU, KE, FF]), sb("raw_d", [P, NC, E])
            raw_u, raw_d = in_u, in_d
        up_scale = sb("up_scale", [P, NU, NC])
        down_scale = sb("down_scale", [P, E])
        out_scale = sb("out_scale", [P, 1])
        h1 = sb("h1", [P, 2, HALF])
        h = sb("h", [P, 2, NC, HALF])
        w_in, cast, cast_d = sem("w_in"), sem("cast"), sem("cast_d")
        turned, evacuated, uped, act_done = sem("turned"), sem("evacuated"), sem("uped"), sem("act_done")
        h_ready, downed, freed = sem("h_ready"), sem("downed"), sem("freed")
        scaled, stored, neg = sem("scaled"), sem("stored"), sem("neg")
        norm = Norm(nc, ctx, t, x_tok, cst)
        ident = cst["ident"]
        N_W = 16 * (NU + 3 + (0 if gated else 1))
        block = ctx.enter_context(nc.Block())
        UP, DOWN = 2, 6

        @block.sync
        def _(sp):
            for s in range(NU):
                sp.dma_start(in_u[:, s], w["up"][s].rearrange("(k p) n -> p k n", p=P)).then_inc(w_in, 16)
            sp.dma_start(in_d[:], w["down"].rearrange("(c p) n -> p c n", p=P)).then_inc(w_in, 16)
            sp.dma_start(up_scale[:], w["up_scale"]).then_inc(w_in, 16)
            sp.dma_start(down_scale[:], w["down_scale"].partition_broadcast(P)).then_inc(w_in, 16)
            if not gated:
                sp.dma_start(out_scale[:], w["out_scale"].partition_broadcast(P)).then_inc(w_in, 16)
            if out is not None:
                for n in range(BLK):
                    sp.wait_ge(norm.done, n + 1)
                    sp.dma_start(out[n * BT:(n + 1) * BT].rearrange("n p c -> p n c"), x_tok[:, n * BT:(n + 1) * BT, :]).then_inc(stored, 16)
                sp.wait_ge(stored, 16 * BLK)

        @block.tensor
        def _(pe):
            def turn(n):
                for k in range(KE):
                    if n >= 1:
                        pe.wait_ge(evacuated, KE * (n - 1) + k + 1)
                    for a in range(BT):
                        last = nc.tensor.transpose(ps[:, k, a * P:(a + 1) * P], x_tok[:, n * BT + a, k * P:(k + 1) * P], ident[:])
                    last.then_inc(turned, 1)

            def down(n, last_wait):
                pe.wait_ge(h_ready, last_wait)
                if n >= 1:
                    pe.wait_ge(freed, n)
                for a in range(BT):
                    for c in range(NC):
                        last = nc.tensor.matmul(ps[:, DOWN + a // 2, (a % 2) * E:(a % 2 + 1) * E], h[:, n % 2, c, a * P:(a + 1) * P],
                                                wd[:, c, :], start=(c == 0), stop=(c == NC - 1))
                last.then_inc(downed, 1)

            turn(0)
            pe.wait_ge(cast, NU)
            m = 0
            for n in range(BLK):
                if n + 1 < BLK:
                    turn(n + 1)
                pe.wait_ge(evacuated, KE * (n + 1))
                for c in range(NC):
                    if m >= 2:
                        pe.wait_ge(h_ready, m - 1)
                    for s in range(NU):
                        for k in range(KE):
                            last = nc.tensor.matmul(ps[:, UP + 2 * (m % 2) + s, :], wu[:, s, k, c * P:(c + 1) * P], xT[:, n % 2, k, :],
                                                    start=(k == 0), stop=(k == KE - 1))
                    last.then_inc(uped, 1)
                    m += 1
                    if c == 1 and n >= 1:
                        if n == 1:
                            pe.wait_ge(cast_d, 1)
                        down(n - 1, NC * n)
            down(BLK - 1, NC * BLK)

        @block.scalar
        def _(act):
            act.wait_ge(w_in, N_W)
            if gated:
                for s in range(NU):
                    nc.scalar.activation(wu[:, s], raw_u[:, s], ACT.Copy).then_inc(cast, 1)
                nc.scalar.activation(wd[:], raw_d[:], ACT.Copy).then_inc(cast_d, 1)
            for n in range(BLK):
                for k in range(KE):
                    act.wait_ge(turned, KE * n + k + 1)
                    if n >= 2:
                        act.wait_ge(uped, NC * (n - 1))
                    nc.scalar.activation(xT[:, n % 2, k, :], ps[:, k, :], ACT.Copy).then_inc(evacuated, 1)
                for c in range(NC):
                    m = n * NC + c
                    act.wait_ge(uped, m + 1)
                    if n >= 2 and c == 0:
                        act.wait_ge(downed, n - 1)
                    if gated:
                        if m >= 2:
                            act.wait_ge(h_ready, m - 1)
                        nc.scalar.activation(h1[:, m % 2], ps[:, UP + 2 * (m % 2), :], ACT.Silu, scale=up_scale[:, 0, c:c + 1]).then_inc(act_done, 1)
                    else:
                        nc.scalar.activation(h[:, n % 2, c, :], ps[:, UP + 2 * (m % 2), :], ACT.Relu, scale=up_scale[:, 0, c:c + 1]).then_inc(h_ready, 1)

        @block.gpsimd
        def _(pool):
            for n in range(BLK):
                norm.inverse_root(pool, n)

        @block.vector
        def _(dve):
            dve.wait_ge(w_in, N_W)
            if not gated:
                nc.vector.tensor_scalar(wu[:, 0], raw_u[:, 0], 0.0, None, ALU.is_lt).then_inc(neg, 1)
                nc.vector.tensor_scalar(wd[:], raw_d[:], 0.0, None, ALU.is_lt).then_inc(neg, 1)
                norm.link(dve, nc.vector.tensor_scalar(down_scale[:], down_scale[:], out_scale[:, 0:1], None, ALU.mult))
                dve.wait_ge(neg, 2)
                fl = lambda v: v.rearrange("p a b -> p (a b)")
                nc.vector.scalar_tensor_tensor(fl(wu[:, 0]), fl(raw_u[:, 0]), 0.0, fl(wu[:, 0]), ALU.is_gt, ALU.subtract).then_inc(cast, 1)
                nc.vector.scalar_tensor_tensor(fl(wd[:]), fl(raw_d[:]), 0.0, fl(wd[:]), ALU.is_gt, ALU.subtract).then_inc(cast_d, 1)

            def close(n):
                dve.wait_ge(downed, n + 1)
                norm.residual(dve, n, pair_view(ps, DOWN), down_scale[:], freed)

            for n in range(BLK):
                for c in range(NC):
                    m = n * NC + c
                    if gated:
                        dve.wait_ge(act_done, m + 1)
                        if n >= 2 and c == 0:
                            dve.wait_ge(downed, n - 1)
                        nc.vector.scalar_tensor_tensor(h[:, n % 2, c, :], ps[:, UP + 2 * (m % 2) + 1, :], up_scale[:, 1, c:c + 1],
                                                       h1[:, m % 2], ALU.mult, ALU.mult).then_inc(h_ready, 1)
                    if c == 3 and n >= 1:
                        close(n - 1)
                    if c == 5 and n >= 1:
                        norm.normalise(dve, n - 1)
            close(BLK - 1)
            norm.normalise(dve, BLK - 1)


H, DK = 16, 128
HUNITS = B * H
QB = 32
LEVELS = (2, 4, 8, 16)
S_LA, S_BETA, S_NGEX, S_G, S_BGC, S_GC = range(6)
NS = 6


def delta_inputs(g):
    w = np.stack([g["L1_attn_" + n].reshape(KE, P, H, DK) for n in ("Wk", "Wq", "Wv", "Wg")])
    conv = np.stack([g[f"L1_attn_conv_{n}_w"].reshape(H, DK, 4) for n in "kqv"])
    bias = np.stack([g[f"L1_attn_conv_{n}_b"].reshape(H, DK) for n in "kqv"])
    par = np.concatenate([conv.transpose(1, 2, 0, 3).reshape(H, DK, 12), bias.transpose(1, 2, 0),
                          np.zeros((H, DK, 1), np.float32)], 2)
    rows, cols = np.arange(P)[:, None], np.arange(P)[None, :]
    r, c = np.arange(P)[:, None] % QB, np.arange(QB)[None, :]
    low = [((r // n) % 2 == 1) & (c // n == r // n - 1) for n in LEVELS]
    first = (r % 2 == 0) & (c == r + 1)
    half = 0.5 * np.ones((1, 16), np.float32)
    half[0, 0:4] = half[0, 12] = 0.5 * DK ** -0.5
    return {
        "dw": w.transpose(3, 2, 1, 0, 4), "dpar": par, "wab": np.concatenate([g["L1_attn_Wa"], g["L1_attn_Wb"]], 1),
        "bab": np.concatenate([g["L1_attn_ba"], g["L1_attn_bb"]]), "ln": np.stack([g["L1_attn_ln_w"], g["L1_attn_ln_b"]], 1),
        "wo1": g["L1_attn_Wo"],
        "c_half": half.astype(np.float32),
        "c_below": (rows > cols).astype(np.float32),
        "c_low": np.stack(low, 1).astype(np.float32),
        "c_first": -first.astype(np.float32),
        "c_eye": (r == c).astype(np.float32),
    }


def delta_scalars(nc, ps, x_tok, xT, sc, cst, a):
    with phase(nc) as ctx:
        sb = lambda n, s, d=F32: ctx.enter_context(nc.sbuf_tensor(f"e_{n}", s, d))
        sem = lambda n: nc.alloc_semaphore(f"e_{n}")
        wab, bab, ones = sb("wab", [P, KE, 2 * H]), sb("bab", [P, 2 * H]), sb("ones", [P, P])
        z, mag, em, ln1 = sb("z", [P, NT, 2 * H]), sb("mag", [P, NT, H]), sb("em", [P, NT, H]), sb("ln1", [P, NT, H])
        eb, eb1 = sb("eb", [P, NT, H]), sb("eb1", [P, NT, H])
        gl = sb("gl", [P, 4, HUNITS * TB])
        la = sb("la", [P, HUNITS, TB])
        w_in, turned, out_a, out_d = sem("w_in"), sem("turned"), sem("out_a"), sem("out_d")
        logits, zs, mags, exps, lns, las, chain = (sem(n) for n in ("logits", "zs", "mags", "exps", "lns", "las", "chain"))
        sums, decays, ones_made = sem("sums"), sem("decays"), sem("ones_made")
        ident, upto, above, below = cst["ident"], cst["upto"], cst["above"], cst["below"]
        NG = NT // 4 * KE
        block = ctx.enter_context(nc.Block())
        by_unit = lambda t: t.rearrange("p (b c) h -> p b h c", b=B)

        @block.sync
        def _(sp):
            sp.dma_start(wab[:], a["wab"].rearrange("(k p) n -> p k n", p=P)).then_inc(w_in, 16)
            sp.dma_start(bab[:], a["bab"].partition_broadcast(P)).then_inc(w_in, 16)

        @block.gpsimd
        def _(pool):
            nc.gpsimd.memset(ones[:], 1.0).then_inc(ones_made, 1)

        @block.tensor
        def _(pe):
            for g in range(NG):
                k, t4 = g % KE, g // KE
                if g >= 2:
                    pe.wait_ge(out_a if g % 2 == 0 else out_d, g // 2)
                for i in range(4):
                    last = nc.tensor.transpose(ps[:, g % 2, i * P:(i + 1) * P], x_tok[:, t4 * 4 + i, k * P:(k + 1) * P], ident[:])
                last.then_inc(turned, 1)
            pe.wait_ge(out_a, NG // 2)
            pe.wait_ge(out_d, NG // 2)
            pe.wait_ge(w_in, 32)
            for n in range(NT):
                for k in range(KE):
                    last = nc.tensor.matmul(ps[:, 2, n * 2 * H:(n + 1) * 2 * H], xT[:, k, n * P:(n + 1) * P], wab[:, k, :],
                                            start=(k == 0), stop=(k == KE - 1))
            last.then_inc(logits, 1)
            pe.wait_ge(las, B)
            pe.wait_ge(ones_made, 1)
            flat = la[:].rearrange("p u c -> p (u c)")
            for n, m in enumerate((above, upto, below, ones)):
                nc.tensor.matmul(ps[:, 4 + n, 0:HUNITS * TB], m[:], flat, start=True, stop=True).then_inc(sums, 1)

        @block.scalar
        def _(act):
            for g in range(0, NG, 2):
                act.wait_ge(turned, g + 1)
                nc.scalar.activation(xT[:, g % KE, g // KE * HALF:(g // KE + 1) * HALF], ps[:, g % 2, :], ACT.Copy).then_inc(out_a, 1)
            act.wait_ge(mags, 1)
            nc.scalar.activation(em[:], mag[:], ACT.Exp, scale=-1.0).then_inc(exps, 1)
            nc.scalar.activation(eb[:], z[:, :, H:2 * H], ACT.Exp, scale=-1.0).then_inc(exps, 1)
            act.wait_ge(exps, 1)
            nc.scalar.activation(ln1[:], em[:], ACT.Ln, bias=1.0).then_inc(lns, 1)
            act.wait_ge(sums, 4)
            for n in range(4):
                nc.scalar.activation(gl[:, n, :], ps[:, 4 + n, 0:HUNITS * TB], ACT.Exp).then_inc(decays, 1)

        @block.vector
        def _(dve):
            n = [0]

            def link(ins):
                n[0] += 1
                ins.then_inc(chain, 1)
                dve.wait_ge(chain, n[0])

            for g in range(1, NG, 2):
                dve.wait_ge(turned, g + 1)
                nc.vector.tensor_copy(xT[:, g % KE, g // KE * HALF:(g // KE + 1) * HALF], ps[:, g % 2, :]).then_inc(out_d, 1)
            dve.wait_ge(w_in, 32)
            dve.wait_ge(logits, 1)
            nc.vector.tensor_tensor(z[:], ps[:, 2, :].rearrange("p (n h) -> p n h", h=2 * H),
                                    bab[:].unsqueeze(1).to_broadcast([P, NT, 2 * H]), ALU.add).then_inc(zs, 1)
            dve.wait_ge(zs, 1)
            nc.vector.scalar_tensor_tensor(mag[:], z[:, :, 0:H], -1.0, z[:, :, 0:H], ALU.mult, ALU.max).then_inc(mags, 1)
            dve.wait_ge(exps, 2)
            link(nc.vector.tensor_scalar(eb1[:], eb[:], 1.0, None, ALU.add))
            link(nc.vector.reciprocal(eb[:], eb1[:]))
            for b in range(B):
                link(nc.vector.tensor_copy(sc[:, b * H:(b + 1) * H, S_BETA, :], by_unit(eb[:])[:, b]))
            dve.wait_ge(lns, 1)
            for b in range(B):
                nc.vector.scalar_tensor_tensor(la[:, b * H:(b + 1) * H, :], by_unit(z[:, :, 0:H])[:, b], 0.0, by_unit(ln1[:])[:, b],
                                               ALU.min, ALU.subtract).then_inc(las, 1)
            dve.wait_ge(las, B)
            link(nc.vector.tensor_copy(sc[:, :, S_LA, :], la[:]))
            dve.wait_ge(decays, 4)
            u = lambda t: t.rearrange("p (u c) -> p u c", c=TB)
            link(nc.vector.tensor_scalar(sc[:, :, S_NGEX, :], u(gl[:, 0]), -1.0, None, ALU.mult))
            link(nc.vector.tensor_copy(sc[:, :, S_G, :], u(gl[:, 1])))
            link(nc.vector.tensor_tensor(sc[:, :, S_BGC, :], u(gl[:, 2]), sc[:, :, S_BETA, :], ALU.mult))
            link(nc.vector.tensor_copy(sc[:, :, S_GC, :], u(gl[:, 3])))


TIMES = {"load": 0.0, "A0": 0.05, "dA": 0.1735, "proj1": 0.03, "tap": 0.08, "conv": 0.1384, "dconv": 0.04, "tanh": 0.25,
         "silu": 0.0906, "pair": 0.2451, "mask0": 0.1991, "mask1": 0.2845, "inv0": 0.36, "inv": 0.7952, "gate": 0.2875, "gate1": 0.35, "v": 0.9, "k": 0.99, "scan0": 0.0, "scan1": 0.7936, "post": 0.988}


def delta_heads(nc, ps, xT, sc, cst, a, scratch_o):
    with phase(nc) as ctx:
        sb = lambda n, s, d=F32: ctx.enter_context(nc.sbuf_tensor(f"d_{n}", s, d))
        two = lambda n, s: [sb(f"{n}{p}", s) for p in range(2)]
        SEM = {}

        def sem(name, count, start=0):
            SEM[name] = (nc.alloc_semaphore("d_" + name), count, start)

        ident, identb, neg_kq, upto, below = (cst[n] for n in ("ident", "identb", "neg_kq", "upto", "below"))
        half, low, first, eye = sb("half", [P, 16]), sb("low", [P, len(LEVELS), QB]), sb("first", [P, QB]), sb("eye", [P, QB])
        ln, ln2 = sb("ln", [P, 2]), sb("ln2", [P, 2])
        w = two("w", [P, KE, 4, DK])
        par, par2 = two("par", [P, 16]), two("par2_", [P, 16])
        ss = two("ss", [P, NS, TB])
        raw, acc, th = ([sb(f"{n}{i}", [P, T]) for i in range(3)] for n in ("raw", "acc", "th"))
        kq = two("kq", [P, TB, 2, P])
        vT = sb("vT", [P, T])
        gate = two("gate", [P, T])
        seg = two("seg", [P, P])
        dec = two("dec", [P, P + 1])
        ap = two("ap", [P, TB, 2, P])
        ktok, vtok = two("ktok", [P, TB, P]), two("vtok", [P, TB, P])
        tp, ttp, ym = (sb(n, [P, TB, QB]) for n in ("tp", "ttp", "ym"))
        tn = sb("tn", [64, TB, 64])
        y2 = sb("y2", [P, TB, 64])
        tt = two("tt", [P, TB, P])
        state, r_sb, w_sb = sb("state", [P, P]), sb("r_sb", [P, P]), sb("w_sb", [P, P])
        os_ = two("os", [P, P])
        o_sb, o_aff = sb("o_sb", [P, TB, P]), sb("o_aff", [P, T])
        o_g = two("o_g", [P, T])
        st6, mv, ve, rs = sb("st6", [P, TB, 6]), sb("mv", [P, TB, 2]), sb("ve", [P, TB]), sb("rs", [P, TB])

        c_in, c_made = nc.alloc_semaphore("d_c_in"), nc.alloc_semaphore("d_c_made")
        w_in = [nc.alloc_semaphore(f"d_w_in{p}") for p in range(2)]
        stored = [nc.alloc_semaphore(f"d_stored{p}") for p in range(2)]
        past = {eng: nc.alloc_semaphore(f"d_past{n}") for n, eng in enumerate((nc.tensor, nc.vector, nc.gpsimd))}
        for name, count, start in (
                ("proj", 6, 0), ("gproj", 2, 0), ("pair", 8, 0), ("k_turned", 2, 0), ("v_turned", 2, 0), ("y", 5, 0), ("z", 5, 0), ("y2", 1, 0),
                ("z2", 1, 0), ("ks", 7, 0), ("qs", 7, 0), ("w", 8, 0), ("pw", 8, 16), ("s", 7, 0), 
                ("o_turned", 2, 2),
                ("raw", 6, 0), ("graw", 2, 0), ("tanh", 3, 0), ("dec", 8, 0), ("v_tok", 2, 0), ("diag", 6, 0), ("off64", 3, 0), ("off128", 1, 0),
                ("qs_out", 7, 0), ("w_out", 8, 0), ("affine", 2, 0),
                ("conv", 9, 0), ("silu", 3, 0), ("ap", 8, 0), ("ap_a", 8, 0), ("k_tok", 2, 0), ("tp", 5, 0), ("ttp", 4, 0), ("ym", 5, 0),
                ("first", 8, 0), ("ttp0", 2, 0), ("y2_out", 1, 0), ("r", 7, 0), ("state", 7, 0), ("o", 8, 1), ("stats", 8, 0), ("mv", 1, 0), ("normed", 2, 0),
                ("gated", 2, 4),
                ("par", 1, 0), ("ss", 1, 0), ("tap", 3, 0), ("seg", 8, 0), 
                ("ve", 1, 0), ("rs", 1, 0)):
            sem(name, count, start)
        block = ctx.enter_context(nc.Block())
        PROJ, RING, INV, KS, QS, ST = 0, 2, 4, 5, 6, 7
        LOOPED = (HUNITS - 2) // 2
        NQ = P // QB

        def spread(steps, t0, t1):
            return [(t0 + (t1 - t0) * n / len(steps), s) for n, s in enumerate(steps)]

        early = [(TIMES["load"], ("load",))]
        for i in range(3):
            t0 = TIMES["A0"] + TIMES["dA"] * i
            early += [(t0, ("proj", i, 0)), (t0 + 0.001, ("raw", i, 0)), (t0 + TIMES["proj1"], ("proj", i, 1)), (t0 + TIMES["proj1"] + 0.001, ("raw", i, 1)),
                      (t0 + TIMES["tap"], ("tap", i))]
            early += [(t0 + TIMES["conv"] + TIMES["dconv"] * m, ("conv", i, m)) for m in range(3)]
            early += [(t0 + TIMES["tanh"], ("tanh", i))]
        inverse = [("first",)]
        for l in range(len(LEVELS)):
            inverse += [("y", l), ("z", l)]
        inverse += [("diag",), ("y64",), ("z64",), ("y128",), ("z128",)]
        late = spread([("scalars",), ("silu", 0), ("silu", 1), ("silu", 2)], 0.0, TIMES["silu"])
        late += spread([(k, c) for c in range(TB) for k in ("seg", "pair")], TIMES["silu"], TIMES["pair"])
        late += spread(inverse, TIMES["inv0"], TIMES["inv"])
        late += [(TIMES["mask0"], ("mask", 0)), (TIMES["mask1"], ("mask", 1))]
        late += spread([("gate", 0), ("gate", 1)], TIMES["gate"], TIMES["gate1"])
        late += [(TIMES["v"], ("v_turn", 0)), (TIMES["v"] + 0.01, ("v_turn", 1)), (TIMES["k"], ("k_turn", 0)), (TIMES["k"] + 0.001, ("k_turn", 1))]
        scan = spread([("scan", c, k) for c in range(TB) for k in range(3)], TIMES["scan0"], TIMES["scan1"])
        scan += spread([("stats",), ("norm", 0), ("norm", 1), ("o_turn", 0), ("o_turn", 1)], TIMES["scan1"], TIMES["post"])

        def stage(*parts):
            out = sorted((t, n, s) for n, steps in parts for t, s in steps)
            assert [s[0] for _, _, s in out if s[0] in ("pair", "gate", "v_turn", "k_turn", "o_turn")][-2:] == ["k_turn", "k_turn"]
            return [(n, s) for _, n, s in out]

        class Engine:

            def __init__(self, eng):
                self.eng, self.lp = eng, Loop()
                self.ring = []

            def wait(self, name, n, k):
                s, count, start = SEM[name]
                self.eng.wait_ge(s, self.lp.at(n * count + k + start, 2 * count))

            def passed(self):
                self.eng.sem_inc(past[self.eng], 1)

            def walk(self, do):
                def steps(lst, base):
                    for n, s in lst:
                        if s[0] in do:
                            do[s[0]](n, n + base, *s[1:])

                steps([(0, s) for _, s in sorted(early)], 0)
                steps(stage((0, late), (1, early)), 0)
                with self.eng.Fori(0, LOOPED) as i:
                    self.lp.i = i
                    steps(stage((0, scan), (1, late), (2, early)), i * 2)
                    steps(stage((1, scan), (2, late), (3, early)), i * 2)
                self.lp.i = LOOPED - 1
                steps(stage((2, scan), (3, late)), 2 * (LOOPED - 1))
                steps([(3, s) for _, s in scan], 2 * (LOOPED - 1))

        inc = lambda ins, name: ins.then_inc(SEM[name][0], 1)

        @block.sync
        def _(sp):
            E_ = Engine(sp)
            for dst, name in ((low, "c_low"), (first, "c_first"), (eye, "c_eye"), (ln, "ln")):
                sp.dma_start(dst[:], a[name]).then_inc(c_in, 16)
            sp.dma_start(half[:], a["c_half"].rearrange("o n -> (o n)").partition_broadcast(P)).then_inc(c_in, 16)

            def fetch(p, u):
                h = u % H
                sp.dma_start(w[p][:].rearrange("p k i d -> p (k i d)"),
                             a["dw"][bass.ds(h, 1)].rearrange("o p k i d -> (o p) (k i d)")).then_inc(w_in[p], 16)
                sp.dma_start(par[p][:], a["dpar"][bass.ds(h, 1)].rearrange("o p n -> (o p) n")).then_inc(w_in[p], 16)

            def ahead(n, u):
                E_.wait("silu", n, 3)
                E_.wait("gproj", n, 2)
                fetch(n % 2, u + 2)

            def store(n, u):
                E_.wait("gated", n, 2)
                sp.dma_start(scratch_o[bass.ds(u, 1)].rearrange("o p t -> (o p) t"), o_g[n % 2][:]).then_inc(stored[n % 2], 16)

            fetch(0, 0)
            fetch(1, 1)
            ahead(0, 0)
            with sp.Fori(0, LOOPED - 1) as i:
                E_.lp.i = i
                for n in range(2):
                    ahead(n + 1, i * 2 + n + 1)
                    store(n, i * 2 + n)
            E_.lp.i = LOOPED - 1
            ahead(1, HUNITS - 3)
            for n in range(4):
                store(n, HUNITS - 4 + n)
            for p in range(2):
                sp.wait_ge(stored[p], 16 * (HUNITS // 2 + 1))

        @block.gpsimd
        def _(pool):
            E_ = Engine(pool)
            W = E_.wait

            def load(n, u):
                p = n % 2
                pool.wait_ge(w_in[p], E_.lp.at(32 * (n // 2 + 1), 32))
                if n >= 2:
                    W("conv", n - 2, 9)
                inc(nc.gpsimd.tensor_tensor(par2[p][:], par[p][:], half[:], ALU.mult), "par")

            def scalars(n, u):
                p = n % 2
                W("pw", n - 2, TB)
                inc(nc.gpsimd.tensor_copy(ss[p][:], sc[:, bass.ds(u, 1)].rearrange("p o k c -> p (o k) c")), "ss")

            def tap(n, u, i):
                W("par", n, 1)
                W("raw", n, 2 * i + 2)
                if n >= 1:
                    W("silu", n - 1, i + 1)
                E_.passed()
                inc(nc.gpsimd.tensor_scalar(acc[i][:], raw[i][:], par2[n % 2][:, 4 * i + 3:4 * i + 4],
                                            par2[n % 2][:, 12 + i:13 + i], ALU.mult, ALU.add), "tap")

            def segs(n, u, c):
                if c == 0:
                    W("ss", n, 1)
                if c >= 2:
                    W("pair", n, c - 1)
                elif n >= 1:
                    W("pair", n - 1, TB + c - 1)
                E_.passed()
                inc(nc.gpsimd.tensor_scalar(seg[c % 2][:], below[:], ss[n % 2][:, S_LA, c:c + 1], None, ALU.mult), "seg")

            def stats(n, u):
                W("mv", n, 1)
                E_.passed()
                inc(nc.gpsimd.tensor_scalar(ve[:], mv[:, :, 1], EPS, None, ALU.add), "ve")
                W("ve", n, 1)
                inc(nc.gpsimd.tensor_tensor(rs[:], ve[:], cst["pow_half"][:, 0:TB], ALU.pow), "rs")
                W("rs", n, 1)

            for p in range(2):
                nc.gpsimd.memset(dec[p][:, 0:1], 0.0).then_inc(c_made, 1)
                nc.gpsimd.memset(tt[p][:], 0.0).then_inc(c_made, 1)
            nc.gpsimd.memset(tn[:], 0.0).then_inc(c_made, 1)
            pool.wait_ge(c_in, 80)
            nc.gpsimd.tensor_scalar(ln2[:], ln[:], 0.5, None, ALU.mult).then_inc(c_made, 1)
            pool.wait_ge(c_made, 6)
            E_.walk({"load": load, "scalars": scalars, "tap": tap, "seg": segs, "stats": stats})

        @block.tensor
        def _(pe):
            E_ = Engine(pe)
            W = E_.wait
            pe.sem_inc(SEM["pw"][0], 2 * TB)
            pe.sem_inc(SEM["o_turned"][0], 2)

            def ring(reader):
                n = len(E_.ring)
                if n >= 2:
                    W(*E_.ring[n - 2])
                E_.ring.append(reader)
                return RING + n % 2

            def proj(n, u, i, h):
                p = n % 2
                if i == 0 and h == 0:
                    pe.wait_ge(w_in[p], E_.lp.at(32 * (n // 2 + 1), 32))
                if i >= 1:
                    W("raw", n, 2 * i + h - 1)
                elif n >= 1:
                    W("raw", n - 1, 5 + h)
                for k in range(KE):
                    last = nc.tensor.matmul(ps[:, PROJ + h, :], w[p][:, k, i, :], xT[:, k, bass.ds((u // H) * T + h * HALF, HALF)],
                                            start=(k == 0), stop=(k == KE - 1))
                inc(last, "proj")

            def gate_(n, u, h):
                bank = ring(("graw", n, h + 1))
                for k in range(KE):
                    last = nc.tensor.matmul(ps[:, bank, :], w[n % 2][:, k, 3, :], xT[:, k, bass.ds((u // H) * T + h * HALF, HALF)],
                                            start=(k == 0), stop=(k == KE - 1))
                inc(last, "gproj")

            def pair(n, u, c):
                bank = ring(("ap", n, c + 1))
                if c == 0:
                    W("silu", n, 2)
                kqc = kq[n % 2][:, c]
                nc.tensor.matmul(ps[:, bank, 0:2 * P], kqc[:, 0, :], kqc.rearrange("p i t -> p (i t)"), start=True, stop=True)
                W("seg", n, c + 1)
                nc.tensor.matmul(ps[:, bank, 2 * P:3 * P], seg[c % 2][:], upto[:], start=True, stop=False)
                inc(nc.tensor.matmul(ps[:, bank, 2 * P:3 * P], identb[:], neg_kq[:], start=False, stop=True), "pair")

            def k_turn(n, u, j):
                bank = ring(("k_tok", n, j + 1))
                for c in range(4):
                    last = nc.tensor.transpose(ps[:, bank, c * P:(c + 1) * P], kq[n % 2][:, 4 * j + c, 0, :], ident[:])
                inc(last, "k_turned")

            def v_turn(n, u, j):
                bank = ring(("v_tok", n, j + 1))
                W("silu", n, 3)
                for c in range(4):
                    last = nc.tensor.transpose(ps[:, bank, c * P:(c + 1) * P], vT[:, (4 * j + c) * P:(4 * j + c + 1) * P], ident[:])
                inc(last, "v_turned")

            def packed(n, lhs, rhs):
                for c in range(TB):
                    for q in range(NQ):
                        r = slice(q * QB, (q + 1) * QB)
                        last = nc.tensor.matmul(ps[r, INV, c * QB:(c + 1) * QB], lhs(c, r), rhs[r, c, :], start=True, stop=True)
                return last

            def y(n, u, l):
                if l == 0:
                    W("ap", n, TB)
                    if n >= 1:
                        W("off128", n - 1, 1)
                W("tp", n, l + 1)
                E_.passed()
                inc(packed(n, lambda c, r: ap[n % 2][r, c, 0, r], tp), "y")

            def z(n, u, l):
                W("ym", n, l + 1)
                E_.passed()
                inc(packed(n, lambda c, r: ttp[r, c, :], ym), "z")

            def y64(n, u):
                W("ttp", n, len(LEVELS))
                E_.passed()
                for c in range(TB):
                    for s in (0, 64):
                        last = nc.tensor.matmul(ps[s + QB:s + 64, INV, c * QB:(c + 1) * QB], ap[n % 2][s:s + QB, c, 0, s + QB:s + 64],
                                                tp[s:s + QB, c, :], start=True, stop=True)
                inc(last, "y")

            def z64(n, u):
                W("ym", n, len(LEVELS) + 1)
                E_.passed()
                for c in range(TB):
                    for s in (0, 64):
                        last = nc.tensor.matmul(ps[s:s + QB, INV, c * QB:(c + 1) * QB], ym[s + QB:s + 64, c, :], ttp[s + QB:s + 64, c, :],
                                                start=True, stop=True)
                    last = nc.tensor.matmul(ps[QB:64, INV, c * QB:(c + 1) * QB], ttp[QB:64, c, :], ym[QB:64, c, :], start=True, stop=True)
                inc(last, "z")

            def y128(n, u):
                W("off64", n, 3)
                W("diag", n, 6)
                E_.passed()
                for c in range(TB):
                    last = nc.tensor.matmul(ps[64:P, INV, c * 64:(c + 1) * 64], ap[n % 2][0:64, c, 0, 64:P], tn[:, c, :], start=True, stop=True)
                inc(last, "y2")

            def z128(n, u):
                W("y2_out", n, 1)
                E_.passed()
                for c in range(TB):
                    last = nc.tensor.matmul(ps[0:64, INV, c * 64:(c + 1) * 64], y2[64:P, c, :], tt[n % 2][64:P, c, 64:P], start=True, stop=True)
                inc(last, "z2")

            def scan_(n, u, c, part):
                p = n % 2
                if part == 0:
                    if c == 0:
                        return
                    W("state", n, c)
                    inc(nc.tensor.matmul(ps[:, KS, 0:P], kq[p][:, c, 0, :], state[:], start=True, stop=True), "ks")
                    W("o", n, c)
                    inc(nc.tensor.matmul(ps[:, QS, 0:P], kq[p][:, c, 1, :], state[:], start=True, stop=True), "qs")
                elif part == 1:
                    if c == 0:
                        W("v_tok", n, 2)
                        W("off128", n, 1)
                        W("diag", n, 6)
                        rhs = vtok[p][:, 0, :]
                    else:
                        W("r", n, c)
                        rhs = r_sb[:]
                    inc(nc.tensor.matmul(ps[:, KS, 0:P], tt[p][:, c, :], rhs, start=True, stop=True), "w")
                else:
                    W("w_out", n, c + 1)
                    if c == 0:
                        W("o", n, 0)
                        W("k_tok", n, 2)
                    if c < TB - 1:
                        inc(nc.tensor.matmul(ps[:, ST, 0:P], ktok[p][:, c, :], w_sb[:], start=True, stop=True), "s")
                    inc(nc.tensor.matmul(ps[:, QS, 0:P], ap[p][:, c, 1, :], w_sb[:], start=True, stop=True), "pw")

            def o_turn(n, u, j):
                bank = ring(("affine", n, j + 1))
                W("normed", n, j + 1)
                for c in range(4):
                    last = nc.tensor.transpose(ps[:, bank, c * P:(c + 1) * P], o_sb[:, 4 * j + c, :], ident[:])
                inc(last, "o_turned")

            pe.wait_ge(c_made, 6)
            E_.walk({"proj": proj, "gate": gate_, "pair": pair, "k_turn": k_turn, "v_turn": v_turn, "y": y, "z": z, "y64": y64, "z64": z64,
                     "y128": y128, "z128": z128, "scan": scan_, "o_turn": o_turn})

        @block.scalar
        def _(act):
            E_ = Engine(act)
            W = E_.wait

            def raw_(n, u, i, h):
                W("proj", n, 2 * i + h + 1)
                c = slice(h * HALF, (h + 1) * HALF)
                if n >= 1:
                    W("conv", n - 1, 3 * i + 3)
                inc(nc.scalar.activation(raw[i][:, c], ps[:, PROJ + h, :], ACT.Copy), "raw")

            def gate_(n, u, h):
                bank = RING + len(E_.ring) % 2
                E_.ring.append(0)
                W("gproj", n, h + 1)
                W("gated", n - 2, 2)
                inc(nc.scalar.activation(gate[n % 2][:, h * HALF:(h + 1) * HALF], ps[:, bank, :], ACT.Tanh, scale=0.5), "graw")

            def tanh(n, u, i):
                W("conv", n, 3 * i + 3)
                if n >= 1:
                    W("silu", n - 1, i + 1)
                inc(nc.scalar.activation(th[i][:], acc[i][:], ACT.Tanh, scale=(float(DK) ** 0.5 if i == 0 else 1.0)), "tanh")

            def pair(n, u, c):
                W("pair", n, c + 1)
                inc(nc.scalar.activation(dec[c % 2][:, 1:P + 1], ps[:, RING + len(E_.ring) % 2, 2 * P:3 * P], ACT.Exp), "dec")
                E_.ring.append(0)

            def k_turn(n, u, j):
                E_.ring.append(0)

            def v_turn(n, u, j):
                bank = RING + len(E_.ring) % 2
                E_.ring.append(0)
                W("v_turned", n, j + 1)
                W("pw", n - 2, TB)
                inc(nc.scalar.activation(vtok[n % 2][:, 4 * j:4 * j + 4, :].rearrange("p c d -> p (c d)"), ps[:, bank, :], ACT.Copy), "v_tok")

            def diag(n, u):
                W("ttp", n, len(LEVELS))
                W("pw", n - 2, TB)
                if n >= 1:
                    W("y2", n - 1, 1)
                for q in range(2):
                    r = slice(q * QB, (q + 1) * QB)
                    inc(nc.scalar.activation(tn[r, :, r], tp[r], ACT.Copy), "diag")
                for q in range(NQ):
                    r = slice(q * QB, (q + 1) * QB)
                    inc(nc.scalar.activation(tt[n % 2][r, :, r], ttp[r], ACT.Copy), "diag")

            def z64(n, u):
                W("z", n, len(LEVELS) + 1)
                v = ps[:, INV, 0:TB * QB].rearrange("p (c t) -> p c t", t=QB)
                inc(nc.scalar.activation(tn[QB:64, :, 0:QB], v[QB:64], ACT.Copy, scale=-1.0), "off64")
                for s in (0, 64):
                    inc(nc.scalar.activation(tt[n % 2][s:s + QB, :, s + QB:s + 64], v[s:s + QB], ACT.Copy, scale=-1.0), "off64")

            def z128(n, u):
                W("z2", n, 1)
                inc(nc.scalar.activation(tt[n % 2][0:64, :, 64:P], ps[0:64, INV, :].rearrange("p (c t) -> p c t", t=64), ACT.Copy, scale=-1.0), "off128")

            def scan_(n, u, c, part):
                if part == 0 and c > 0:
                    W("qs", n, c)
                    inc(nc.scalar.activation(os_[c % 2][:], ps[:, QS, 0:P], ACT.Copy, scale=ss[n % 2][:, S_G, c:c + 1]), "qs_out")
                elif part == 1:
                    W("w", n, c + 1)
                    inc(nc.scalar.activation(w_sb[:], ps[:, KS, 0:P], ACT.Copy), "w_out")

            def o_turn(n, u, j):
                bank = RING + len(E_.ring) % 2
                E_.ring.append(0)
                W("o_turned", n, j + 1)
                W("gated", n - 1, j + 1)
                inc(nc.scalar.activation(o_aff[:, j * HALF:(j + 1) * HALF], ps[:, bank, :], ACT.Identity, bias=ln2[:, 1:2],
                                         scale=ln2[:, 0:1]), "affine")

            act.wait_ge(c_made, 6)
            E_.walk({"raw": raw_, "gate": gate_, "tanh": tanh, "pair": pair, "k_turn": k_turn, "v_turn": v_turn, "diag": diag, "z64": z64, "z128": z128,
                     "scan": scan_, "o_turn": o_turn})

        @block.vector
        def _(dve):
            E_ = Engine(dve)
            W = E_.wait
            dve.sem_inc(SEM["o"][0], 1)
            dve.sem_inc(SEM["gated"][0], 4)
            for p in range(2):
                dve.sem_inc(stored[p], 16)

            def conv(n, u, i, m):
                d, j = m + 1, 2 - m
                if m == 0:
                    W("tap", n, i + 1)
                else:
                    W("conv", n, 3 * i + m)
                inc(nc.vector.scalar_tensor_tensor(acc[i][:, d:T], raw[i][:, 0:T - d], par2[n % 2][:, 4 * i + j:4 * i + j + 1],
                                                   acc[i][:, d:T], ALU.mult, ALU.add), "conv")

            def gate_(n, u, h):
                E_.ring.append(0)

            def silu(n, u, i):
                W("tanh", n, i + 1)
                if i == 0:
                    W("pw", n - 2, TB)
                if i == 2:
                    if n >= 1:
                        W("v_turned", n - 1, 2)
                    dst, t_, a_ = vT[:], th[i][:], acc[i][:]
                else:
                    dst = kq[n % 2][:, :, i, :]
                    t_, a_ = (v[i][:].rearrange("p (c t) -> p c t", t=P) for v in (th, acc))
                inc(nc.vector.scalar_tensor_tensor(dst, t_, 1.0, a_, ALU.add, ALU.mult), "silu")

            def pair(n, u, c):
                bank = RING + len(E_.ring) % 2
                E_.ring.append(0)
                W("dec", n, c + 1)
                beta = ss[n % 2][:, S_BETA, c:c + 1]
                inc(nc.vector.scalar_tensor_tensor(ap[n % 2][:, c, 0, :], ps[:, bank, 0:P], beta, dec[c % 2][:, 0:P], ALU.mult, ALU.mult), "ap_a")
                inc(nc.vector.scalar_tensor_tensor(ap[n % 2][:, c, 1, :], ps[:, bank, P:2 * P], beta, dec[c % 2][:, 1:P + 1], ALU.mult, ALU.mult), "ap")

            def k_turn(n, u, j):
                bank = RING + len(E_.ring) % 2
                E_.ring.append(0)
                W("k_turned", n, j + 1)
                inc(nc.vector.tensor_tensor(ktok[n % 2][:, 4 * j:4 * j + 4, :], ps[:, bank, :].rearrange("p (c d) -> p c d", d=P),
                                            ss[n % 2][:, S_BGC, 4 * j:4 * j + 4].unsqueeze(2).to_broadcast([P, 4, P]), ALU.mult), "k_tok")

            def v_turn(n, u, j):
                E_.ring.append(0)

            def mask(n, u, h):
                cs = slice(h * TB // 2, (h + 1) * TB // 2)
                W("ap_a", n, (h + 1) * TB // 2)
                if n >= 1:
                    W("off128", n - 1, 1)
                for q in range(NQ):
                    r = slice(q * QB, (q + 1) * QB)
                    inc(nc.vector.tensor_tensor(ttp[r, cs], ap[n % 2][r, cs, 0, r], first[r].unsqueeze(1).to_broadcast([QB, TB // 2, QB]),
                                                ALU.mult), "first")
                W("first", n, (h + 1) * NQ)
                inc(nc.vector.tensor_tensor(ttp[:, cs], ttp[:, cs], eye[:].unsqueeze(1).to_broadcast([P, TB // 2, QB]), ALU.add), "ttp0")

            def first_(n, u):
                W("ttp0", n, 2)
                inc(nc.vector.transpose(tp[:].rearrange("p c t -> p (c t)"), ttp[:].rearrange("p c t -> p (c t)")), "tp")

            v = ps[:, INV, 0:TB * QB].rearrange("p (c t) -> p c t", t=QB)

            def y(n, u, l):
                W("y", n, l + 1)
                inc(nc.vector.tensor_tensor(ym[:], v, low[:, l].unsqueeze(1).to_broadcast([P, TB, QB]), ALU.mult), "ym")

            def z(n, u, l):
                W("z", n, l + 1)
                inc(nc.vector.tensor_tensor(tp[:], tp[:], v, ALU.subtract), "tp")
                W("tp", n, l + 2)
                inc(nc.vector.transpose(ttp[:].rearrange("p c t -> p (c t)"), tp[:].rearrange("p c t -> p (c t)")), "ttp")

            def y64(n, u):
                W("y", n, len(LEVELS) + 1)
                inc(nc.vector.tensor_copy(ym[:], v), "ym")

            def y128(n, u):
                W("y2", n, 1)
                inc(nc.vector.tensor_copy(y2[64:P], ps[64:P, INV, :].rearrange("p (c t) -> p c t", t=64)), "y2_out")

            def scan_(n, u, c, part):
                p = n % 2
                if part == 0 and c > 0:
                    W("ks", n, c)
                    inc(nc.vector.scalar_tensor_tensor(r_sb[:], ps[:, KS, 0:P], ss[p][:, S_NGEX, c:c + 1], vtok[p][:, c, :],
                                                       ALU.mult, ALU.add), "r")
                elif part == 2:
                    if c < TB - 1:
                        W("s", n, c + 1)
                        if c == 0:
                            ins = nc.vector.tensor_copy(state[:], ps[:, ST, 0:P])
                        else:
                            ins = nc.vector.scalar_tensor_tensor(state[:], state[:], ss[p][:, S_GC, c:c + 1], ps[:, ST, 0:P], ALU.mult, ALU.add)
                        inc(ins, "state")
                    W("pw", n, c + 1)
                    if c == 0:
                        W("o_turned", n - 1, 2)
                        ins = nc.vector.tensor_copy(o_sb[:, 0, :], ps[:, QS, 0:P])
                    else:
                        W("qs_out", n, c)
                        ins = nc.vector.tensor_tensor(o_sb[:, c, :], ps[:, QS, 0:P], os_[c % 2][:], ALU.add)
                    inc(ins, "o")
                    W("o", n, c + 1)
                    inc(nc.vector.bn_stats(st6[:, c, :], o_sb[:, c, :]), "stats")

            def stats(n, u):
                W("stats", n, TB)
                E_.passed()
                for c in range(TB):
                    ins = nc.vector.bn_aggr(mv[:, c, :], st6[:, c, :])
                inc(ins, "mv")

            def norm(n, u, j):
                W("rs", n, 1)
                for c in range(4 * j, 4 * j + 4):
                    ins = nc.vector.tensor_scalar(o_sb[:, c, :], o_sb[:, c, :], mv[:, c, 0:1], rs[:, c:c + 1], ALU.subtract, ALU.mult)
                inc(ins, "normed")

            def o_turn(n, u, j):
                E_.ring.append(0)
                W("affine", n, j + 1)
                c = slice(j * HALF, (j + 1) * HALF)
                dve.wait_ge(stored[n % 2], E_.lp.at(16 * (n // 2 + 1), 16))
                inc(nc.vector.scalar_tensor_tensor(o_g[n % 2][:, c], gate[n % 2][:, c], 1.0, o_aff[:, c], ALU.add, ALU.mult), "gated")

            dve.wait_ge(c_made, 6)
            dve.wait_ge(c_in, 80)
            E_.walk({"conv": conv, "gate": gate_, "silu": silu, "pair": pair, "k_turn": k_turn, "v_turn": v_turn, "mask": mask, "first": first_, "y": y, "z": z,
                     "y64": y64, "y128": y128, "scan": scan_, "stats": stats, "norm": norm, "o_turn": o_turn})


def delta_output(nc, ps, x_tok, cst, a, scratch_o):
    with phase(nc) as ctx:
        sb = lambda n, s, d=F32: ctx.enter_context(nc.sbuf_tensor(f"w_{n}", s, d))
        sem = lambda n: nc.alloc_semaphore(f"w_{n}")
        o = sb("o", [P, 2, H, HALF])
        wo = sb("wo", [P, H, E])
        w_in, o_in = sem("w_in"), [sem("o_in0"), sem("o_in1")]
        projected, freed = sem("projected"), sem("freed")
        norm = Norm(nc, ctx, "w", x_tok, cst)
        block = ctx.enter_context(nc.Block())

        @block.sync
        def _(sp):
            sp.dma_start(wo[:], a["wo1"].rearrange("(h p) n -> p h n", p=P)).then_inc(w_in, 16)
            for n in range(BLK):
                b, t0 = n // (BLK // B), n % (BLK // B) * HALF
                if n >= 2:
                    sp.wait_ge(projected, n - 1)
                sp.dma_start(o[:, n % 2], scratch_o[b * H:(b + 1) * H, :, t0:t0 + HALF].rearrange("h p t -> p h t")).then_inc(o_in[n % 2], 16)

        @block.tensor
        def _(pe):
            pe.wait_ge(w_in, 16)
            for n in range(BLK):
                pe.wait_ge(o_in[n % 2], 16 * (n // 2 + 1))
                if n >= 2:
                    pe.wait_ge(freed, n - 1)
                for t in range(BT):
                    for h in range(H):
                        last = nc.tensor.matmul(ps[:, 2 * (n % 2) + t // 2, (t % 2) * E:(t % 2 + 1) * E], o[:, n % 2, h, t * P:(t + 1) * P],
                                                wo[:, h, :], start=(h == 0), stop=(h == H - 1))
                last.then_inc(projected, 1)

        @block.gpsimd
        def _(pool):
            for n in range(BLK):
                norm.inverse_root(pool, n)

        @block.vector
        def _(dve):
            for n in range(BLK):
                dve.wait_ge(projected, n + 1)
                norm.residual(dve, n, pair_view(ps, 2 * (n % 2)), None, freed)
                if n >= 1:
                    norm.normalise(dve, n - 1)
            norm.normalise(dve, BLK - 1)


def delta_layer(nc, ps, x_tok, cst, a):
    scratch_o = nc.dram_tensor("scratch_o", [HUNITS, P, T], F32).ap()
    with ExitStack() as ctx:
        sb = lambda n, s: ctx.enter_context(nc.sbuf_tensor(n, s, F32))
        xT, sc = sb("x1T", [P, KE, TOK]), sb("sc", [P, HUNITS, NS, TB])
        delta_scalars(nc, ps, x_tok, xT, sc, cst, a)
        delta_heads(nc, ps, xT, sc, cst, a, scratch_o)
    delta_output(nc, ps, x_tok, cst, a, scratch_o)


def constants():
    rows, cols = np.arange(P)[:, None], np.arange(P)[None, :]
    pos = np.arange(1, T + 1, dtype=np.float32)[None, :]
    freqs = (np.float32(10000.0) ** (-(np.float32(2.0) * np.arange(D // 2, dtype=np.float32)) / np.float32(D))).astype(np.float32)
    theta = (pos * freqs[np.arange(P) % (D // 2)][:, None]).astype(np.float32)
    sign = np.where(np.arange(P) % D < D // 2, -1.0, 1.0).astype(np.float32)[:, None]
    return {
        "c_ident": (rows == cols).astype(np.float32),
        "c_above": (cols > rows).astype(np.float32),
        "c_upto": (cols >= rows).astype(np.float32),
        "c_cos": np.cos(theta).astype(np.float32),
        "c_sin": (sign * np.sin(theta)).astype(np.float32),
    }


def build(nc, a, out):
    ctx = ExitStack()
    with ctx:
        sb = lambda n, s, d=F32: ctx.enter_context(nc.sbuf_tensor(n, s, d))
        ps = ctx.enter_context(nc.psum_tensor("ps", [P, 8, HALF], F32))
        x_tok = sb("x_tok", [P, NT, E])
        cst = {"ident": sb("ident", [P, P]), "identb": sb("identb", [P, P], BF16), "neg_qk": sb("neg_qk", [P, P], BF16),
               "neg_kq": sb("neg_kq", [P, P], BF16), "pow_half": sb("pow_half", [P, 8]), "above": sb("above", [P, P]),
               "upto": sb("upto", [P, P]), "below": sb("below", [P, P])}
        scratch = {"x": a["x"].rearrange("(n p) c -> n p c", p=P),
                   "q": nc.dram_tensor("scratch_q", [3, HQ * D, TOK], BF16).ap(),
                   "k": nc.dram_tensor("scratch_k", [3, HKV * D, TOK], BF16).ap()}
        o = out.rearrange("(n p) c -> n p c", p=P)
        cst["in"], cst["in_n"] = ctx.enter_context(nc.semaphore("c_in")), 64
        made = ctx.enter_context(nc.semaphore("c_made"))
        with nc.Block() as block:
            @block.sync
            def _(sp):
                for n, name in enumerate(("ident", "above", "upto", "below")):
                    sp.dma_start(cst[name][:], a["c_" + name]).then_inc(cst["in"], 16)

            @block.gpsimd
            def _(pool):
                nc.gpsimd.memset(cst["pow_half"][:], -0.5).then_inc(made, 1)

            @block.vector
            def _(dve):
                dve.wait_ge(cst["in"], cst["in_n"])
                nc.vector.tensor_copy(cst["identb"][:], cst["ident"][:]).then_inc(made, 1)
                nc.vector.tensor_scalar(cst["neg_qk"][:], cst["above"][:], BIG, None, ALU.mult).then_inc(made, 1)
                nc.vector.tensor_scalar(cst["neg_kq"][:], cst["upto"][:], -BIG, BIG, ALU.mult, ALU.add).then_inc(made, 1)

        with ExitStack() as layer:
            cst["v_aug"] = layer.enter_context(nc.sbuf_tensor("v_aug", [P, NT, HKV, VW], F32))
            for name, shape in (("q1", [P, G, T]), ("k1", [P, T]), ("q2", [P, G, T]), ("k2", [P, T])):
                cst[name] = [layer.enter_context(nc.sbuf_tensor(f"{name}_{p}", shape, BF16)) for p in range(2)]
            load_and_project(nc, ps, x_tok, cst, scratch,
                             {"wq": a["wq2"], "wk": a["wk2"], "wv": a["wv"], "bq": a["bq2"], "bk": a["bk2"], "bv": a["bv"],
                              "cos": a["c_cos"], "sin": a["c_sin"]})
            y_tok = layer.enter_context(nc.sbuf_tensor("y_tok", [P, NT, E], F32))
            attention(nc, ps, y_tok, cst, scratch)
            output_projection(nc, ps, x_tok, y_tok, cst, {"wo": a["wo"], "bo": a["bo"]})
        feed_forward(nc, ps, x_tok, cst, {"up": a["f0_up"], "down": a["f0_down"], "up_scale": a["f0_us"], "down_scale": a["f0_ds"]}, True)
        delta_layer(nc, ps, x_tok, cst, a)
        feed_forward(nc, ps, x_tok, cst, {"up": a["f1_up"], "down": a["f1_down"], "up_scale": a["f1_us"],
                                          "down_scale": a["f1_ds"], "out_scale": a["f1_os"]}, False, out=o)


def laid_out(inp):
    g = {n: np.asarray(v) for n, v in inp.items()}
    swap = lambda n: np.arange(n) ^ (D // 2)
    wq, bq, wk, bk = (g["L0_attn_" + n] for n in ("Wq", "bq", "Wk", "bk"))
    a = {
        "x": g["L0_attn_x"].reshape(TOK, E),
        "wq2": np.stack([wq, wq[:, swap(HQ * D)]], 1), "bq2": np.stack([bq, bq[swap(HQ * D)]]).reshape(2, KE, P).transpose(2, 0, 1),
        "wk2": np.stack([wk, wk[:, swap(HKV * D)]], 1), "bk2": np.stack([bk, bk[swap(HKV * D)]]).T,
        "wv": g["L0_attn_Wv"], "bv": g["L0_attn_bv"], "wo": g["L0_attn_Wo"], "bo": g["L0_attn_bo"],
        "f0_up": np.stack([g["L0_ffn_w_gate"], g["L0_ffn_w_up"]]).view(np.int32), "f0_down": np.ascontiguousarray(g["L0_ffn_w_down"]).view(np.int32),
        "f0_us": np.stack([g["L0_ffn_s_gate"], g["L0_ffn_s_up"]]).reshape(2, -1, P).transpose(2, 0, 1), "f0_ds": g["L0_ffn_s_down"],
        "f1_up": g["L1_ffn_up_weight"].T[None], "f1_down": g["L1_ffn_down_weight"].T, "f1_us": g["L1_ffn_up_scale"].reshape(1, -1, P).transpose(2, 0, 1),
        "f1_ds": g["L1_ffn_down_scale"], "f1_os": g["L1_ffn_output_scale"],
    }
    a.update(delta_inputs(g))
    a.update(constants())
    return {n: np.ascontiguousarray(v) for n, v in a.items()}


def kernel(**inputs):
    import concourse.bacc as bacc
    from concourse.bass_utils import run_bass_kernel_spmd

    nc = bacc.Bacc("TRN2", target_bir_lowering=False, num_devices=1)
    arrays = {f"in_{n}": v for n, v in laid_out(inputs).items()}
    aps = {n[3:]: nc.dram_tensor(n, v.shape, mybir.dt.from_np(v.dtype), kind="ExternalInput").ap() for n, v in arrays.items()}
    out = nc.dram_tensor("out", (TOK, E), F32, kind="ExternalOutput").ap()
    build(nc, aps, out)
    r = run_bass_kernel_spmd(nc, [arrays], core_ids=[0])
    return r.results[0]["out"].reshape(B, T, E)
```

```python
from contextlib import ExitStack, contextmanager

import numpy as np
import concourse.bass as bass
from concourse import mybir

F32 = mybir.dt.float32
BF16 = mybir.dt.bfloat16
ALU = mybir.AluOpType
ACT = mybir.ActivationFunctionType
AX = mybir.AxisListType

B, T, E = 2, 1024, 256
P = 128
NT = B * T // P
TB = T // P
KE = E // P
TOK = B * T
HQ, HKV, D = 32, 8, 8
G = HQ // HKV
BIG = -1.0e30
HALF = 512
EPS = 1e-5


@contextmanager
def phase(nc):
    before = nc.snapshot_sems()
    with ExitStack() as ctx:
        yield ctx
    nc.clear_and_free_semaphores(nc.allocated_since(before))
    nc.all_engine_barrier()


class Loop:

    def __init__(self):
        self.i = 0

    def at(self, n, per):
        return n + self.i * per


def load_and_project(nc, ps, x_tok, cst, dram, w, later):
    with phase(nc) as ctx:
        sb = lambda n, s, d=F32: ctx.enter_context(nc.sbuf_tensor(n, s, d))
        sem = lambda n: nc.alloc_semaphore(n)
        xT = sb("p_xT", [P, KE, TOK])
        wq = sb("p_wq", [P, KE, 2, E])
        wk = sb("p_wk", [P, KE, 2, HKV * D])
        wv = sb("p_wv", [P, KE, HKV * D])
        bq = sb("p_bq", [P, 2, KE])
        bk = sb("p_bk", [HKV * D, 2])
        bv = sb("p_bv", [P, HKV * D])
        cos = sb("p_cos", [P, T])
        sin = sb("p_sin", [P, T])
        t1 = sb("p_t1", [P, 2, HALF])
        t2 = sb("p_t2", [P, 2, HALF])
        rot = sb("p_rot", [P, 2, HALF])
        rest = sb("p_rest", [P, 2, HALF])
        rest2 = sb("p_rest2", [P, 2, HALF])
        parts = sb("p_parts", [P, 2, 3, HALF], BF16)
        ident, v_aug = cst["ident"], cst["v_aug"]

        x_in, w_in = sem("p_x_in"), sem("p_w_in")
        transposed = sem("p_transposed")
        xT_done_act, xT_done_dve = sem("p_xT_act"), sem("p_xT_dve")
        projected = sem("p_projected")
        rotated, summed = sem("p_rotated"), sem("p_summed")
        high, high_left, mid = sem("p_high"), sem("p_high_left"), sem("p_mid")
        low, stored = sem("p_low"), [sem("p_stored0"), sem("p_stored1")]
        v_ready, v_added, v_clear = sem("p_v_ready"), sem("p_v_added"), sem("p_v_clear")

        NG = NT // 4 * KE
        NB = TOK // HALF
        kinds = [("q", 0), ("q", 1), ("k", 0)]
        jobs = [(kind, c, n) for kind, c in kinds for n in range(NB)]
        rows = {"q": P, "k": HKV * D}
        block = ctx.enter_context(nc.Block())

        @block.sync
        def _(sp):
            sp.dma_start(x_tok[:, 0:NT // 2, :], dram["x"][0:NT // 2].rearrange("n p c -> p n c")).then_inc(x_in, 16)
            sp.dma_start(x_tok[:, NT // 2:, :], dram["x"][NT // 2:].rearrange("n p c -> p n c")).then_inc(x_in, 16)
            sp.dma_start(wq[:], w["wq"].rearrange("(k p) s n -> p k s n", p=P)).then_inc(w_in, 16)
            sp.dma_start(wk[:], w["wk"].rearrange("(k p) s n -> p k s n", p=P)).then_inc(w_in, 16)
            sp.dma_start(wv[:], w["wv"].rearrange("(k p) n -> p k n", p=P)).then_inc(w_in, 16)
            sp.dma_start(bq[:], w["bq"]).then_inc(w_in, 16)
            sp.dma_start(bk[:], w["bk"]).then_inc(w_in, 16)
            sp.dma_start(bv[:], w["bv"].partition_broadcast(P)).then_inc(w_in, 16)
            sp.dma_start(cos[:], w["cos"]).then_inc(w_in, 16)
            sp.dma_start(sin[:], w["sin"]).then_inc(w_in, 16)
            later.fetch(sp)
            for m, (kind, c, n) in enumerate(jobs):
                r = rows[kind]
                sp.wait_ge(low, m + 1)
                sp.dma_start(dram[kind][:, c * P:c * P + r, n * HALF:(n + 1) * HALF].rearrange("s p t -> p s t"),
                             parts[0:r, m % 2]).then_inc(stored[m % 2], 16)
            for s in range(2):
                sp.wait_ge(stored[s], 16 * (len(jobs) // 2))

        @block.tensor
        def _(pe):
            pe.wait_ge(cst["in"], cst["in_n"])
            for g in range(NG):
                k, t4 = g % KE, g // KE
                if g == 0:
                    pe.wait_ge(x_in, 32)
                if g >= 2:
                    pe.wait_ge(xT_done_act if g % 2 == 0 else xT_done_dve, g // 2)
                for a in range(4):
                    last = nc.tensor.transpose(ps[:, g % 2, a * P:(a + 1) * P],
                                               x_tok[:, t4 * 4 + a, k * P:(k + 1) * P], ident[:])
                last.then_inc(transposed, 1)
            pe.wait_ge(xT_done_act, NG // 2)
            pe.wait_ge(xT_done_dve, NG // 2)
            pe.wait_ge(w_in, 16 * 8)
            for n in range(NT):
                for k in range(KE):
                    last = nc.tensor.matmul(ps[:, 2 + n // 8, (n % 8) * 64:(n % 8) * 64 + 64],
                                            xT[:, k, n * P:(n + 1) * P], wv[:, k, :], start=(k == 0), stop=(k == KE - 1))
                last.then_inc(v_ready, 1)
            for m, (kind, c, n) in enumerate(jobs):
                r, wt = rows[kind], wq if kind == "q" else wk
                if m >= 2:
                    pe.wait_ge(rotated, 2 * (m - 1))
                for s in range(2):
                    for k in range(KE):
                        last = nc.tensor.matmul(ps[0:r, 4 + 2 * (m % 2) + s, :], wt[:, k, s, c * P:c * P + r],
                                                xT[:, k, n * HALF:(n + 1) * HALF], start=(k == 0), stop=(k == KE - 1))
                last.then_inc(projected, 1)

        @block.gpsimd
        def _(pool):
            nc.gpsimd.memset(v_aug[:], 0.0).then_inc(v_clear, 1)
            pool.wait_ge(v_clear, 1)
            nc.gpsimd.memset(v_aug[:, :, :, D:D + 1], 1.0).then_inc(v_clear, 1)
            U32 = mybir.dt.uint32
            for p in range(2):
                for buf in (cst["q1"][p], cst["q2"][p]):
                    nc.gpsimd.memset(buf[:].rearrange("p g t -> p (g t)").bitcast(U32), 0).then_inc(v_clear, 1)
                nc.gpsimd.memset(cst["k1"][p][:].bitcast(U32), 0).then_inc(v_clear, 1)
                nc.gpsimd.memset(cst["k2"][p][:], 1.0).then_inc(v_clear, 1)
            pool.wait_ge(v_clear, 10)
            for m, (kind, c, n) in enumerate(jobs):
                r = rows[kind]
                pool.wait_ge(rotated, 2 * m + 2)
                if m >= 2:
                    pool.wait_ge(high_left, m - 1)
                nc.gpsimd.tensor_tensor(rot[0:r, m % 2], t1[0:r, m % 2], t2[0:r, m % 2], ALU.add).then_inc(summed, 1)

        @block.scalar
        def _(act):
            for g in range(0, NG, 2):
                k, t4 = g % KE, g // KE
                act.wait_ge(transposed, g + 1)
                nc.scalar.activation(xT[:, k, t4 * HALF:(t4 + 1) * HALF], ps[:, g % 2, :], ACT.Copy).then_inc(xT_done_act, 1)
            for m, (kind, c, n) in enumerate(jobs):
                r = rows[kind]
                act.wait_ge(summed, m + 1)
                if m >= 2:
                    act.wait_ge(stored[m % 2], 16 * (m // 2))
                nc.scalar.activation(parts[0:r, m % 2, 0], rot[0:r, m % 2], ACT.Copy).then_inc(high, 1)
                act.wait_ge(high_left, m + 1)
                nc.scalar.activation(parts[0:r, m % 2, 1], rest[0:r, m % 2], ACT.Copy).then_inc(mid, 1)

        @block.vector
        def _(dve):
            for g in range(1, NG, 2):
                k, t4 = g % KE, g // KE
                dve.wait_ge(transposed, g + 1)
                nc.vector.tensor_copy(xT[:, k, t4 * HALF:(t4 + 1) * HALF], ps[:, g % 2, :]).then_inc(xT_done_dve, 1)
            dve.wait_ge(v_clear, 2)
            dve.wait_ge(w_in, 16 * 8)
            for n in range(NT):
                dve.wait_ge(v_ready, (n // 8 + 1) * 8)
                nc.vector.tensor_tensor(v_aug[:, n, :, 0:D],
                                        ps[:, 2 + n // 8, (n % 8) * 64:(n % 8) * 64 + 64].rearrange("p (h d) -> p h d", d=D),
                                        bv[:].rearrange("p (h d) -> p h d", d=D), ALU.add).then_inc(v_added, 1)
            def split(m):
                r = rows[jobs[m][0]]
                dve.wait_ge(high, m + 1)
                nc.vector.tensor_tensor(rest[0:r, m % 2], rot[0:r, m % 2], parts[0:r, m % 2, 0], ALU.subtract).then_inc(high_left, 1)

            def split_low(m):
                r = rows[jobs[m][0]]
                dve.wait_ge(mid, m + 1)
                nc.vector.tensor_tensor(parts[0:r, m % 2, 2], rest[0:r, m % 2], parts[0:r, m % 2, 1],
                                        ALU.subtract).then_inc(low, 1)

            for m, (kind, c, n) in enumerate(jobs):
                r = rows[kind]
                tt = (n * HALF) % T
                bias = bq if kind == "q" else bk
                dve.wait_ge(projected, m + 1)
                if m >= 2:
                    dve.wait_ge(summed, m - 1)
                b0 = bias[0:r, 0, c:c + 1] if kind == "q" else bias[0:r, 0:1]
                b1 = bias[0:r, 1, c:c + 1] if kind == "q" else bias[0:r, 1:2]
                nc.vector.scalar_tensor_tensor(t1[0:r, m % 2], ps[0:r, 4 + 2 * (m % 2), :], b0, cos[0:r, tt:tt + HALF],
                                               ALU.add, ALU.mult).then_inc(rotated, 1)
                nc.vector.scalar_tensor_tensor(t2[0:r, m % 2], ps[0:r, 5 + 2 * (m % 2), :], b1, sin[0:r, tt:tt + HALF],
                                               ALU.add, ALU.mult).then_inc(rotated, 1)
                if m >= 1:
                    split(m - 1)
                    split_low(m - 1)
            split(len(jobs) - 1)
            split_low(len(jobs) - 1)


Q_PARTS = (0, 0, 1, 0, 2, 1)
K_PARTS = (0, 1, 0, 2, 0, 1)
NPROD = len(Q_PARTS) * D
UNITS = B * HKV
VW = 32
W_STEP, W_COL, W_VALUE_COL, W_LAST_VALUES, W_OUTPUT, W_PIECE = 72, 0.79, 1.5, 308, 790, 136
MAXCOLS = TB + TB // 2


def head_pieces():
    out = []
    for i in range(TB):
        n = (i + 1) * P
        for c0 in range(0, n, HALF):
            w = min(HALF, n - c0)
            out.append((i, c0, w, c0 + w == n, i if c0 == 0 else TB + i - TB // 2))
    return out


def attention(nc, ps, y_tok, cst, dram):
    with phase(nc) as ctx:
        sb = lambda n, s, d=F32: ctx.enter_context(nc.sbuf_tensor(n, s, d))
        sem = lambda n: nc.alloc_semaphore(n)
        ident, identb, neg_qk, neg_kq, v_aug = (cst[n] for n in ("ident", "identb", "neg_qk", "neg_kq", "v_aug"))
        q1, k1, q2, k2 = (cst[n] for n in ("q1", "k1", "q2", "k2"))
        v1 = [sb(f"a_v_{p}", [P, TB, VW]) for p in range(2)]
        mx = sb("a_mx", [P, 2, G, MAXCOLS])
        nm = sb("a_nm", [P, 2, G, TB])
        nmT = sb("a_nmT", [G * TB, P])
        nrest = sb("a_nrest", [G * TB, 2, P])
        nparts = sb("a_nparts", [G * TB, 3, P], BF16)
        prob = sb("a_prob", [P, 2, G, T])
        oT = sb("a_oT", [P, T])
        rden = sb("a_rden", [P, TB, G])

        q1_in = [sem(f"a_q1_in{p}") for p in range(2)]
        q2_in = [sem(f"a_q2_in{p}") for p in range(2)]
        row_in = [sem(f"a_row_in{p}") for p in range(2)]
        scored = sem("a_scored")
        reduced = sem("a_reduced")
        piece_max = sem("a_piece_max")
        maxima = sem("a_maxima")
        copied = sem("a_copied")
        high, rest, mid, rest2, low = (sem(f"a_{n}") for n in ("high", "rest", "mid", "rest2", "low"))
        st_ready = sem("a_st_ready")
        st_exp = sem("a_st_exp")
        pv_done = sem("a_pv_done")
        o_copied = sem("a_o_copied")
        o_turned = sem("a_o_turned")
        o_recip = sem("a_o_recip")
        o_scaled = sem("a_o_scaled")
        v_in = sem("a_v_in")
        past = sem("a_past")
        block = ctx.enter_context(nc.Block())
        S1, ST, O = 0, 2, 6
        PIECES = head_pieces()
        ITEMS = len(PIECES) * G + 1
        STEPS = TB * G
        LOOPED = (UNITS - 2) // 2
        Q_DMAS = 16 * 2 * len(Q_PARTS)

        def items_of(heads):
            out = [("piece", u, g, x) for u, g in heads for x in PIECES]
            for n, (_, u, g, x) in enumerate(out):
                if g == G - 1 and x is PIECES[-1]:
                    out.insert(min(n + 5, len(out)), ("turn", u, None, None))
                    break
            return out

        FIRST = items_of([(0, g) for g in range(G)] + [(1, 0), (1, 1)])

        def stage_plan(u, last):
            heads = [] if u == last else [(u + 1, 2), (u + 1, 3)]
            if u + 2 <= last:
                heads += [(u + 2, 0), (u + 2, 1)]
            items = items_of(heads)
            steps = []
            for s in range(2, STEPS):
                steps.append((W_STEP + W_COL * (T - s // G * P), ("scores", u, s, None)))
                if s % G == 1:
                    steps += [(W_VALUE_COL * (min(T, (h + 1) * HALF) - max(h * HALF, (s // G - 1) * P)), ("values", u, s // G - 1, h))
                              for h in range(2) if (s // G - 1) * P < (h + 1) * HALF]
            if u < last:
                steps += [(W_STEP + W_COL * T, ("scores", u + 1, n, None)) for n in range(2)]
            steps += [(W_LAST_VALUES, ("values", u, TB - 1, 1)), (W_OUTPUT, ("output", u, None, None))]
            cost = lambda it: W_PIECE + (it[3][2] if it[0] == "piece" else P)
            total, items_total = sum(c for c, _ in steps), sum(map(cost, items)) * 4 / max(1, len(heads))
            plan, done, items_done, n = [], 0, 0, 0
            for c, step in steps:
                if step[0] == "output":
                    done += c
                while n < len(items) and (items_done + cost(items[n]) / 2) * total <= done * items_total:
                    items_done += cost(items[n])
                    plan.append(items[n])
                    n += 1
                plan.append(step)
                if step[0] != "output":
                    done += c
            plan = plan[:-1] + items[n:] + plan[-1:]
            return plan

        def stages(eng, run, lp):
            with eng.Fori(0, LOOPED) as i:
                lp.i = i
                for u in range(2):
                    run(stage_plan(u, 99), i * 2)
            lp.i = LOOPED - 1
            for u in range(2, 4):
                run(stage_plan(u, 3), (LOOPED - 1) * 2)

        @block.sync
        def _(sp):
            lp = Loop()

            def load(dst_q, dst_k, u, arrived):
                b, kv = u // HKV, u % HKV
                for j in range(len(Q_PARTS)):
                    sp.dma_start(dst_q[j * D:(j + 1) * D, :, :],
                                 dram["q"][Q_PARTS[j], bass.ds(kv * (G * D), G * D), bass.ds(b * T, T)]
                                 .rearrange("(g d) t -> d g t", d=D)).then_inc(arrived, 16)
                    sp.dma_start(dst_k[j * D:(j + 1) * D, :],
                                 dram["k"][K_PARTS[j], bass.ds(kv * D, D), bass.ds(b * T, T)]).then_inc(arrived, 16)

            def rows(p):
                for j in range(3):
                    sp.dma_start(q2[p][NPROD + j:NPROD + j + 1, :, :].rearrange("o g (i t) -> o (g i) t", t=P),
                                 nparts[:, j, :]).then_inc(row_in[p], 16)

            load(q1[0], k1[0], 0, q1_in[0])
            load(q1[1], k1[1], 1, q1_in[1])
            load(q2[0], k2[0], 0, q2_in[0])
            sp.wait_ge(low, 1)
            rows(0)

            def stage(u, n, ahead):
                p = n % 2
                if ahead == 2:
                    sp.wait_ge(maxima, lp.at(n + 1, 2))
                    load(q1[p], k1[p], u + 2, q1_in[p])
                sp.wait_ge(pv_done, lp.at(TB * n + 2, 2 * TB))
                load(q2[1 - p], k2[1 - p], u + 1, q2_in[1 - p])
                sp.wait_ge(low, lp.at(n + 2, 2))
                rows(1 - p)

            with sp.Fori(0, LOOPED) as i:
                lp.i = i
                stage(i * 2, 0, 2)
                stage(i * 2 + 1, 1, 2)
            lp.i = LOOPED - 1
            stage(UNITS - 2, 2, 1)

        @block.gpsimd
        def _(pool):
            lp = Loop()
            def values(u, n):
                nc.gpsimd.tensor_copy(v1[n % 2][:], v_aug[:, bass.ds((u // HKV) * TB, TB), bass.ds(u % HKV, 1), :]
                                      .rearrange("p n o c -> p n (o c)")).then_inc(v_in, 1)

            def cut(n):
                c = lp.at(n + 1, 2)
                pool.wait_ge(copied, c)
                pool.sem_inc(past, 1)
                nc.gpsimd.tensor_copy(nparts[:, 0, :], nmT[:]).then_inc(high, 1)
                pool.wait_ge(high, c)
                nc.gpsimd.tensor_tensor(nrest[:, 0, :], nmT[:], nparts[:, 0, :], ALU.subtract).then_inc(rest, 1)
                pool.wait_ge(rest, c)
                pool.sem_inc(past, 1)
                nc.gpsimd.tensor_copy(nparts[:, 1, :], nrest[:, 0, :]).then_inc(mid, 1)
                pool.wait_ge(mid, c)
                nc.gpsimd.tensor_tensor(nrest[:, 1, :], nrest[:, 0, :], nparts[:, 1, :], ALU.subtract).then_inc(rest2, 1)
                pool.wait_ge(rest2, c)
                pool.sem_inc(past, 1)
                nc.gpsimd.tensor_copy(nparts[:, 2, :], nrest[:, 1, :]).then_inc(low, 1)

            values(0, 0)
            cut(0)

            def stage(u, n):
                pool.wait_ge(pv_done, lp.at(TB * n + 2, 2 * TB))
                values(u + 1, n + 1)
                pool.wait_ge(row_in[n % 2], lp.at(48 * (n // 2 + 1), 48))
                cut(n + 1)

            with pool.Fori(0, LOOPED) as i:
                lp.i = i
                stage(i * 2, 0)
                stage(i * 2 + 1, 1)
            lp.i = LOOPED - 1
            stage(UNITS - 2, 2)

        @block.tensor
        def _(pe):
            lp = Loop()
            n_item, n_step, n_pv, n_out = [0], [0], [0], [0]

            def item(it):
                kind, u, g, x = it
                p, bank = u % 2, S1 + n_item[0] % 2
                n_item[0] += 1
                if kind == "piece":
                    i, c0, w, diagonal, _ = x
                    if g == 0 and x is PIECES[0]:
                        pe.wait_ge(q1_in[p], lp.at(Q_DMAS * (u // 2 + 1), Q_DMAS))
                    pe.wait_ge(reduced, lp.at(n_item[0], 2 * ITEMS))
                    q = q1[p][:, g, i * P:(i + 1) * P]
                    last = nc.tensor.matmul(ps[:, bank, 0:w], q, k1[p][:, c0:c0 + w], start=True, stop=not diagonal)
                    if diagonal:
                        last = nc.tensor.matmul(ps[:, bank, w - P:w], identb[:], neg_qk[:], start=False, stop=True)
                else:
                    pe.wait_ge(maxima, lp.at(u + 1, 2))
                    pe.wait_ge(reduced, lp.at(n_item[0], 2 * ITEMS))
                    last = nc.tensor.transpose(ps[0:G * TB, bank, 0:P], nm[:, p].rearrange("p g i -> p (g i)"), ident[:])
                last.then_inc(scored, 1)

            def scores(u, s):
                j, g = s // G, s % G
                p, bank = u % 2, ST + 2 * (s % 2)
                n_step[0] += 1
                if s == 0:
                    pe.wait_ge(q2_in[p], lp.at(Q_DMAS * (u // 2 + 1), Q_DMAS))
                    pe.wait_ge(row_in[p], lp.at(48 * (u // 2 + 1), 48))
                pe.wait_ge(st_exp, lp.at(n_step[0], 2 * STEPS))
                k = k2[p][:, j * P:(j + 1) * P]
                c0 = j * P
                while c0 < T:
                    w = min(HALF - c0 % HALF, T - c0)
                    out = ps[:, bank + c0 // HALF, c0 % HALF:c0 % HALF + w]
                    masked = c0 == j * P
                    last = nc.tensor.matmul(out, k, q2[p][:, g, c0:c0 + w], start=True, stop=not masked)
                    if masked:
                        last = nc.tensor.matmul(out[:, 0:P], identb[:], neg_kq[:], start=False, stop=True)
                    c0 += w
                last.then_inc(st_ready, 1)

            def products(u, j, half):
                p = u % 2
                first = half == 0 or j * P >= HALF
                n_pv[0] += first
                if j == 0 and first:
                    pe.wait_ge(v_in, lp.at(u + 1, 2))
                    pe.wait_ge(o_scaled, lp.at(u + 1, 2))
                if first:
                    pe.wait_ge(st_exp, lp.at(2 + G * n_pv[0], 2 * STEPS))
                c0, c1 = max(j * P, half * HALF), (half + 1) * HALF
                for g in range(G):
                    last = nc.tensor.matmul(ps[g * VW:(g + 1) * VW, O + half, c0 % HALF:c0 % HALF + c1 - c0], v1[p][:, j, :],
                                            prob[:, j % 2, g, c0:c1], start=(j == 0),
                                            stop=(j == min(TB - 1, c1 // P - 1)), skip_group_check=True)
                if half == 1:
                    last.then_inc(pv_done, 1)

            def output(u):
                n_out[0] += 1
                pe.wait_ge(o_copied, lp.at(n_out[0], 2))
                for i in range(TB):
                    last = nc.tensor.transpose(ps[:, O + i // 4, (i % 4) * P:(i % 4 + 1) * P], oT[:, i * P:(i + 1) * P], ident[:])
                last.then_inc(o_turned, 1)

            def run(plan, _):
                for ev in plan:
                    if ev[0] == "scores":
                        scores(ev[1], ev[2])
                    elif ev[0] == "values":
                        products(ev[1], ev[2], ev[3])
                    elif ev[0] == "output":
                        output(ev[1])
                    else:
                        item(ev)

            pe.sem_inc(pv_done, 2)
            for it in FIRST:
                item(it)
            scores(0, 0)
            scores(0, 1)
            stages(pe, run, lp)

        @block.scalar
        def _(act):
            lp = Loop()
            n_step, n_out = [0], [0]
            act.sem_inc(st_exp, 2)

            def exponentials(u, s):
                j, g = s // G, s % G
                n_step[0] += 1
                act.wait_ge(st_ready, lp.at(n_step[0], 2 * STEPS))
                if g == 0:
                    act.wait_ge(pv_done, lp.at(TB * u + j + 1, 2 * TB))
                bank = ST + 2 * (s % 2)
                st = ps[:, bank:bank + 2, :].rearrange("p b c -> p (b c)")
                nc.scalar.activation(prob[:, j % 2, g, j * P:T], st[:, j * P:T], ACT.Exp, scale=float(D) ** -0.5).then_inc(st_exp, 1)

            def output(u):
                n_out[0] += 1
                act.wait_ge(pv_done, lp.at(TB * n_out[0] + 2, 2 * TB))
                nc.scalar.activation(oT[:], ps[:, O:O + 2, :].rearrange("p b c -> p (b c)"), ACT.Copy).then_inc(o_copied, 1)

            def run(plan, _):
                for ev in plan:
                    if ev[0] == "scores":
                        exponentials(ev[1], ev[2])
                    elif ev[0] == "output":
                        output(ev[1])

            exponentials(0, 0)
            exponentials(0, 1)
            stages(act, run, lp)

        @block.vector
        def _(dve):
            lp = Loop()
            n_item, n_out = [0], [0]
            dve.sem_inc(reduced, 2)
            dve.sem_inc(o_scaled, 1)

            def item(it):
                kind, u, g, x = it
                p, bank = u % 2, S1 + n_item[0] % 2
                n_item[0] += 1
                dve.wait_ge(scored, lp.at(n_item[0], 2 * ITEMS))
                if kind == "turn":
                    if u:
                        dve.wait_ge(low, lp.at(u, 2))
                    nc.vector.tensor_copy(nmT[:], ps[0:G * TB, bank, 0:P]).then_inc(copied, 1)
                    dve.wait_ge(copied, lp.at(u + 1, 2))
                    dve.sem_inc(reduced, 1)
                    return
                i, c0, w, diagonal, col = x
                nc.vector.tensor_reduce(mx[:, p, g, col:col + 1], ps[:, bank, 0:w], AX.X, ALU.max, negate=True).then_inc(reduced, 1)
                if g == G - 1 and x is PIECES[-1]:
                    dve.wait_ge(reduced, lp.at(n_item[0] + 2, 2 * ITEMS))
                    nc.vector.tensor_copy(nm[:, p, :, 0:TB // 2], mx[:, p, :, 0:TB // 2]).then_inc(piece_max, 1)
                    dve.wait_ge(piece_max, lp.at(u + 1, 2))
                    nc.vector.tensor_tensor(nm[:, p, :, TB // 2:], mx[:, p, :, TB // 2:TB], mx[:, p, :, TB:], ALU.min).then_inc(maxima, 1)

            def output(u, base):
                n_out[0] += 1
                unit = base + u
                dve.wait_ge(o_turned, lp.at(n_out[0], 2))
                o = ps[:, O:O + 2, :].rearrange("p b (i g c) -> p (b i) g c", g=G, c=VW)
                nc.vector.reciprocal(rden[:], o[:, :, :, D]).then_inc(o_recip, 1)
                dve.wait_ge(o_recip, lp.at(n_out[0], 2))
                y = y_tok[:, bass.ds((unit // HKV) * TB, TB), bass.ds((unit % HKV) * (G * D), G * D)]
                nc.vector.tensor_tensor(y.rearrange("p i (g d) -> p i g d", d=D), o[:, :, :, 0:D],
                                        rden[:].unsqueeze(3).to_broadcast([P, TB, G, D]), ALU.mult).then_inc(o_scaled, 1)

            def run(plan, base):
                for ev in plan:
                    if ev[0] in ("piece", "turn"):
                        item(ev)
                    elif ev[0] == "output":
                        output(ev[1], base)

            for it in FIRST:
                item(it)
            stages(dve, run, lp)


BLK = TOK // HALF
BT = HALF // P


class Norm:

    def __init__(self, nc, ctx, name, x_tok, cst):
        sb = lambda n, s, d=F32: ctx.enter_context(nc.sbuf_tensor(f"{name}_{n}", s, d))
        sem = lambda n: nc.alloc_semaphore(f"{name}_{n}")
        self.nc, self.x, self.pow_half = nc, x_tok, cst["pow_half"]
        self.tmp, self.st = sb("tmp", [P, BT, E]), sb("st", [P, BT, 6])
        self.mv, self.rs = sb("mv", [P, 2, BT, 2]), sb("rs", [P, 2, 2, BT])
        self.chain, self.links = sem("chain"), 0
        self.stats, self.eps_in, self.rstd, self.done = sem("stats"), sem("eps_in"), sem("rstd"), sem("normed")

    def link(self, dve, ins):
        self.links += 1
        ins.then_inc(self.chain, 1)
        dve.wait_ge(self.chain, self.links)

    def residual(self, dve, n, acc, scale, freed):
        nc, xs = self.nc, self.x[:, n * BT:(n + 1) * BT, :]
        if scale is None:
            ins = nc.vector.tensor_tensor(xs, acc, xs, ALU.add)
        else:
            self.link(dve, nc.vector.tensor_tensor(self.tmp[:], acc, scale.unsqueeze(1).to_broadcast([P, BT, E]), ALU.mult))
            ins = nc.vector.tensor_tensor(xs, self.tmp[:], xs, ALU.add)
        ins.then_inc(freed, 1)

    def statistics(self, dve, n, summed=None):
        nc, xs = self.nc, self.x[:, n * BT:(n + 1) * BT, :]
        if summed is not None:
            dve.wait_ge(summed, n + 1)
        if n >= 1:
            dve.wait_ge(self.stats, n)
        for a in range(BT):
            ins = nc.vector.bn_stats(self.st[:, a, :], xs[:, a, :])
        self.link(dve, ins)
        if n >= 2:
            dve.wait_ge(self.done, n - 1)
        for a in range(BT):
            ins = nc.vector.bn_aggr(self.mv[:, n % 2, a, :], self.st[:, a, :])
        ins.then_inc(self.stats, 1)

    def inverse_root(self, pool, n):
        nc = self.nc
        pool.wait_ge(self.stats, n + 1)
        nc.gpsimd.tensor_scalar(self.rs[:, n % 2, 0], self.mv[:, n % 2, :, 1], EPS, None, ALU.add).then_inc(self.eps_in, 1)
        pool.wait_ge(self.eps_in, n + 1)
        nc.gpsimd.tensor_tensor(self.rs[:, n % 2, 1], self.rs[:, n % 2, 0], self.pow_half[:, 0:BT], ALU.pow).then_inc(self.rstd, 1)

    def normalise(self, dve, n):
        nc, xs = self.nc, self.x[:, n * BT:(n + 1) * BT, :]
        dve.wait_ge(self.rstd, n + 1)
        for a in range(BT):
            ins = nc.vector.tensor_scalar(xs[:, a, :], xs[:, a, :], self.mv[:, n % 2, a, 0:1], self.rs[:, n % 2, 1, a:a + 1],
                                          ALU.subtract, ALU.mult)
        ins.then_inc(self.done, 1)


def pair_view(ps, bank):
    return ps[:, bank:bank + 2, :].rearrange("p b (h c) -> p (b h) c", c=E)


def output_projection(nc, ps, x_tok, y_tok, cst, w):
    with phase(nc) as ctx:
        sb = lambda n, s, d=F32: ctx.enter_context(nc.sbuf_tensor(n, s, d))
        sem = lambda n: nc.alloc_semaphore(n)
        yT = sb("o_yT", [P, 2, KE, HALF])
        wo, bo = sb("o_wo", [P, KE, E]), sb("o_bo", [P, E])
        w_in, biased = sem("o_w_in"), sem("o_biased")
        turned, evacuated, projected, freed = sem("o_turned"), sem("o_evacuated"), sem("o_projected"), sem("o_freed")
        norm = Norm(nc, ctx, "o", x_tok, cst)
        ident = cst["ident"]
        block = ctx.enter_context(nc.Block())

        @block.sync
        def _(sp):
            sp.dma_start(wo[:], w["wo"].rearrange("(k p) n -> p k n", p=P)).then_inc(w_in, 16)
            sp.dma_start(bo[:], w["bo"].partition_broadcast(P)).then_inc(w_in, 16)

        @block.tensor
        def _(pe):
            def turn(n):
                for k in range(KE):
                    if n >= 1:
                        pe.wait_ge(evacuated, KE * (n - 1) + k + 1)
                    for a in range(BT):
                        last = nc.tensor.transpose(ps[:, k, a * P:(a + 1) * P], y_tok[:, n * BT + a, k * P:(k + 1) * P], ident[:])
                    last.then_inc(turned, 1)

            turn(0)
            pe.wait_ge(w_in, 32)
            for n in range(BLK):
                if n + 1 < BLK:
                    turn(n + 1)
                pe.wait_ge(evacuated, KE * (n + 1))
                if n >= 2:
                    pe.wait_ge(freed, n - 1)
                for a in range(BT):
                    for k in range(KE):
                        last = nc.tensor.matmul(ps[:, 2 + 2 * (n % 2) + a // 2, (a % 2) * E:(a % 2 + 1) * E],
                                                yT[:, n % 2, k, a * P:(a + 1) * P], wo[:, k, :], start=(k == 0), stop=(k == KE - 1))
                last.then_inc(projected, 1)

        @block.scalar
        def _(act):
            for n in range(BLK):
                for k in range(KE):
                    act.wait_ge(turned, KE * n + k + 1)
                    if n >= 2:
                        act.wait_ge(projected, n - 1)
                    nc.scalar.activation(yT[:, n % 2, k, :], ps[:, k, :], ACT.Copy).then_inc(evacuated, 1)

        @block.gpsimd
        def _(pool):
            pool.wait_ge(w_in, 32)
            for n in range(BLK):
                nc.gpsimd.tensor_tensor(x_tok[:, n * BT:(n + 1) * BT, :], x_tok[:, n * BT:(n + 1) * BT, :],
                                        bo[:].unsqueeze(1).to_broadcast([P, BT, E]), ALU.add).then_inc(biased, 1)
            for n in range(BLK):
                norm.inverse_root(pool, n)

        @block.vector
        def _(dve):
            for n in range(BLK):
                dve.wait_ge(biased, n + 1)
                dve.wait_ge(projected, n + 1)
                norm.residual(dve, n, pair_view(ps, 2 + 2 * (n % 2)), None, freed)
                norm.statistics(dve, n, freed)
                if n >= 1:
                    norm.normalise(dve, n - 1)
            norm.normalise(dve, BLK - 1)


FF = 1024
NC = FF // P
DEEP = 3


class Weights:

    def __init__(self, nc, ctx, t, w):
        sb = lambda n, s, d=F32: ctx.enter_context(nc.sbuf_tensor(f"{t}_{n}", s, d))
        self.t, self.w, self.n_up = t, w, w["up"].shape[0]
        self.arrived, self.count = ctx.enter_context(nc.semaphore(f"{t}_w_in")), 0
        pack = 1 if w["up"].dtype == F32 else 4
        self.raw_up, self.raw_down = sb("raw_up", [P, self.n_up, KE, FF // pack], w["up"].dtype), sb("raw_down", [P, NC, E // pack], w["up"].dtype)
        as_stored = (lambda v: v[:]) if pack == 1 else (lambda v: v[:].bitcast(mybir.dt.int8))
        self.up, self.down = as_stored(self.raw_up), as_stored(self.raw_down)
        self.up_scale, self.down_scale, self.out_scale = sb("up_scale", [P, self.n_up, NC]), sb("down_scale", [P, E]), sb("out_scale", [P, 1])

    def fetch(self, sp):
        w = self.w
        loads = [(self.raw_up[:, s], w["up"][s].rearrange("(k p) n -> p k n", p=P)) for s in range(self.n_up)]
        loads += [(self.raw_down[:], w["down"].rearrange("(c p) n -> p c n", p=P)), (self.up_scale[:], w["up_scale"]),
                  (self.down_scale[:], w["down_scale"].partition_broadcast(P))]
        if "out_scale" in w:
            loads += [(self.out_scale[:], w["out_scale"].partition_broadcast(P))]
        for dst, src in loads:
            sp.dma_start(dst, src).then_inc(self.arrived, 16)
        self.count = 16 * len(loads)


def feed_forward(nc, ps, x_tok, cst, w, gated, out=None):
    t, NU = w.t, w.n_up
    with phase(nc) as ctx:
        sb = lambda n, s, d=F32: ctx.enter_context(nc.sbuf_tensor(f"{t}_{n}", s, d))
        sem = lambda n: nc.alloc_semaphore(f"{t}_{n}")
        xT, x_rest = sb("xT", [P, KE, HALF]), sb("x_rest", [P, KE, HALF])
        xp = sb("xp", [P, 2, 3, KE, HALF], BF16)
        wu, wd = sb("wu", [P, NU, KE, FF], BF16), sb("wd", [P, NC, E], BF16)
        h1 = sb("h1", [P, 2, HALF])
        h, h_rest = sb("h", [P, DEEP, HALF]), sb("h_rest", [P, DEEP, HALF])
        hp = sb("hp", [P, 2, 3, NC, HALF], BF16)
        cast, cast_d, neg, folded = sem("cast"), sem("cast_d"), sem("neg"), sem("folded")
        turned, evacuated, uped, act_done = sem("turned"), sem("evacuated"), sem("uped"), sem("act_done")
        x_high, x_left, x_mid, x_low = sem("x_high"), sem("x_left"), sem("x_mid"), sem("x_low")
        h_ready, h_high, h_left, h_mid, h_low = sem("h_ready"), sem("h_high"), sem("h_left"), sem("h_mid"), sem("h_low")
        downed, freed, stored = sem("downed"), sem("freed"), sem("stored")
        norm = Norm(nc, ctx, t, x_tok, cst)
        ident = cst["ident"]
        block = ctx.enter_context(nc.Block())
        D0 = 3 if gated else 4
        UP, DOWN = 2, 6

        @block.sync
        def _(sp):
            if out is not None:
                for n in range(BLK):
                    sp.wait_ge(norm.done, n + 1)
                    sp.dma_start(out[n * BT:(n + 1) * BT].rearrange("n p c -> p n c"), x_tok[:, n * BT:(n + 1) * BT, :]).then_inc(stored, 16)
                sp.wait_ge(stored, 16 * BLK)

        @block.tensor
        def _(pe):
            def turn(n):
                for k in range(KE):
                    if n >= 1:
                        pe.wait_ge(evacuated, KE * (n - 1) + k + 1)
                    for a in range(BT):
                        last = nc.tensor.transpose(ps[:, k, a * P:(a + 1) * P], x_tok[:, n * BT + a, k * P:(k + 1) * P], ident[:])
                    last.then_inc(turned, 1)

            def down(n, a):
                if a == 0:
                    pe.wait_ge(cast_d, 1)
                    pe.wait_ge(h_low, NC * (n + 1))
                    if n >= 1:
                        pe.wait_ge(freed, n)
                for c in range(NC):
                    for i in range(3):
                        last = nc.tensor.matmul(ps[:, DOWN + a // 2, (a % 2) * E:(a % 2 + 1) * E], hp[:, n % 2, i, c, a * P:(a + 1) * P],
                                                wd[:, c, :], start=(c == 0 and i == 0), stop=(c == NC - 1 and i == 2))
                if a == BT - 1:
                    last.then_inc(downed, 1)

            turn(0)
            pe.wait_ge(cast, NU)
            m = 0
            for n in range(BLK):
                if n + 1 < BLK:
                    turn(n + 1)
                pe.wait_ge(x_low, KE * (n + 1))
                for c in range(NC):
                    if m >= 2:
                        pe.wait_ge(h_ready, m - 1)
                    for s in range(NU):
                        for k in range(KE):
                            for i in range(3):
                                last = nc.tensor.matmul(ps[:, UP + 2 * (m % 2) + s, :], wu[:, s, k, c * P:(c + 1) * P], xp[:, n % 2, i, k, :],
                                                        start=(k == 0 and i == 0), stop=(k == KE - 1 and i == 2))
                    last.then_inc(uped, 1)
                    m += 1
                    if n >= 1 and D0 <= c < D0 + BT:
                        down(n - 1, c - D0)
            for a in range(BT):
                down(BLK - 1, a)

        @block.scalar
        def _(act):
            act.wait_ge(w.arrived, w.count)
            if gated:
                for s in range(NU):
                    nc.scalar.activation(wu[:, s], w.up[:, s], ACT.Copy).then_inc(cast, 1)

            def high_x(n):
                for k in range(KE):
                    act.wait_ge(turned, KE * n + k + 1)
                    if n >= 1:
                        act.wait_ge(x_left, KE * (n - 1) + k + 1)
                    nc.scalar.activation(xT[:, k, :], ps[:, k, :], ACT.Copy).then_inc(evacuated, 1)
                for k in range(KE):
                    act.wait_ge(evacuated, KE * n + k + 1)
                    if n >= 2:
                        act.wait_ge(uped, NC * (n - 1))
                    nc.scalar.activation(xp[:, n % 2, 0, k, :], xT[:, k, :], ACT.Copy).then_inc(x_high, 1)

            def middle_x(n):
                for k in range(KE):
                    act.wait_ge(x_left, KE * n + k + 1)
                    nc.scalar.activation(xp[:, n % 2, 1, k, :], x_rest[:, k, :], ACT.Copy).then_inc(x_mid, 1)

            def high(m):
                n, c = m // NC, m % NC
                act.wait_ge(h_ready, m + 1)
                if n >= 2 and c == 0:
                    act.wait_ge(downed, n - 1)
                nc.scalar.activation(hp[:, n % 2, 0, c, :], h[:, m % DEEP], ACT.Copy).then_inc(h_high, 1)

            def middle(m):
                act.wait_ge(h_left, m + 1)
                nc.scalar.activation(hp[:, m // NC % 2, 1, m % NC, :], h_rest[:, m % DEEP], ACT.Copy).then_inc(h_mid, 1)

            high_x(0)
            middle_x(0)
            if gated:
                nc.scalar.activation(wd[:], w.down, ACT.Copy).then_inc(cast_d, 1)
            for n in range(BLK):
                for c in range(NC):
                    m = n * NC + c
                    act.wait_ge(uped, m + 1)
                    if gated and m >= 2:
                        act.wait_ge(h_ready, m - 1)
                    if not gated and m >= DEEP:
                        act.wait_ge(h_left, m - DEEP + 1)
                    if gated:
                        nc.scalar.activation(h1[:, m % 2], ps[:, UP + 2 * (m % 2), :], ACT.Silu, scale=w.up_scale[:, 0, c:c + 1]).then_inc(act_done, 1)
                    else:
                        nc.scalar.activation(h[:, m % DEEP], ps[:, UP + 2 * (m % 2), :], ACT.Relu, scale=w.up_scale[:, 0, c:c + 1]).then_inc(h_ready, 1)
                    if m >= 1:
                        high(m - 1)
                    if m >= 2:
                        middle(m - 2)
                    if c == 1 and n + 1 < BLK:
                        high_x(n + 1)
                    if c == 3 and n + 1 < BLK:
                        middle_x(n + 1)
            high(BLK * NC - 1)
            middle(BLK * NC - 2)
            middle(BLK * NC - 1)

        @block.gpsimd
        def _(pool):
            for n in range(BLK):
                norm.inverse_root(pool, n)

        @block.vector
        def _(dve):
            dve.wait_ge(w.arrived, w.count)
            if not gated:
                nc.vector.tensor_scalar(wu[:, 0], w.up[:, 0], 0.0, None, ALU.is_lt).then_inc(neg, 1)
                nc.vector.tensor_scalar(wd[:], w.down, 0.0, None, ALU.is_lt).then_inc(neg, 1)
                nc.vector.tensor_scalar(w.down_scale[:], w.down_scale[:], w.out_scale[:, 0:1], None, ALU.mult).then_inc(folded, 1)
                fl = lambda v: v.rearrange("p a b -> p (a b)")
                dve.wait_ge(neg, 1)
                nc.vector.scalar_tensor_tensor(fl(wu[:, 0]), fl(w.up[:, 0]), 0.0, fl(wu[:, 0]), ALU.is_gt, ALU.subtract).then_inc(cast, 1)

            def rest_x(n):
                for k in range(KE):
                    dve.wait_ge(x_high, KE * n + k + 1)
                    if n >= 1:
                        dve.wait_ge(x_low, KE * (n - 1) + k + 1)
                    nc.vector.tensor_tensor(x_rest[:, k, :], xT[:, k, :], xp[:, n % 2, 0, k, :], ALU.subtract).then_inc(x_left, 1)

            def low_x(n):
                for k in range(KE):
                    dve.wait_ge(x_mid, KE * n + k + 1)
                    nc.vector.tensor_tensor(xp[:, n % 2, 2, k, :], x_rest[:, k, :], xp[:, n % 2, 1, k, :], ALU.subtract).then_inc(x_low, 1)

            def close(n):
                dve.wait_ge(downed, n + 1)
                norm.residual(dve, n, pair_view(ps, DOWN), w.down_scale[:], freed)

            def left(m):
                n, c = m // NC, m % NC
                dve.wait_ge(h_high, m + 1)
                if m >= DEEP:
                    dve.wait_ge(h_low, m - DEEP + 1)
                nc.vector.tensor_tensor(h_rest[:, m % DEEP], h[:, m % DEEP], hp[:, n % 2, 0, c, :], ALU.subtract).then_inc(h_left, 1)

            def low(m):
                n, c = m // NC, m % NC
                dve.wait_ge(h_mid, m + 1)
                nc.vector.tensor_tensor(hp[:, n % 2, 2, c, :], h_rest[:, m % DEEP], hp[:, n % 2, 1, c, :], ALU.subtract).then_inc(h_low, 1)

            rest_x(0)
            low_x(0)
            if not gated:
                dve.wait_ge(neg, 2)
                nc.vector.scalar_tensor_tensor(fl(wd[:]), fl(w.down), 0.0, fl(wd[:]), ALU.is_gt, ALU.subtract).then_inc(cast_d, 1)
                dve.wait_ge(folded, 1)
            for n in range(BLK):
                for c in range(NC):
                    m = n * NC + c
                    if gated:
                        dve.wait_ge(act_done, m + 1)
                        if m >= DEEP:
                            dve.wait_ge(h_left, m - DEEP + 1)
                        nc.vector.scalar_tensor_tensor(h[:, m % DEEP], ps[:, UP + 2 * (m % 2) + 1, :], w.up_scale[:, 1, c:c + 1],
                                                       h1[:, m % 2], ALU.mult, ALU.mult).then_inc(h_ready, 1)
                    if m >= 1:
                        left(m - 1)
                    if m >= 2:
                        low(m - 2)
                    if c == 2 and n + 1 < BLK:
                        rest_x(n + 1)
                    if c == 4 and n + 1 < BLK:
                        low_x(n + 1)
                    for b in range(BLK):
                        if m == NC * (b + 1) + D0 + BT:
                            close(b)
                        if m == NC * (b + 1) + D0 + BT + 1:
                            norm.statistics(dve, b, freed)
                        if m == NC * (b + 1) + D0 + BT + 2:
                            norm.normalise(dve, b)
            left(BLK * NC - 1)
            low(BLK * NC - 2)
            low(BLK * NC - 1)
            if D0 + BT >= NC:
                close(BLK - 2)
            norm.statistics(dve, BLK - 2, freed)
            norm.normalise(dve, BLK - 2)
            close(BLK - 1)
            norm.statistics(dve, BLK - 1, freed)
            norm.normalise(dve, BLK - 1)


H, DK = 16, 128
HUNITS = B * H
QB = 32
LEVELS = (2, 4, 8, 16)
S_LA, S_BETA, S_NGEX, S_G, S_BGC, S_GC = range(6)
NS = 6


def delta_inputs(g):
    w = np.stack([g["L1_attn_" + n].reshape(KE, P, H, DK) for n in ("Wk", "Wq", "Wv", "Wg")])
    conv = np.stack([g[f"L1_attn_conv_{n}_w"].reshape(H, DK, 4) for n in "kqv"])
    bias = np.stack([g[f"L1_attn_conv_{n}_b"].reshape(H, DK) for n in "kqv"])
    par = np.concatenate([conv.transpose(1, 2, 0, 3).reshape(H, DK, 12), bias.transpose(1, 2, 0),
                          np.zeros((H, DK, 1), np.float32)], 2)
    rows, cols = np.arange(P)[:, None], np.arange(P)[None, :]
    r, c = np.arange(P)[:, None] % QB, np.arange(QB)[None, :]
    low = [((r // n) % 2 == 1) & (c // n == r // n - 1) for n in LEVELS]
    first = (r % 2 == 0) & (c == r + 1)
    half = 0.5 * np.ones((1, 16), np.float32)
    half[0, 0:4] = half[0, 12] = 0.5 * DK ** -0.5
    return {
        "dw": w[:3].transpose(3, 2, 1, 0, 4), "dwg": w[3].transpose(2, 1, 0, 3), "dpar": par, "wab": np.concatenate([g["L1_attn_Wa"], g["L1_attn_Wb"]], 1),
        "bab": np.concatenate([g["L1_attn_ba"], g["L1_attn_bb"]]), "ln": np.stack([g["L1_attn_ln_w"], g["L1_attn_ln_b"]], 1),
        "wo1": g["L1_attn_Wo"],
        "c_half": half.astype(np.float32),
        "c_below": (rows > cols).astype(np.float32),
        "c_low": np.stack(low, 1).astype(np.float32),
        "c_first": -first.astype(np.float32),
        "c_eye": (r == c).astype(np.float32),
    }


def delta_scalars(nc, ps, x_tok, xT, sc, cst, a):
    with phase(nc) as ctx:
        sb = lambda n, s, d=F32: ctx.enter_context(nc.sbuf_tensor(f"e_{n}", s, d))
        sem = lambda n: nc.alloc_semaphore(f"e_{n}")
        wab, bab, ones = sb("wab", [P, KE, 2 * H]), sb("bab", [P, 2 * H]), sb("ones", [P, P])
        z, mag, em, ln1 = sb("z", [P, NT, 2 * H]), sb("mag", [P, NT, H]), sb("em", [P, NT, H]), sb("ln1", [P, NT, H])
        eb, eb1 = sb("eb", [P, NT, H]), sb("eb1", [P, NT, H])
        gl = sb("gl", [P, 4, HUNITS * TB])
        la = sb("la", [P, HUNITS, TB])
        w_in, turned, out_a, out_d = sem("w_in"), sem("turned"), sem("out_a"), sem("out_d")
        logits, zs, mags, exps, lns, las, chain = (sem(n) for n in ("logits", "zs", "mags", "exps", "lns", "las", "chain"))
        sums, decays, ones_made = sem("sums"), sem("decays"), sem("ones_made")
        ident, upto, above, below = cst["ident"], cst["upto"], cst["above"], cst["below"]
        NG = NT // 4 * KE
        block = ctx.enter_context(nc.Block())
        by_unit = lambda t: t.rearrange("p (b c) h -> p b h c", b=B)

        @block.sync
        def _(sp):
            sp.dma_start(wab[:], a["wab"].rearrange("(k p) n -> p k n", p=P)).then_inc(w_in, 16)
            sp.dma_start(bab[:], a["bab"].partition_broadcast(P)).then_inc(w_in, 16)

        @block.gpsimd
        def _(pool):
            nc.gpsimd.memset(ones[:], 1.0).then_inc(ones_made, 1)

        @block.tensor
        def _(pe):
            for g in range(NG):
                k, t4 = g % KE, g // KE
                if g >= 2:
                    pe.wait_ge(out_a if g % 2 == 0 else out_d, g // 2)
                for i in range(4):
                    last = nc.tensor.transpose(ps[:, g % 2, i * P:(i + 1) * P], x_tok[:, t4 * 4 + i, k * P:(k + 1) * P], ident[:])
                last.then_inc(turned, 1)
            pe.wait_ge(out_a, NG // 2)
            pe.wait_ge(out_d, NG // 2)
            pe.wait_ge(w_in, 32)
            for n in range(NT):
                for k in range(KE):
                    last = nc.tensor.matmul(ps[:, 2, n * 2 * H:(n + 1) * 2 * H], xT[:, k, n * P:(n + 1) * P], wab[:, k, :],
                                            start=(k == 0), stop=(k == KE - 1))
            last.then_inc(logits, 1)
            pe.wait_ge(las, B)
            pe.wait_ge(ones_made, 1)
            flat = la[:].rearrange("p u c -> p (u c)")
            for n, m in enumerate((above, upto, below, ones)):
                nc.tensor.matmul(ps[:, 4 + n, 0:HUNITS * TB], m[:], flat, start=True, stop=True).then_inc(sums, 1)

        @block.scalar
        def _(act):
            for g in range(0, NG, 2):
                act.wait_ge(turned, g + 1)
                nc.scalar.activation(xT[:, g % KE, g // KE * HALF:(g // KE + 1) * HALF], ps[:, g % 2, :], ACT.Copy).then_inc(out_a, 1)
            act.wait_ge(mags, 1)
            nc.scalar.activation(em[:], mag[:], ACT.Exp, scale=-1.0).then_inc(exps, 1)
            nc.scalar.activation(eb[:], z[:, :, H:2 * H], ACT.Exp, scale=-1.0).then_inc(exps, 1)
            act.wait_ge(exps, 1)
            nc.scalar.activation(ln1[:], em[:], ACT.Ln, bias=1.0).then_inc(lns, 1)
            act.wait_ge(sums, 4)
            for n in range(4):
                nc.scalar.activation(gl[:, n, :], ps[:, 4 + n, 0:HUNITS * TB], ACT.Exp).then_inc(decays, 1)

        @block.vector
        def _(dve):
            n = [0]

            def link(ins):
                n[0] += 1
                ins.then_inc(chain, 1)
                dve.wait_ge(chain, n[0])

            for g in range(1, NG, 2):
                dve.wait_ge(turned, g + 1)
                nc.vector.tensor_copy(xT[:, g % KE, g // KE * HALF:(g // KE + 1) * HALF], ps[:, g % 2, :]).then_inc(out_d, 1)
            dve.wait_ge(w_in, 32)
            dve.wait_ge(logits, 1)
            nc.vector.tensor_tensor(z[:], ps[:, 2, :].rearrange("p (n h) -> p n h", h=2 * H),
                                    bab[:].unsqueeze(1).to_broadcast([P, NT, 2 * H]), ALU.add).then_inc(zs, 1)
            dve.wait_ge(zs, 1)
            nc.vector.scalar_tensor_tensor(mag[:], z[:, :, 0:H], -1.0, z[:, :, 0:H], ALU.mult, ALU.max).then_inc(mags, 1)
            dve.wait_ge(exps, 2)
            link(nc.vector.tensor_scalar(eb1[:], eb[:], 1.0, None, ALU.add))
            link(nc.vector.reciprocal(eb[:], eb1[:]))
            for b in range(B):
                link(nc.vector.tensor_copy(sc[:, b * H:(b + 1) * H, S_BETA, :], by_unit(eb[:])[:, b]))
            dve.wait_ge(lns, 1)
            for b in range(B):
                nc.vector.scalar_tensor_tensor(la[:, b * H:(b + 1) * H, :], by_unit(z[:, :, 0:H])[:, b], 0.0, by_unit(ln1[:])[:, b],
                                               ALU.min, ALU.subtract).then_inc(las, 1)
            dve.wait_ge(las, B)
            link(nc.vector.tensor_copy(sc[:, :, S_LA, :], la[:]))
            dve.wait_ge(decays, 4)
            u = lambda t: t.rearrange("p (u c) -> p u c", c=TB)
            link(nc.vector.tensor_scalar(sc[:, :, S_NGEX, :], u(gl[:, 0]), -1.0, None, ALU.mult))
            link(nc.vector.tensor_copy(sc[:, :, S_G, :], u(gl[:, 1])))
            link(nc.vector.tensor_tensor(sc[:, :, S_BGC, :], u(gl[:, 2]), sc[:, :, S_BETA, :], ALU.mult))
            link(nc.vector.tensor_copy(sc[:, :, S_GC, :], u(gl[:, 3])))


PLACES = {
    "load": 0.0427, "first_proj": 0.04, "proj_step": 0.25, "second_half": 0.0727, "tap": 0.1516, "conv": 0.1646, "conv_step": 0.04, "tanh": 0.25,
    "silu_end": 0.0906, "pair_end": 0.2877, "mask_0": 0.26, "mask_1": 0.4215, "inverse": 0.44, "join": 0.75, "join_end": 0.9848,
    "gate": 0.5, "gate_end": 0.8, "turn_v": 0.7624, "turn_k": 0.99,
    "scan": 0.0, "scan_end": 0.988,
    "stats": 0.0013, "norm": 0.0973, "turn_o": 0.1226, "out": 0.2, "out_end": 0.3676,
}


def delta_heads(nc, ps, x_tok, xT, sc, cst, a):
    with phase(nc) as ctx:
        sb = lambda n, s, d=F32: ctx.enter_context(nc.sbuf_tensor(f"d_{n}", s, d))
        two = lambda n, s: [sb(f"{n}{p}", s) for p in range(2)]
        SEM = {}

        def sem(name, count, start=0):
            SEM[name] = (nc.alloc_semaphore("d_" + name), count, start)

        ident, identb, neg_kq, upto, below = (cst[n] for n in ("ident", "identb", "neg_kq", "upto", "below"))
        half, low, first, eye = sb("half", [P, 16]), sb("low", [P, len(LEVELS), QB]), sb("first", [P, QB]), sb("eye", [P, QB])
        ln, ln2 = sb("ln", [P, 2]), sb("ln2", [P, 2])
        w, wg = two("w", [P, KE, 3, DK]), two("wg", [P, KE, DK])
        wo = two("wo", [P, E])
        par, par2 = two("par", [P, 16]), two("par2_", [P, 16])
        ss = two("ss", [P, NS, TB])
        raw, acc, th = ([sb(f"{n}{i}", [P, T]) for i in range(3)] for n in ("raw", "acc", "th"))
        kq = two("kq", [P, TB, 2, P])
        vT = sb("vT", [P, T])
        gate = two("gate", [P, T])
        seg = two("seg", [P, P])
        dec = two("dec", [P, P + 1])
        ap = two("ap", [P, TB, 2, P])
        ktok, vtok = two("ktok", [P, TB, P]), two("vtok", [P, TB, P])
        tp, ttp, ym = (sb(n, [P, TB, QB]) for n in ("tp", "ttp", "ym"))
        tn = sb("tn", [64, TB, 64])
        y2 = sb("y2", [P, TB, 64])
        tt = two("tt", [P, TB, P])
        state, r_sb, w_sb = sb("state", [P, P]), sb("r_sb", [P, P]), sb("w_sb", [P, P])
        os_ = two("os", [P, P])
        o_sb, o_aff = two("o_sb", [P, TB, P]), sb("o_aff", [P, T])
        o_g = two("o_g", [P, T])
        st6, mv, ve, rs = sb("st6", [P, 2, TB, 6]), sb("mv", [P, TB, 2]), sb("ve", [P, TB]), sb("rs", [P, TB])

        c_in, c_made = nc.alloc_semaphore("d_c_in"), nc.alloc_semaphore("d_c_made")
        w_in = [nc.alloc_semaphore(f"d_w_in{p}") for p in range(2)]
        wg_in = [nc.alloc_semaphore(f"d_wg_in{p}") for p in range(2)]
        wo_in = [nc.alloc_semaphore(f"d_wo_in{p}") for p in range(2)]
        past = {eng: nc.alloc_semaphore(f"d_past{n}") for n, eng in enumerate((nc.tensor, nc.vector, nc.gpsimd))}
        for name, count, start in (
                ("proj", 6, 0), ("gproj", 2, 0), ("pair", 8, 0), ("k_turned", 2, 0), ("v_turned", 2, 0), ("y", 9, 0), ("z", 9, 0), ("y2", 1, 0),
                ("z2", 1, 0), ("ks", 7, 0), ("qs", 7, 0), ("w", 8, 0), ("pw", 8, 16), ("s", 7, 0), 
                ("o_turned", 2, 4), ("outp", 4, 8),
                ("raw", 6, 0), ("graw", 2, 0), ("tanh", 3, 0), ("dec", 8, 0), ("v_tok", 2, 0), ("diag", 6, 0), ("off64", 3, 0), ("off128", 1, 0),
                ("qs_out", 7, 0), ("w_out", 8, 0), ("affine", 2, 0),
                ("conv", 9, 0), ("silu", 3, 0), ("ap", 8, 0), ("ap_a", 8, 0), ("k_tok", 2, 0), ("tp", 9, 0), ("ttp", 8, 0), ("ym", 9, 0),
                ("first", 8, 0), ("ttp0", 2, 0), ("y2_out", 1, 0), ("r", 7, 0), ("state", 7, 0), ("o", 8, 1), ("stats", 8, 0), ("mv", 1, 0), ("normed", 2, 0),
                ("gated", 2, 4), ("added", 4, 4),
                ("par", 1, 0), ("ss", 1, 0), ("tap", 3, 0), ("seg", 8, 0), 
                ("ve", 1, 0), ("rs", 1, 0)):
            sem(name, count, start)
        block = ctx.enter_context(nc.Block())
        PROJ, RING, INV, KS, QS = 0, 2, 4, 6, 7
        LV = 2 * len(LEVELS)
        LOOPED = (HUNITS - 4) // 2
        NQ = P // QB

        def spread(steps, t0, t1):
            return [(t0 + (t1 - t0) * n / len(steps), s) for n, s in enumerate(steps)]

        early = [(PLACES["load"], ("load",))]
        for i in range(3):
            t0 = PLACES["first_proj"] + PLACES["proj_step"] * i
            early += [(t0, ("proj", i, 0)), (t0 + 0.001, ("raw", i, 0)), (t0 + PLACES["second_half"], ("proj", i, 1)), (t0 + PLACES["second_half"] + 0.001, ("raw", i, 1)),
                      (t0 + PLACES["tap"], ("tap", i))]
            early += [(t0 + PLACES["conv"] + PLACES["conv_step"] * m, ("conv", i, m)) for m in range(3)]
            early += [(t0 + PLACES["tanh"], ("tanh", i))]
        inverse = [("first",)]
        for l in range(len(LEVELS)):
            inverse += [("level", l)]
        joined = [("diag",), ("y64",), ("z64",), ("y128",), ("z128",)]
        late = spread([("scalars",), ("silu", 0), ("silu", 1), ("silu", 2)], 0.0, PLACES["silu_end"])
        late += spread([(k, c) for c in range(TB) for k in ("seg", "pair")], PLACES["silu_end"], PLACES["pair_end"])
        late += spread(inverse, PLACES["inverse"], PLACES["join"]) + spread(joined, PLACES["join"], PLACES["join_end"])
        late += [(PLACES["mask_0"], ("mask", 0)), (PLACES["mask_1"], ("mask", 1))]
        late += spread([("gate", 0), ("gate", 1)], PLACES["gate"], PLACES["gate_end"])
        late += [(PLACES["turn_v"], ("v_turn", 0)), (PLACES["turn_v"] + 0.01, ("v_turn", 1)), (PLACES["turn_k"], ("k_turn", 0)), (PLACES["turn_k"] + 0.001, ("k_turn", 1))]
        scan = spread([("scan", c, k) for c in range(TB) for k in range(3)], PLACES["scan"], PLACES["scan_end"])
        post = [(PLACES["stats"], ("stats",))] + spread([("norm", 0), ("norm", 1)], PLACES["norm"], PLACES["norm"] + 0.02)
        post += spread([("o_turn", 0), ("o_turn", 1)], PLACES["turn_o"], PLACES["turn_o"] + 0.03)
        post += spread([("out", q) for q in range(4)], PLACES["out"], PLACES["out_end"])

        def stage(*parts):
            out = sorted((t, n, s) for n, steps in parts for t, s in steps)
            assert len(parts) < 3 or [s[0] for _, _, s in out if s[0] in ("pair", "gate", "v_turn", "k_turn", "o_turn", "out")][-2:] == ["k_turn", "k_turn"]
            return [(n, x) for _, n, s in out
                    for x in ([(k, s[1], h) for k in "yz" for h in range(2)] if s[0] == "level" else [s])]

        class Engine:

            def __init__(self, eng):
                self.eng, self.lp = eng, Loop()
                self.ring = []

            def wait(self, name, n, k):
                s, count, start = SEM[name]
                self.eng.wait_ge(s, self.lp.at(n * count + k + start, 2 * count))

            def passed(self):
                self.eng.sem_inc(past[self.eng], 1)

            def walk(self, do):
                def steps(lst, base):
                    for n, s in lst:
                        if s[0] in do:
                            do[s[0]](n, n + base, *s[1:])

                steps([(0, s) for _, s in sorted(early)], 0)
                steps(stage((0, late), (1, early)), 0)
                steps(stage((0, scan), (1, late), (2, early)), 0)
                with self.eng.Fori(0, LOOPED) as i:
                    self.lp.i = i
                    steps(stage((0, post), (1, scan), (2, late), (3, early)), i * 2)
                    steps(stage((1, post), (2, scan), (3, late), (4, early)), i * 2)
                self.lp.i = LOOPED - 1
                for parts in (((2, post), (3, scan), (4, late), (5, early)), ((3, post), (4, scan), (5, late)), ((4, post), (5, scan)), ((5, post),)):
                    steps(stage(*parts), 2 * (LOOPED - 1))

        inc = lambda ins, name: ins.then_inc(SEM[name][0], 1)

        @block.sync
        def _(sp):
            E_ = Engine(sp)
            for dst, name in ((low, "c_low"), (first, "c_first"), (eye, "c_eye"), (ln, "ln")):
                sp.dma_start(dst[:], a[name]).then_inc(c_in, 16)
            sp.dma_start(half[:], a["c_half"].rearrange("o n -> (o n)").partition_broadcast(P)).then_inc(c_in, 16)

            def fetch(p, u):
                h = u % H
                sp.dma_start(w[p][:].rearrange("p k i d -> p (k i d)"),
                             a["dw"][bass.ds(h, 1)].rearrange("o p k i d -> (o p) (k i d)")).then_inc(w_in[p], 16)
                sp.dma_start(par[p][:], a["dpar"][bass.ds(h, 1)].rearrange("o p n -> (o p) n")).then_inc(w_in[p], 16)

            def ahead(n, u):
                E_.wait("silu", n, 3)
                fetch(n % 2, u + 2)

            def fetch_gate(p, u):
                sp.dma_start(wg[p][:].rearrange("p k d -> p (k d)"),
                             a["dwg"][bass.ds(u % H, 1)].rearrange("o p k d -> (o p) (k d)")).then_inc(wg_in[p], 16)

            def ahead_gate(n, u):
                E_.wait("gproj", n, 2)
                fetch_gate(n % 2, u + 2)

            def fetch_wo(p, u):
                sp.dma_start(wo[p][:], a["wo1"].rearrange("(h p) n -> h p n", p=P)[bass.ds(u % H, 1)].rearrange("o p n -> (o p) n")).then_inc(wo_in[p], 16)

            def ahead_wo(n, u):
                E_.wait("outp", n, 4)
                fetch_wo(n % 2, u + 2)

            fetch(0, 0)
            fetch(1, 1)
            for p in range(2):
                fetch_gate(p, p)
                fetch_wo(p, p)
            ahead(0, 0)
            ahead_gate(0, 0)
            ahead(1, 1)
            ahead_gate(1, 1)
            with sp.Fori(0, LOOPED) as i:
                E_.lp.i = i
                for n in range(2):
                    ahead(n + 2, i * 2 + n + 2)
                    ahead_wo(n, i * 2 + n)
                    ahead_gate(n + 2, i * 2 + n + 2)
            E_.lp.i = LOOPED - 1
            for n in range(2, 4):
                ahead_wo(n, HUNITS - 6 + n)

        @block.gpsimd
        def _(pool):
            E_ = Engine(pool)
            W = E_.wait

            def load(n, u):
                p = n % 2
                pool.wait_ge(w_in[p], E_.lp.at(32 * (n // 2 + 1), 32))
                if n >= 2:
                    W("conv", n - 2, 9)
                inc(nc.gpsimd.tensor_tensor(par2[p][:], par[p][:], half[:], ALU.mult), "par")

            def scalars(n, u):
                p = n % 2
                W("pw", n - 2, TB)
                inc(nc.gpsimd.tensor_copy(ss[p][:], sc[:, bass.ds(u, 1)].rearrange("p o k c -> p (o k) c")), "ss")

            def tap(n, u, i):
                W("par", n, 1)
                W("raw", n, 2 * i + 2)
                if n >= 1:
                    W("silu", n - 1, i + 1)
                E_.passed()
                inc(nc.gpsimd.tensor_scalar(acc[i][:], raw[i][:], par2[n % 2][:, 4 * i + 3:4 * i + 4],
                                            par2[n % 2][:, 12 + i:13 + i], ALU.mult, ALU.add), "tap")

            def segs(n, u, c):
                if c == 0:
                    W("ss", n, 1)
                if c >= 2:
                    W("pair", n, c - 1)
                elif n >= 1:
                    W("pair", n - 1, TB + c - 1)
                E_.passed()
                inc(nc.gpsimd.tensor_scalar(seg[c % 2][:], below[:], ss[n % 2][:, S_LA, c:c + 1], None, ALU.mult), "seg")

            def stats(n, u):
                W("mv", n, 1)
                E_.passed()
                inc(nc.gpsimd.tensor_scalar(ve[:], mv[:, :, 1], EPS, None, ALU.add), "ve")
                W("ve", n, 1)
                inc(nc.gpsimd.tensor_tensor(rs[:], ve[:], cst["pow_half"][:, 0:TB], ALU.pow), "rs")
                W("rs", n, 1)

            for p in range(2):
                nc.gpsimd.memset(dec[p][:, 0:1], 0.0).then_inc(c_made, 1)
                nc.gpsimd.memset(tt[p][:], 0.0).then_inc(c_made, 1)
            nc.gpsimd.memset(tn[:], 0.0).then_inc(c_made, 1)
            pool.wait_ge(c_in, 80)
            nc.gpsimd.tensor_scalar(ln2[:], ln[:], 0.5, None, ALU.mult).then_inc(c_made, 1)
            pool.wait_ge(c_made, 7)
            E_.walk({"load": load, "scalars": scalars, "tap": tap, "seg": segs, "stats": stats})

        @block.tensor
        def _(pe):
            E_ = Engine(pe)
            W = E_.wait
            pe.sem_inc(SEM["pw"][0], 2 * TB)
            pe.sem_inc(SEM["o_turned"][0], 4)
            pe.sem_inc(SEM["outp"][0], 8)

            def ring(reader):
                n = len(E_.ring)
                if n >= 2:
                    W(*E_.ring[n - 2])
                E_.ring.append(reader)
                return RING + n % 2

            def proj(n, u, i, h):
                p = n % 2
                if i == 0 and h == 0:
                    pe.wait_ge(w_in[p], E_.lp.at(32 * (n // 2 + 1), 32))
                if i >= 1:
                    W("raw", n, 2 * i + h - 1)
                elif n >= 1:
                    W("raw", n - 1, 5 + h)
                for k in range(KE):
                    last = nc.tensor.matmul(ps[:, PROJ + h, :], w[p][:, k, i, :], xT[:, k, bass.ds((u // H) * T + h * HALF, HALF)],
                                            start=(k == 0), stop=(k == KE - 1))
                inc(last, "proj")

            def gate_(n, u, h):
                bank = ring(("graw", n, h + 1))
                if h == 0:
                    pe.wait_ge(wg_in[n % 2], E_.lp.at(16 * (n // 2 + 1), 16))
                for k in range(KE):
                    last = nc.tensor.matmul(ps[:, bank, :], wg[n % 2][:, k, :], xT[:, k, bass.ds((u // H) * T + h * HALF, HALF)],
                                            start=(k == 0), stop=(k == KE - 1))
                inc(last, "gproj")

            def pair(n, u, c):
                bank = ring(("ap", n, c + 1))
                if c == 0:
                    W("silu", n, 2)
                kqc = kq[n % 2][:, c]
                nc.tensor.matmul(ps[:, bank, 0:2 * P], kqc[:, 0, :], kqc.rearrange("p i t -> p (i t)"), start=True, stop=True)
                W("seg", n, c + 1)
                nc.tensor.matmul(ps[:, bank, 2 * P:3 * P], seg[c % 2][:], upto[:], start=True, stop=False)
                inc(nc.tensor.matmul(ps[:, bank, 2 * P:3 * P], identb[:], neg_kq[:], start=False, stop=True), "pair")

            def k_turn(n, u, j):
                bank = ring(("k_tok", n, j + 1))
                for c in range(4):
                    last = nc.tensor.transpose(ps[:, bank, c * P:(c + 1) * P], kq[n % 2][:, 4 * j + c, 0, :], ident[:])
                inc(last, "k_turned")

            def v_turn(n, u, j):
                bank = ring(("v_tok", n, j + 1))
                W("silu", n, 3)
                for c in range(4):
                    last = nc.tensor.transpose(ps[:, bank, c * P:(c + 1) * P], vT[:, (4 * j + c) * P:(4 * j + c + 1) * P], ident[:])
                inc(last, "v_turned")

            def packed(h, lhs, rhs):
                for c in range(h * TB // 2, (h + 1) * TB // 2):
                    for q in range(NQ):
                        r = slice(q * QB, (q + 1) * QB)
                        last = nc.tensor.matmul(ps[r, INV + h, c * QB:(c + 1) * QB], lhs(c, r), rhs[r, c, :], start=True, stop=True)
                return last

            def y(n, u, l, h):
                if l == 0 and h == 0:
                    W("ap", n, TB)
                    if n >= 1:
                        W("off128", n - 1, 1)
                W("tp", n, max(1, 2 * l + h))
                E_.passed()
                inc(packed(h, lambda c, r: ap[n % 2][r, c, 0, r], tp), "y")

            def z(n, u, l, h):
                W("ym", n, 2 * l + h + 1)
                E_.passed()
                inc(packed(h, lambda c, r: ttp[r, c, :], ym), "z")

            def y64(n, u):
                W("ttp", n, LV)
                E_.passed()
                for c in range(TB):
                    for s in (0, 64):
                        last = nc.tensor.matmul(ps[s + QB:s + 64, INV, c * QB:(c + 1) * QB], ap[n % 2][s:s + QB, c, 0, s + QB:s + 64],
                                                tp[s:s + QB, c, :], start=True, stop=True)
                inc(last, "y")

            def z64(n, u):
                W("ym", n, LV + 1)
                E_.passed()
                for c in range(TB):
                    for s in (0, 64):
                        last = nc.tensor.matmul(ps[s:s + QB, INV, c * QB:(c + 1) * QB], ym[s + QB:s + 64, c, :], ttp[s + QB:s + 64, c, :],
                                                start=True, stop=True)
                    last = nc.tensor.matmul(ps[QB:64, INV, c * QB:(c + 1) * QB], ttp[QB:64, c, :], ym[QB:64, c, :], start=True, stop=True)
                inc(last, "z")

            def y128(n, u):
                W("off64", n, 3)
                W("diag", n, 6)
                E_.passed()
                for c in range(TB):
                    last = nc.tensor.matmul(ps[64:P, INV, c * 64:(c + 1) * 64], ap[n % 2][0:64, c, 0, 64:P], tn[:, c, :], start=True, stop=True)
                inc(last, "y2")

            def z128(n, u):
                W("y2_out", n, 1)
                E_.passed()
                for c in range(TB):
                    last = nc.tensor.matmul(ps[0:64, INV, c * 64:(c + 1) * 64], y2[64:P, c, :], tt[n % 2][64:P, c, 64:P], start=True, stop=True)
                inc(last, "z2")

            def scan_(n, u, c, part):
                p = n % 2
                if part == 0:
                    if c == 0:
                        return
                    W("state", n, c)
                    inc(nc.tensor.matmul(ps[:, KS, 0:P], kq[p][:, c, 0, :], state[:], start=True, stop=True), "ks")
                    W("o", n, c)
                    inc(nc.tensor.matmul(ps[:, QS, 0:P], kq[p][:, c, 1, :], state[:], start=True, stop=True), "qs")
                elif part == 1:
                    if c == 0:
                        W("v_tok", n, 2)
                        W("off128", n, 1)
                        W("diag", n, 6)
                        rhs = vtok[p][:, 0, :]
                    else:
                        W("r", n, c)
                        rhs = r_sb[:]
                    inc(nc.tensor.matmul(ps[:, KS, 0:P], tt[p][:, c, :], rhs, start=True, stop=True), "w")
                else:
                    W("w_out", n, c + 1)
                    if c == 0:
                        W("o", n, 0)
                        W("k_tok", n, 2)
                    if c < TB - 1:
                        inc(nc.tensor.matmul(ps[:, KS, 0:P], ktok[p][:, c, :], w_sb[:], start=True, stop=True), "s")
                    inc(nc.tensor.matmul(ps[:, QS, 0:P], ap[p][:, c, 1, :], w_sb[:], start=True, stop=True), "pw")

            def o_turn(n, u, j):
                bank = ring(("affine", n, j + 1))
                W("normed", n, j + 1)
                for c in range(4):
                    last = nc.tensor.transpose(ps[:, bank, c * P:(c + 1) * P], o_sb[n % 2][:, 4 * j + c, :], ident[:])
                inc(last, "o_turned")

            def out(n, u, q):
                bank = ring(("added", n, q + 1))
                if q == 0:
                    pe.wait_ge(wo_in[n % 2], E_.lp.at(16 * (n // 2 + 1), 16))
                W("gated", n, q // 2 + 1)
                for t in range(2):
                    last = nc.tensor.matmul(ps[:, bank, t * E:(t + 1) * E], o_g[n % 2][:, (2 * q + t) * P:(2 * q + t + 1) * P], wo[n % 2][:],
                                            start=True, stop=True)
                inc(last, "outp")

            pe.wait_ge(c_made, 7)
            E_.walk({"proj": proj, "gate": gate_, "pair": pair, "k_turn": k_turn, "v_turn": v_turn, "y": y, "z": z, "y64": y64, "z64": z64,
                     "y128": y128, "z128": z128, "scan": scan_, "o_turn": o_turn, "out": out})

        @block.scalar
        def _(act):
            E_ = Engine(act)
            W = E_.wait

            def raw_(n, u, i, h):
                W("proj", n, 2 * i + h + 1)
                c = slice(h * HALF, (h + 1) * HALF)
                if n >= 1:
                    W("conv", n - 1, 3 * i + 3)
                inc(nc.scalar.activation(raw[i][:, c], ps[:, PROJ + h, :], ACT.Copy), "raw")

            def gate_(n, u, h):
                bank = RING + len(E_.ring) % 2
                E_.ring.append(0)
                W("gproj", n, h + 1)
                W("gated", n - 2, 2)
                inc(nc.scalar.activation(gate[n % 2][:, h * HALF:(h + 1) * HALF], ps[:, bank, :], ACT.Tanh, scale=0.5), "graw")

            def tanh(n, u, i):
                W("conv", n, 3 * i + 3)
                if n >= 1:
                    W("silu", n - 1, i + 1)
                inc(nc.scalar.activation(th[i][:], acc[i][:], ACT.Tanh, scale=(float(DK) ** 0.5 if i == 0 else 1.0)), "tanh")

            def pair(n, u, c):
                W("pair", n, c + 1)
                inc(nc.scalar.activation(dec[c % 2][:, 1:P + 1], ps[:, RING + len(E_.ring) % 2, 2 * P:3 * P], ACT.Exp), "dec")
                E_.ring.append(0)

            def k_turn(n, u, j):
                E_.ring.append(0)

            def v_turn(n, u, j):
                bank = RING + len(E_.ring) % 2
                E_.ring.append(0)
                W("v_turned", n, j + 1)
                W("pw", n - 2, TB)
                inc(nc.scalar.activation(vtok[n % 2][:, 4 * j:4 * j + 4, :].rearrange("p c d -> p (c d)"), ps[:, bank, :], ACT.Copy), "v_tok")

            def diag(n, u):
                W("ttp", n, LV)
                W("pw", n - 2, TB)
                if n >= 1:
                    W("y2", n - 1, 1)
                for q in range(2):
                    r = slice(q * QB, (q + 1) * QB)
                    inc(nc.scalar.activation(tn[r, :, r], tp[r], ACT.Copy), "diag")
                for q in range(NQ):
                    r = slice(q * QB, (q + 1) * QB)
                    inc(nc.scalar.activation(tt[n % 2][r, :, r], ttp[r], ACT.Copy), "diag")

            def z64(n, u):
                W("z", n, LV + 1)
                v = ps[:, INV, 0:TB * QB].rearrange("p (c t) -> p c t", t=QB)
                inc(nc.scalar.activation(tn[QB:64, :, 0:QB], v[QB:64], ACT.Copy, scale=-1.0), "off64")
                for s in (0, 64):
                    inc(nc.scalar.activation(tt[n % 2][s:s + QB, :, s + QB:s + 64], v[s:s + QB], ACT.Copy, scale=-1.0), "off64")

            def z128(n, u):
                W("z2", n, 1)
                inc(nc.scalar.activation(tt[n % 2][0:64, :, 64:P], ps[0:64, INV, :].rearrange("p (c t) -> p c t", t=64), ACT.Copy, scale=-1.0), "off128")

            def scan_(n, u, c, part):
                if part == 0 and c > 0:
                    W("qs", n, c)
                    inc(nc.scalar.activation(os_[c % 2][:], ps[:, QS, 0:P], ACT.Copy, scale=ss[n % 2][:, S_G, c:c + 1]), "qs_out")
                elif part == 1:
                    W("w", n, c + 1)
                    inc(nc.scalar.activation(w_sb[:], ps[:, KS, 0:P], ACT.Copy), "w_out")

            def o_turn(n, u, j):
                bank = RING + len(E_.ring) % 2
                E_.ring.append(0)
                W("o_turned", n, j + 1)
                W("gated", n - 1, j + 1)
                inc(nc.scalar.activation(o_aff[:, j * HALF:(j + 1) * HALF], ps[:, bank, :], ACT.Identity, bias=ln2[:, 1:2],
                                         scale=ln2[:, 0:1]), "affine")

            def out(n, u, q):
                E_.ring.append(0)

            act.wait_ge(c_made, 7)
            E_.walk({"raw": raw_, "gate": gate_, "tanh": tanh, "pair": pair, "k_turn": k_turn, "v_turn": v_turn, "diag": diag, "z64": z64, "z128": z128,
                     "scan": scan_, "o_turn": o_turn, "out": out})

        @block.vector
        def _(dve):
            E_ = Engine(dve)
            W = E_.wait
            dve.sem_inc(SEM["o"][0], 1)
            dve.sem_inc(SEM["gated"][0], 4)
            dve.sem_inc(SEM["added"][0], 4)
            nc.vector.memset(ps[:, INV, :], 0.0).then_inc(c_made, 1)

            def conv(n, u, i, m):
                d, j = m + 1, 2 - m
                if m == 0:
                    W("tap", n, i + 1)
                else:
                    W("conv", n, 3 * i + m)
                inc(nc.vector.scalar_tensor_tensor(acc[i][:, d:T], raw[i][:, 0:T - d], par2[n % 2][:, 4 * i + j:4 * i + j + 1],
                                                   acc[i][:, d:T], ALU.mult, ALU.add), "conv")

            def gate_(n, u, h):
                E_.ring.append(0)

            def silu(n, u, i):
                W("tanh", n, i + 1)
                if i == 0:
                    W("pw", n - 2, TB)
                if i == 2:
                    if n >= 1:
                        W("v_turned", n - 1, 2)
                    dst, t_, a_ = vT[:], th[i][:], acc[i][:]
                else:
                    dst = kq[n % 2][:, :, i, :]
                    t_, a_ = (v[i][:].rearrange("p (c t) -> p c t", t=P) for v in (th, acc))
                inc(nc.vector.scalar_tensor_tensor(dst, t_, 1.0, a_, ALU.add, ALU.mult), "silu")

            def pair(n, u, c):
                bank = RING + len(E_.ring) % 2
                E_.ring.append(0)
                W("dec", n, c + 1)
                beta = ss[n % 2][:, S_BETA, c:c + 1]
                inc(nc.vector.scalar_tensor_tensor(ap[n % 2][:, c, 0, :], ps[:, bank, 0:P], beta, dec[c % 2][:, 0:P], ALU.mult, ALU.mult), "ap_a")
                inc(nc.vector.scalar_tensor_tensor(ap[n % 2][:, c, 1, :], ps[:, bank, P:2 * P], beta, dec[c % 2][:, 1:P + 1], ALU.mult, ALU.mult), "ap")

            def k_turn(n, u, j):
                bank = RING + len(E_.ring) % 2
                E_.ring.append(0)
                W("k_turned", n, j + 1)
                inc(nc.vector.tensor_tensor(ktok[n % 2][:, 4 * j:4 * j + 4, :], ps[:, bank, :].rearrange("p (c d) -> p c d", d=P),
                                            ss[n % 2][:, S_BGC, 4 * j:4 * j + 4].unsqueeze(2).to_broadcast([P, 4, P]), ALU.mult), "k_tok")

            def v_turn(n, u, j):
                E_.ring.append(0)

            def mask(n, u, h):
                cs = slice(h * TB // 2, (h + 1) * TB // 2)
                W("ap_a", n, (h + 1) * TB // 2)
                if n >= 1:
                    W("off128", n - 1, 1)
                for q in range(NQ):
                    r = slice(q * QB, (q + 1) * QB)
                    inc(nc.vector.tensor_tensor(ttp[r, cs], ap[n % 2][r, cs, 0, r], first[r].unsqueeze(1).to_broadcast([QB, TB // 2, QB]),
                                                ALU.mult), "first")
                W("first", n, (h + 1) * NQ)
                inc(nc.vector.tensor_tensor(ttp[:, cs], ttp[:, cs], eye[:].unsqueeze(1).to_broadcast([P, TB // 2, QB]), ALU.add), "ttp0")

            def first_(n, u):
                W("ttp0", n, 2)
                inc(nc.vector.transpose(tp[:].rearrange("p c t -> p (c t)"), ttp[:].rearrange("p c t -> p (c t)")), "tp")

            v = ps[:, INV, 0:TB * QB].rearrange("p (c t) -> p c t", t=QB)
            half_of = lambda h: ps[:, INV + h, h * TB // 2 * QB:(h + 1) * TB // 2 * QB].rearrange("p (c t) -> p c t", t=QB)

            def y(n, u, l, h):
                cs = slice(h * TB // 2, (h + 1) * TB // 2)
                W("y", n, 2 * l + h + 1)
                inc(nc.vector.tensor_tensor(ym[:, cs], half_of(h), low[:, l].unsqueeze(1).to_broadcast([P, TB // 2, QB]), ALU.mult), "ym")

            def z(n, u, l, h):
                cs = slice(h * TB // 2, (h + 1) * TB // 2)
                W("z", n, 2 * l + h + 1)
                inc(nc.vector.tensor_tensor(tp[:, cs], tp[:, cs], half_of(h), ALU.subtract), "tp")
                W("tp", n, 2 * l + h + 2)
                inc(nc.vector.transpose(ttp[:, cs].rearrange("p c t -> p (c t)"), tp[:, cs].rearrange("p c t -> p (c t)")), "ttp")

            def y64(n, u):
                W("y", n, LV + 1)
                inc(nc.vector.tensor_copy(ym[:], v), "ym")

            def y128(n, u):
                W("y2", n, 1)
                inc(nc.vector.tensor_copy(y2[64:P], ps[64:P, INV, :].rearrange("p (c t) -> p c t", t=64)), "y2_out")

            def scan_(n, u, c, part):
                p = n % 2
                if part == 0 and c > 0:
                    W("ks", n, c)
                    inc(nc.vector.scalar_tensor_tensor(r_sb[:], ps[:, KS, 0:P], ss[p][:, S_NGEX, c:c + 1], vtok[p][:, c, :],
                                                       ALU.mult, ALU.add), "r")
                elif part == 2:
                    if c < TB - 1:
                        W("s", n, c + 1)
                        if c == 0:
                            ins = nc.vector.tensor_copy(state[:], ps[:, KS, 0:P])
                        else:
                            ins = nc.vector.scalar_tensor_tensor(state[:], state[:], ss[p][:, S_GC, c:c + 1], ps[:, KS, 0:P], ALU.mult, ALU.add)
                        inc(ins, "state")
                    W("pw", n, c + 1)
                    if c == 0:
                        W("o_turned", n - 2, 2)
                        ins = nc.vector.tensor_copy(o_sb[p][:, 0, :], ps[:, QS, 0:P])
                    else:
                        W("qs_out", n, c)
                        ins = nc.vector.tensor_tensor(o_sb[p][:, c, :], ps[:, QS, 0:P], os_[c % 2][:], ALU.add)
                    inc(ins, "o")
                    W("o", n, c + 1)
                    inc(nc.vector.bn_stats(st6[:, p, c, :], o_sb[p][:, c, :]), "stats")

            def stats(n, u):
                W("stats", n, TB)
                E_.passed()
                for c in range(TB):
                    ins = nc.vector.bn_aggr(mv[:, c, :], st6[:, n % 2, c, :])
                inc(ins, "mv")

            def norm(n, u, j):
                W("rs", n, 1)
                for c in range(4 * j, 4 * j + 4):
                    ins = nc.vector.tensor_scalar(o_sb[n % 2][:, c, :], o_sb[n % 2][:, c, :], mv[:, c, 0:1], rs[:, c:c + 1], ALU.subtract, ALU.mult)
                inc(ins, "normed")

            def o_turn(n, u, j):
                E_.ring.append(0)
                W("affine", n, j + 1)
                c = slice(j * HALF, (j + 1) * HALF)
                W("outp", n - 2, 2 * j + 2)
                inc(nc.vector.scalar_tensor_tensor(o_g[n % 2][:, c], gate[n % 2][:, c], 1.0, o_aff[:, c], ALU.add, ALU.mult), "gated")

            def out(n, u, q):
                bank = RING + len(E_.ring) % 2
                E_.ring.append(0)
                xs = x_tok[:, bass.ds((u // H) * TB + 2 * q, 2), :]
                W("outp", n, q + 1)
                W("added", n - 1, q + 1)
                inc(nc.vector.tensor_tensor(xs, xs, ps[:, bank, :].rearrange("p (i c) -> p i c", c=E), ALU.add), "added")

            dve.wait_ge(c_made, 7)
            dve.wait_ge(c_in, 80)
            E_.walk({"conv": conv, "gate": gate_, "silu": silu, "pair": pair, "k_turn": k_turn, "v_turn": v_turn, "mask": mask, "first": first_, "y": y, "z": z,
                     "y64": y64, "y128": y128, "scan": scan_, "stats": stats, "norm": norm, "o_turn": o_turn, "out": out})


def closing_norm(nc, x_tok, cst, later):
    with phase(nc) as ctx:
        norm = Norm(nc, ctx, "w", x_tok, cst)
        block = ctx.enter_context(nc.Block())

        @block.sync
        def _(sp):
            later.fetch(sp)

        @block.gpsimd
        def _(pool):
            for n in range(BLK):
                norm.inverse_root(pool, n)

        @block.vector
        def _(dve):
            for n in range(BLK):
                norm.statistics(dve, n)
                if n >= 1:
                    norm.normalise(dve, n - 1)
            norm.normalise(dve, BLK - 1)


def delta_layer(nc, ps, x_tok, cst, a):
    with ExitStack() as ctx:
        sb = lambda n, s: ctx.enter_context(nc.sbuf_tensor(n, s, F32))
        xT, sc = sb("x1T", [P, KE, TOK]), sb("sc", [P, HUNITS, NS, TB])
        delta_scalars(nc, ps, x_tok, xT, sc, cst, a)
        delta_heads(nc, ps, x_tok, xT, sc, cst, a)


def constants():
    rows, cols = np.arange(P)[:, None], np.arange(P)[None, :]
    pos = np.arange(1, T + 1, dtype=np.float32)[None, :]
    freqs = (np.float32(10000.0) ** (-(np.float32(2.0) * np.arange(D // 2, dtype=np.float32)) / np.float32(D))).astype(np.float32)
    theta = (pos * freqs[np.arange(P) % (D // 2)][:, None]).astype(np.float32)
    sign = np.where(np.arange(P) % D < D // 2, -1.0, 1.0).astype(np.float32)[:, None]
    return {
        "c_ident": (rows == cols).astype(np.float32),
        "c_above": (cols > rows).astype(np.float32),
        "c_upto": (cols >= rows).astype(np.float32),
        "c_cos": np.cos(theta).astype(np.float32),
        "c_sin": (sign * np.sin(theta)).astype(np.float32),
    }


def build(nc, a, out):
    ctx = ExitStack()
    with ctx:
        sb = lambda n, s, d=F32: ctx.enter_context(nc.sbuf_tensor(n, s, d))
        ps = ctx.enter_context(nc.psum_tensor("ps", [P, 8, HALF], F32))
        x_tok = sb("x_tok", [P, NT, E])
        cst = {"ident": sb("ident", [P, P]), "identb": sb("identb", [P, P], BF16), "neg_qk": sb("neg_qk", [P, P], BF16),
               "neg_kq": sb("neg_kq", [P, P], BF16), "pow_half": sb("pow_half", [P, 8]), "above": sb("above", [P, P]),
               "upto": sb("upto", [P, P]), "below": sb("below", [P, P])}
        scratch = {"x": a["x"].rearrange("(n p) c -> n p c", p=P),
                   "q": nc.dram_tensor("scratch_q", [3, HQ * D, TOK], BF16).ap(),
                   "k": nc.dram_tensor("scratch_k", [3, HKV * D, TOK], BF16).ap()}
        o = out.rearrange("(n p) c -> n p c", p=P)
        cst["in"], cst["in_n"] = ctx.enter_context(nc.semaphore("c_in")), 64
        made = ctx.enter_context(nc.semaphore("c_made"))
        with nc.Block() as block:
            @block.sync
            def _(sp):
                for n, name in enumerate(("ident", "above", "upto", "below")):
                    sp.dma_start(cst[name][:], a["c_" + name]).then_inc(cst["in"], 16)

            @block.gpsimd
            def _(pool):
                nc.gpsimd.memset(cst["pow_half"][:], -0.5).then_inc(made, 1)

            @block.vector
            def _(dve):
                dve.wait_ge(cst["in"], cst["in_n"])
                nc.vector.tensor_copy(cst["identb"][:], cst["ident"][:]).then_inc(made, 1)
                nc.vector.tensor_scalar(cst["neg_qk"][:], cst["above"][:], BIG, None, ALU.mult).then_inc(made, 1)
                nc.vector.tensor_scalar(cst["neg_kq"][:], cst["upto"][:], -BIG, BIG, ALU.mult, ALU.add).then_inc(made, 1)

        first_ffn = ExitStack()
        w0 = Weights(nc, first_ffn, "g", {"up": a["f0_up"], "down": a["f0_down"], "up_scale": a["f0_us"], "down_scale": a["f0_ds"]})
        with ExitStack() as layer:
            cst["v_aug"] = layer.enter_context(nc.sbuf_tensor("v_aug", [P, NT, HKV, VW], F32))
            for name, shape in (("q1", [P, G, T]), ("k1", [P, T]), ("q2", [P, G, T]), ("k2", [P, T])):
                cst[name] = [layer.enter_context(nc.sbuf_tensor(f"{name}_{p}", shape, BF16)) for p in range(2)]
            load_and_project(nc, ps, x_tok, cst, scratch,
                             {"wq": a["wq2"], "wk": a["wk2"], "wv": a["wv"], "bq": a["bq2"], "bk": a["bk2"], "bv": a["bv"],
                              "cos": a["c_cos"], "sin": a["c_sin"]}, w0)
            y_tok = layer.enter_context(nc.sbuf_tensor("y_tok", [P, NT, E], F32))
            attention(nc, ps, y_tok, cst, scratch)
            output_projection(nc, ps, x_tok, y_tok, cst, {"wo": a["wo"], "bo": a["bo"]})
        feed_forward(nc, ps, x_tok, cst, w0, True)
        first_ffn.close()
        delta_layer(nc, ps, x_tok, cst, a)
        w1 = Weights(nc, ctx, "s", {"up": a["f1_up"], "down": a["f1_down"], "up_scale": a["f1_us"],
                                    "down_scale": a["f1_ds"], "out_scale": a["f1_os"]})
        closing_norm(nc, x_tok, cst, w1)
        feed_forward(nc, ps, x_tok, cst, w1, False, out=o)


def laid_out(inp):
    g = {n: np.asarray(v) for n, v in inp.items()}
    swap = lambda n: np.arange(n) ^ (D // 2)
    wq, bq, wk, bk = (g["L0_attn_" + n] for n in ("Wq", "bq", "Wk", "bk"))
    a = {
        "x": g["L0_attn_x"].reshape(TOK, E),
        "wq2": np.stack([wq, wq[:, swap(HQ * D)]], 1), "bq2": np.stack([bq, bq[swap(HQ * D)]]).reshape(2, KE, P).transpose(2, 0, 1),
        "wk2": np.stack([wk, wk[:, swap(HKV * D)]], 1), "bk2": np.stack([bk, bk[swap(HKV * D)]]).T,
        "wv": g["L0_attn_Wv"], "bv": g["L0_attn_bv"], "wo": g["L0_attn_Wo"], "bo": g["L0_attn_bo"],
        "f0_up": np.stack([g["L0_ffn_w_gate"], g["L0_ffn_w_up"]]).view(np.int32), "f0_down": np.ascontiguousarray(g["L0_ffn_w_down"]).view(np.int32),
        "f0_us": np.stack([g["L0_ffn_s_gate"], g["L0_ffn_s_up"]]).reshape(2, -1, P).transpose(2, 0, 1), "f0_ds": g["L0_ffn_s_down"],
        "f1_up": g["L1_ffn_up_weight"].T[None], "f1_down": g["L1_ffn_down_weight"].T, "f1_us": g["L1_ffn_up_scale"].reshape(1, -1, P).transpose(2, 0, 1),
        "f1_ds": g["L1_ffn_down_scale"], "f1_os": g["L1_ffn_output_scale"],
    }
    a.update(delta_inputs(g))
    a.update(constants())
    return {n: np.ascontiguousarray(v) for n, v in a.items()}


def kernel(**inputs):
    import concourse.bacc as bacc
    from concourse.bass_utils import run_bass_kernel_spmd

    nc = bacc.Bacc("TRN2", target_bir_lowering=False, num_devices=1)
    arrays = {f"in_{n}": v for n, v in laid_out(inputs).items()}
    aps = {n[3:]: nc.dram_tensor(n, v.shape, mybir.dt.from_np(v.dtype), kind="ExternalInput").ap() for n, v in arrays.items()}
    out = nc.dram_tensor("out", (TOK, E), F32, kind="ExternalOutput").ap()
    build(nc, aps, out)
    r = run_bass_kernel_spmd(nc, [arrays], core_ids=[0])
    return r.results[0]["out"].reshape(B, T, E)
```
